# Optimizing a Trainium2 kernel written in Bass

```python
import numpy as np
import jax
import jax.numpy as jnp

def _softmax(x, axis=-1):
    return jax.nn.softmax(x, axis=axis)

def _gelu(x):
    return jax.nn.gelu(x, approximate=True)

def _silu(x):
    return jax.nn.silu(x)

def _sigmoid(x):
    return jax.nn.sigmoid(x)

def _layernorm(x, axis=-1, eps=1e-05):
    m = jnp.mean(x, axis=axis, keepdims=True)
    v = jnp.var(x, axis=axis, keepdims=True)
    return (x - m) / jnp.sqrt(v + eps)

def _scatter_add(tgt, idx, src, axis=0):
    return tgt.at[idx].add(src)

def _segment_sum(src, seg, n):
    return jax.ops.segment_sum(src, seg, n)
kernel_name = 'mk_decoder_preln_d2_seqx_r8_9543f6'

def setup_inputs(seed: int=0):
    np.random.seed(seed)
    _w = jnp.asarray

    def _rec_inputs():
        import jax
        import jax.numpy as jnp
        _rk = jax.random.key(seed)
        x = -0.0003929 + 0.9999 * jax.random.normal(jax.random.fold_in(_rk, 1), (8, 128, 256), jnp.float32)
        _lenS = 128 - jax.random.randint(jax.random.fold_in(_rk, 7), (8,), 0, max(1, 128 // 4) + 1, jnp.int32)
        _lenS2 = 128 - jax.random.randint(jax.random.fold_in(_rk, 8), (8,), 0, max(1, 128 // 4) + 1, jnp.int32)
        _ctx_2048P = jax.random.normal(jax.random.fold_in(_rk, 11), (8, 16, 256), jnp.float32)
        _ctx_2048c = jax.random.dirichlet(jax.random.fold_in(_rk, 511), 0.3 * jnp.ones((16,), jnp.float32), (8, 128))
        _ctx_2048t = jnp.einsum('bsk,bkd->bsd', _ctx_2048c, _ctx_2048P)
        _ctx_2048t = _ctx_2048t * jax.lax.rsqrt(jnp.mean(jnp.square(_ctx_2048t)) + 1e-12) * 0.953939
        ctx_2048 = -1.39393e-06 + 0.999914 * (_ctx_2048t + 0.3 * jax.random.normal(jax.random.fold_in(_rk, 611), (8, 128, 256), jnp.float32))
        itok_BxS_0_1023 = jax.random.randint(jax.random.fold_in(_rk, 12), (8, 128), 0, 128, jnp.int32)
        return (x, ctx_2048, itok_BxS_0_1023)
    x, ctx_2048, itok_BxS_0_1023 = _rec_inputs()

    def _L0_attn_setup():
        import jax, jax.numpy as jnp
        import numpy as np
        D_IN = 256
        D_OUT = 256
        H = 16
        QK_ROPE = 64
        QK_NOPE = 64
        QK_HEAD = QK_NOPE + QK_ROPE
        V_HEAD = 128
        KV_RANK = 64
        THETA = 10000.0
        EPS = 1e-06

        def rms_norm(x, w):
            var = jnp.mean(x * x, axis=-1, keepdims=True)
            return x * jax.lax.rsqrt(var + EPS) * w

        def apply_rope(x, theta=THETA):
            B, S, NH, D = x.shape
            half = D // 2
            freqs = 1.0 / theta ** (jnp.arange(0, D, 2, dtype=jnp.float32) / D)
            ang = jnp.arange(S, dtype=jnp.float32)[:, None] * freqs[None, :]
            cos = jnp.cos(ang)[None, :, None, :]
            sin = jnp.sin(ang)[None, :, None, :]
            xp = x.reshape(B, S, NH, half, 2)
            x1, x2 = (xp[..., 0], xp[..., 1])
            out = jnp.stack([x1 * cos - x2 * sin, x2 * cos + x1 * sin], axis=-1)
            return out.reshape(B, S, NH, D).astype(x.dtype)
        key = jax.random.key(seed)
        ks = jax.random.split(key, 6)
        B, S = (2, 256)
        s = lambda fan_in: 1.0 / np.sqrt(fan_in)
        x = jax.random.normal(ks[0], (B, S, D_IN), dtype=jnp.float32)
        w_query = jax.random.uniform(ks[1], (D_IN, H * QK_HEAD), jnp.float32, -s(D_IN), s(D_IN))
        wkv_a = jax.random.uniform(ks[2], (D_IN, KV_RANK + QK_ROPE), jnp.float32, -s(D_IN), s(D_IN))
        wkv_b = jax.random.uniform(ks[3], (KV_RANK, H * (QK_NOPE + V_HEAD)), jnp.float32, -s(KV_RANK), s(KV_RANK))
        kv_norm_w = jnp.ones((KV_RANK,), jnp.float32)
        out_proj_w = jax.random.uniform(ks[4], (H * V_HEAD, D_OUT), jnp.float32, -s(H * V_HEAD), s(H * V_HEAD))
        return {'x': x, 'w_query': w_query, 'wkv_a': wkv_a, 'wkv_b': wkv_b, 'kv_norm_w': kv_norm_w, 'out_proj_w': out_proj_w}
    _L0_attn_all = _L0_attn_setup()
    _L0_attn_in = {k: v for k, v in _L0_attn_all.items() if k in ('w_query', 'wkv_a', 'wkv_b', 'kv_norm_w', 'out_proj_w')}
    del _L0_attn_all

    def _L0_xattn_setup():
        import jax, jax.numpy as jnp
        import numpy as np
        B, Lq, Lk = (2, 512, 128)
        Q_DIM, KV_DIM = (256, 256)
        H, HD = (16, 128)
        KVC, QC, R = (64, 96, 64)
        LOOKBACK = 8
        NEG = -1e+30

        def _rope(x, L):
            half = x.shape[-1] // 2
            inv_freq = 1.0 / 10000.0 ** (jnp.arange(half, dtype=jnp.float32) / half)
            ang = jnp.arange(L, dtype=jnp.float32)[:, None] * inv_freq
            cos, sin = (jnp.cos(ang), jnp.sin(ang))
            x1, x2 = (x[..., :half], x[..., half:])
            return jnp.concatenate([x1 * cos - x2 * sin, x1 * sin + x2 * cos], axis=-1)
        key = jax.random.key(seed)
        ks = jax.random.split(key, 11)

        def w(k, shape, fan_in):
            return jax.random.normal(k, shape, jnp.float32) / np.sqrt(fan_in).astype(np.float32)
        return {'q': jax.random.normal(ks[0], (B, Lq, Q_DIM), jnp.float32), 'kv': jax.random.normal(ks[1], (B, Lk, KV_DIM), jnp.float32), 'seg_id': jnp.sort(jax.random.randint(ks[2], (B, Lq), 0, Lk), axis=-1), 'W_kvc': w(ks[3], (KV_DIM, KVC), KV_DIM), 'W_dq': w(ks[4], (Q_DIM, QC), Q_DIM), 'W_uq': w(ks[5], (QC, H * HD), QC), 'W_qr': w(ks[6], (QC, H * R), QC), 'W_uk': w(ks[7], (KVC, H * HD), KVC), 'W_kr': w(ks[8], (KVC, R), KVC), 'W_uv': w(ks[9], (KVC, H * HD), KVC), 'W_o': w(ks[10], (H * HD, Q_DIM), H * HD)}
    _L0_xattn_all = _L0_xattn_setup()
    _L0_xattn_in = {k: v for k, v in _L0_xattn_all.items() if k in ('W_kvc', 'W_dq', 'W_uq', 'W_qr', 'W_uk', 'W_kr', 'W_uv', 'W_o')}
    del _L0_xattn_all

    def _L0_ffn_setup():
        import jax, jax.numpy as jnp
        import numpy as np
        SWIGLU_ALPHA = 1.702
        SWIGLU_LIMIT = 7.0
        B, S, H, E, K, I = (2, 256, 256, 32, 4, 128)
        key = jax.random.key(seed)
        ks = jax.random.split(key, 8)
        return {'hidden_states': jax.random.normal(ks[0], (B, S, H), jnp.float32), 'gate_w': jax.random.normal(ks[1], (E, H), jnp.float32) * 0.02, 'gate_b': jnp.zeros((E,), jnp.float32), 'w_gate': jax.random.normal(ks[2], (E, H, I), jnp.float32) * 0.02, 'b_gate': jnp.zeros((E, I), jnp.float32), 'w_up': jax.random.normal(ks[3], (E, H, I), jnp.float32) * 0.02, 'b_up': jnp.zeros((E, I), jnp.float32), 'w_down': jax.random.normal(ks[4], (E, I, H), jnp.float32) * 0.02, 'b_down': jnp.zeros((E, H), jnp.float32)}
    _L0_ffn_all = _L0_ffn_setup()
    _L0_ffn_in = {k: v for k, v in _L0_ffn_all.items() if k in ('gate_w', 'gate_b', 'w_gate', 'b_gate', 'w_up', 'b_up', 'w_down', 'b_down')}
    del _L0_ffn_all

    def _L1_attn_setup():
        import jax, jax.numpy as jnp
        import numpy as np
        D_MODEL = 256
        STATE = 16
        KCONV = 4
        EXPAND = 2
        D_INNER = D_MODEL * EXPAND
        EPS = 1e-05

        def _silu(v):
            return v * jax.nn.sigmoid(v)
        key = jax.random.key(seed)
        ks = jax.random.split(key, 10)
        s = 0.02
        x = jax.random.normal(ks[0], (2, 256, D_MODEL), dtype=jnp.float32)
        norm_w = jnp.ones((D_MODEL,), jnp.float32)
        in_proj_w = jax.random.normal(ks[1], (D_INNER * 2, D_MODEL), jnp.float32) * s
        conv_w = jax.random.normal(ks[2], (D_INNER, 1, KCONV), jnp.float32) * s
        conv_b = jnp.zeros((D_INNER,), jnp.float32)
        x_proj_w = jax.random.normal(ks[3], (STATE * 2 + 1, D_INNER), jnp.float32) * s
        dt_w = jax.random.normal(ks[4], (D_INNER, 1), jnp.float32) * s
        dt_b = jnp.zeros((D_INNER,), jnp.float32)
        A_log = jnp.log(jnp.broadcast_to(jnp.arange(1, STATE + 1, dtype=jnp.float32)[None, :], (D_INNER, STATE)))
        D_param = jnp.ones((D_INNER,), jnp.float32)
        out_proj_w = jax.random.normal(ks[5], (D_MODEL, D_INNER), jnp.float32) * s
        return {'x': x, 'norm_w': norm_w, 'in_proj_w': in_proj_w, 'conv_w': conv_w, 'conv_b': conv_b, 'x_proj_w': x_proj_w, 'dt_w': dt_w, 'dt_b': dt_b, 'A_log': A_log, 'D_param': D_param, 'out_proj_w': out_proj_w}
    _L1_attn_all = _L1_attn_setup()
    _L1_attn_in = {k: v for k, v in _L1_attn_all.items() if k in ('norm_w', 'in_proj_w', 'conv_w', 'conv_b', 'x_proj_w', 'dt_w', 'dt_b', 'A_log', 'D_param', 'out_proj_w')}
    del _L1_attn_all

    def _L1_xattn_setup():
        import jax, jax.numpy as jnp
        import numpy as np
        B_DIM, T_DIM, C_DIM = (16, 128, 256)

        def _wkv(w, u, k, v):
            Bn, Tn, Cn = k.shape
            NEG_INF = jnp.float32(-1e+38)

            def step(carry, kv_t):
                p, q, o = carry
                kt, vt = kv_t
                no = jnp.maximum(o, u + kt)
                A = jnp.exp(o - no)
                E = jnp.exp(u + kt - no)
                y = (A * p + E * vt) / (A * q + E)
                no2 = jnp.maximum(w + o, kt)
                A2 = jnp.exp(w + o - no2)
                E2 = jnp.exp(kt - no2)
                return ((A2 * p + E2 * vt, A2 * q + E2, no2), y)
            init = (jnp.zeros((Bn, Cn), k.dtype), jnp.zeros((Bn, Cn), k.dtype), jnp.full((Bn, Cn), NEG_INF, k.dtype))
            kT = jnp.moveaxis(k, 1, 0)
            vT = jnp.moveaxis(v, 1, 0)
            _, yT = jax.lax.scan(step, init, (kT, vT))
            return jnp.moveaxis(yT, 0, 1)
        key = jax.random.key(seed)
        k1, k2, k3, k4 = jax.random.split(key, 4)
        w = -jnp.exp(jax.random.normal(k1, (C_DIM,), jnp.float32))
        u = jax.random.normal(k2, (C_DIM,), jnp.float32)
        k = jax.random.normal(k3, (B_DIM, T_DIM, C_DIM), jnp.float32)
        v = jax.random.normal(k4, (B_DIM, T_DIM, C_DIM), jnp.float32)
        return {'B': B_DIM, 'T': T_DIM, 'C': C_DIM, 'w': w, 'u': u, 'k': k, 'v': v}
    _L1_xattn_all = _L1_xattn_setup()
    _L1_xattn_in = {k: v for k, v in _L1_xattn_all.items() if k in ('w', 'u')}
    del _L1_xattn_all

    def _L1_ffn_setup():
        import jax, jax.numpy as jnp
        import numpy as np
        DIM = 256
        INNER = 4 * DIM
        EPS = 1e-05

        def simple_rms_norm(x):
            d = x.shape[-1]
            n = jnp.linalg.norm(x, axis=-1, keepdims=True)
            return x / jnp.maximum(n, 1e-12) * jnp.sqrt(jnp.asarray(d, x.dtype))

        def activation_quant(x):
            scale = 127.0 / jnp.clip(jnp.max(jnp.abs(x), axis=-1, keepdims=True), EPS)
            return jnp.clip(jnp.round(x * scale), -128, 127) / scale

        def weight_quant(w):
            scale = 1.0 / jnp.clip(jnp.mean(jnp.abs(w)), EPS)
            return jnp.clip(jnp.round(w * scale), -1, 1) / scale

        def ste(x, q):
            return x + jax.lax.stop_gradient(q - x)

        def bitlinear158(x, w):
            xn = simple_rms_norm(x)
            xq = ste(xn, activation_quant(xn))
            wq = ste(w, weight_quant(w))
            return jnp.einsum('bsi,oi->bso', xq, wq)
        key = jax.random.key(seed)
        k1, k2, k3 = jax.random.split(key, 3)
        x = jax.random.normal(k1, (4, 256, DIM), dtype=jnp.float32)
        w1 = jax.random.normal(k2, (INNER, DIM), dtype=jnp.float32) * DIM ** (-0.5)
        w2 = jax.random.normal(k3, (DIM, INNER), dtype=jnp.float32) * INNER ** (-0.5)
        return {'x': x, 'w1': w1, 'w2': w2}
    _L1_ffn_all = _L1_ffn_setup()
    _L1_ffn_in = {k: v for k, v in _L1_ffn_all.items() if k in ('w1', 'w2')}
    del _L1_ffn_all
    return {'x': x, 'ctx_2048': ctx_2048, 'itok_BxS_0_1023': itok_BxS_0_1023, 'L0_attn_w_query': _L0_attn_in['w_query'], 'L0_attn_wkv_a': _L0_attn_in['wkv_a'], 'L0_attn_wkv_b': _L0_attn_in['wkv_b'], 'L0_attn_kv_norm_w': _L0_attn_in['kv_norm_w'], 'L0_attn_out_proj_w': _L0_attn_in['out_proj_w'], 'L0_xattn_W_kvc': _L0_xattn_in['W_kvc'], 'L0_xattn_W_dq': _L0_xattn_in['W_dq'], 'L0_xattn_W_uq': _L0_xattn_in['W_uq'], 'L0_xattn_W_qr': _L0_xattn_in['W_qr'], 'L0_xattn_W_uk': _L0_xattn_in['W_uk'], 'L0_xattn_W_kr': _L0_xattn_in['W_kr'], 'L0_xattn_W_uv': _L0_xattn_in['W_uv'], 'L0_xattn_W_o': _L0_xattn_in['W_o'], 'L0_ffn_gate_w': _L0_ffn_in['gate_w'], 'L0_ffn_gate_b': _L0_ffn_in['gate_b'], 'L0_ffn_w_gate': _L0_ffn_in['w_gate'], 'L0_ffn_b_gate': _L0_ffn_in['b_gate'], 'L0_ffn_w_up': _L0_ffn_in['w_up'], 'L0_ffn_b_up': _L0_ffn_in['b_up'], 'L0_ffn_w_down': _L0_ffn_in['w_down'], 'L0_ffn_b_down': _L0_ffn_in['b_down'], 'L1_attn_norm_w': _L1_attn_in['norm_w'], 'L1_attn_in_proj_w': _L1_attn_in['in_proj_w'], 'L1_attn_conv_w': _L1_attn_in['conv_w'], 'L1_attn_conv_b': _L1_attn_in['conv_b'], 'L1_attn_x_proj_w': _L1_attn_in['x_proj_w'], 'L1_attn_dt_w': _L1_attn_in['dt_w'], 'L1_attn_dt_b': _L1_attn_in['dt_b'], 'L1_attn_A_log': _L1_attn_in['A_log'], 'L1_attn_D_param': _L1_attn_in['D_param'], 'L1_attn_out_proj_w': _L1_attn_in['out_proj_w'], 'L1_xattn_w': _L1_xattn_in['w'], 'L1_xattn_u': _L1_xattn_in['u'], 'L1_ffn_w1': _L1_ffn_in['w1'], 'L1_ffn_w2': _L1_ffn_in['w2']}

def reference(x, ctx_2048, itok_BxS_0_1023, L0_attn_w_query, L0_attn_wkv_a, L0_attn_wkv_b, L0_attn_kv_norm_w, L0_attn_out_proj_w, L0_xattn_W_kvc, L0_xattn_W_dq, L0_xattn_W_uq, L0_xattn_W_qr, L0_xattn_W_uk, L0_xattn_W_kr, L0_xattn_W_uv, L0_xattn_W_o, L0_ffn_gate_w, L0_ffn_gate_b, L0_ffn_w_gate, L0_ffn_b_gate, L0_ffn_w_up, L0_ffn_b_up, L0_ffn_w_down, L0_ffn_b_down, L1_attn_norm_w, L1_attn_in_proj_w, L1_attn_conv_w, L1_attn_conv_b, L1_attn_x_proj_w, L1_attn_dt_w, L1_attn_dt_b, L1_attn_A_log, L1_attn_D_param, L1_attn_out_proj_w, L1_xattn_w, L1_xattn_u, L1_ffn_w1, L1_ffn_w2):
    import jax
    import jax.numpy as jnp

    def _L0_attn_ref(x, w_query, wkv_a, wkv_b, kv_norm_w, out_proj_w):
        import jax, jax.numpy as jnp
        import numpy as np
        D_IN = 256
        D_OUT = 256
        H = 16
        QK_ROPE = 64
        QK_NOPE = 64
        QK_HEAD = QK_NOPE + QK_ROPE
        V_HEAD = 128
        KV_RANK = 64
        THETA = 10000.0
        EPS = 1e-06

        def rms_norm(x, w):
            var = jnp.mean(x * x, axis=-1, keepdims=True)
            return x * jax.lax.rsqrt(var + EPS) * w

        def apply_rope(x, theta=THETA):
            B, S, NH, D = x.shape
            half = D // 2
            freqs = 1.0 / theta ** (jnp.arange(0, D, 2, dtype=jnp.float32) / D)
            ang = jnp.arange(S, dtype=jnp.float32)[:, None] * freqs[None, :]
            cos = jnp.cos(ang)[None, :, None, :]
            sin = jnp.sin(ang)[None, :, None, :]
            xp = x.reshape(B, S, NH, half, 2)
            x1, x2 = (xp[..., 0], xp[..., 1])
            out = jnp.stack([x1 * cos - x2 * sin, x2 * cos + x1 * sin], axis=-1)
            return out.reshape(B, S, NH, D).astype(x.dtype)
        B, S, _ = x.shape
        scale = QK_HEAD ** (-0.5)
        q = (x @ w_query).reshape(B, S, H, QK_HEAD)
        kv = x @ wkv_a
        kv_c, k_pe = (kv[..., :KV_RANK], kv[..., KV_RANK:])
        kv_dec = (rms_norm(kv_c, kv_norm_w) @ wkv_b).reshape(B, S, H, QK_NOPE + V_HEAD)
        k_nope, v = (kv_dec[..., :QK_NOPE], kv_dec[..., QK_NOPE:])
        k_pe = jnp.broadcast_to(k_pe[:, :, None, :], (B, S, H, QK_ROPE))
        q_nope, q_pe = (q[..., :QK_NOPE], q[..., QK_NOPE:])
        q_pe = apply_rope(q_pe)
        k_pe = apply_rope(k_pe)
        queries = jnp.concatenate([q_nope, q_pe], axis=-1)
        keys = jnp.concatenate([k_nope, k_pe], axis=-1)
        scores = jnp.einsum('bqhd,bkhd->bhqk', queries, keys) * scale
        mask = jnp.triu(jnp.ones((S, S), dtype=bool), k=1)
        scores = jnp.where(mask[None, None], -jnp.inf, scores)
        attn = jax.nn.softmax(scores.astype(jnp.float32), axis=-1).astype(x.dtype)
        out = jnp.einsum('bhqk,bkhd->bqhd', attn, v).reshape(B, S, H * V_HEAD)
        return out @ out_proj_w

    def _L0_xattn_ref(q, kv, seg_id, W_kvc, W_dq, W_uq, W_qr, W_uk, W_kr, W_uv, W_o):
        import jax, jax.numpy as jnp
        import numpy as np
        B, Lq, Lk = (2, 512, 128)
        Q_DIM, KV_DIM = (256, 256)
        H, HD = (16, 128)
        KVC, QC, R = (64, 96, 64)
        LOOKBACK = 8
        NEG = -1e+30

        def _rope(x, L):
            half = x.shape[-1] // 2
            inv_freq = 1.0 / 10000.0 ** (jnp.arange(half, dtype=jnp.float32) / half)
            ang = jnp.arange(L, dtype=jnp.float32)[:, None] * inv_freq
            cos, sin = (jnp.cos(ang), jnp.sin(ang))
            x1, x2 = (x[..., :half], x[..., half:])
            return jnp.concatenate([x1 * cos - x2 * sin, x1 * sin + x2 * cos], axis=-1)
        b, lq, _ = q.shape
        lk = kv.shape[1]
        kv_c = kv @ W_kvc
        q_c = q @ W_dq
        q_nope = (q_c @ W_uq).reshape(b, lq, H, HD).transpose(0, 2, 1, 3)
        q_rope = (q_c @ W_qr).reshape(b, lq, H, R).transpose(0, 2, 1, 3)
        k_nope = (kv_c @ W_uk).reshape(b, lk, H, HD)
        v = (kv_c @ W_uv).reshape(b, lk, H, HD)
        k_rope = kv_c @ W_kr
        q_rope = _rope(q_rope, lq)
        k_rope = _rope(k_rope, lk)
        scale = 1.0 / np.sqrt(HD + R).astype(np.float32)
        scores = (jnp.einsum('bhqd,bkhd->bhqk', q_nope, k_nope) + jnp.einsum('bhqr,bkr->bhqk', q_rope, k_rope)) * scale
        k_ids = jnp.arange(lk)[None, None, :]
        qs = seg_id[:, :, None]
        good = (k_ids <= qs) & (k_ids >= qs - LOOKBACK)
        scores = jnp.where(good[:, None, :, :], scores, NEG)
        attn = jax.nn.softmax(scores, axis=-1)
        out = jnp.einsum('bhqk,bkhd->bqhd', attn, v).reshape(b, lq, H * HD)
        return out @ W_o

    def _L0_ffn_ref(hidden_states, gate_w, gate_b, w_gate, b_gate, w_up, b_up, w_down, b_down):
        import jax, jax.numpy as jnp
        import numpy as np
        SWIGLU_ALPHA = 1.702
        SWIGLU_LIMIT = 7.0
        B, S, H, E, K, I = (2, 256, 256, 32, 4, 128)
        Bb, Ss, Hh = hidden_states.shape
        x = hidden_states.reshape(-1, Hh)
        logits = x @ gate_w.T + gate_b
        topk_logits, topk_idx = jax.lax.top_k(logits, K)
        topk_weight = jax.nn.softmax(topk_logits.astype(jnp.float32), axis=-1)
        flat_idx = topk_idx.reshape(-1)
        xs = jnp.repeat(x, K, axis=0)
        order = jnp.argsort(flat_idx)
        xt = xs[order]
        gid = flat_idx[order]
        group_sizes = jnp.bincount(flat_idx, length=E).astype(jnp.int32)
        gate = jax.lax.ragged_dot(xt, w_gate, group_sizes) + b_gate[gid]
        up = jax.lax.ragged_dot(xt, w_up, group_sizes) + b_up[gid]
        gate = jnp.minimum(gate, SWIGLU_LIMIT)
        up = jnp.clip(up, -SWIGLU_LIMIT, SWIGLU_LIMIT)
        glu = gate * jax.nn.sigmoid(SWIGLU_ALPHA * gate)
        activated = (up + 1.0) * glu
        outs = jax.lax.ragged_dot(activated, w_down, group_sizes) + b_down[gid]
        inv = jnp.argsort(order)
        outs = outs[inv].reshape(-1, K, Hh)
        y = jnp.sum(outs * topk_weight[..., None], axis=1).astype(x.dtype)
        return y.reshape(Bb, Ss, Hh)

    def _L1_attn_ref(x, norm_w, in_proj_w, conv_w, conv_b, x_proj_w, dt_w, dt_b, A_log, D_param, out_proj_w):
        import jax, jax.numpy as jnp
        import numpy as np
        D_MODEL = 256
        STATE = 16
        KCONV = 4
        EXPAND = 2
        D_INNER = D_MODEL * EXPAND
        EPS = 1e-05

        def _silu(v):
            return v * jax.nn.sigmoid(v)
        residual = x
        xn = x * jax.lax.rsqrt(jnp.mean(x * x, axis=-1, keepdims=True) + EPS) * norm_w
        xz = jnp.einsum('bld,ed->ble', xn, in_proj_w)
        x_inner, z = jnp.split(xz, 2, axis=-1)
        xc = jnp.transpose(x_inner, (0, 2, 1))
        xc = jax.lax.conv_general_dilated(xc, conv_w, window_strides=(1,), padding=[(KCONV - 1, 0)], dimension_numbers=('NCH', 'OIH', 'NCH'), feature_group_count=D_INNER)
        xc = xc + conv_b[None, :, None]
        xc = _silu(jnp.transpose(xc, (0, 2, 1)))
        x_ssm = jnp.einsum('bld,ed->ble', xc, x_proj_w)
        dt = jax.nn.softplus(x_ssm[..., -1:] * dt_w[:, 0] + dt_b)
        B_p = x_ssm[..., :STATE]
        C_p = x_ssm[..., STATE:2 * STATE]
        A = -jnp.exp(A_log)
        batch = x.shape[0]
        h0 = jnp.zeros((batch, D_INNER, STATE), x.dtype)

        def step(h, inp):
            dt_t, B_t, C_t, u_t = inp
            dA = jnp.exp(dt_t[..., None] * A)
            h = dA * h + (dt_t * u_t)[..., None] * B_t[:, None, :]
            y_t = jnp.sum(h * C_t[:, None, :], axis=-1) + D_param * u_t
            return (h, y_t)
        seq_first = lambda a: jnp.swapaxes(a, 0, 1)
        _, ys = jax.lax.scan(step, h0, (seq_first(dt), seq_first(B_p), seq_first(C_p), seq_first(xc)))
        y = jnp.swapaxes(ys, 0, 1)
        y = y * _silu(z)
        return jnp.einsum('ble,de->bld', y, out_proj_w) + residual

    def _L1_xattn_ref(B, T, C, w, u, k, v):
        import jax, jax.numpy as jnp
        import numpy as np
        B_DIM, T_DIM, C_DIM = (16, 128, 256)

        def _wkv(w, u, k, v):
            Bn, Tn, Cn = k.shape
            NEG_INF = jnp.float32(-1e+38)

            def step(carry, kv_t):
                p, q, o = carry
                kt, vt = kv_t
                no = jnp.maximum(o, u + kt)
                A = jnp.exp(o - no)
                E = jnp.exp(u + kt - no)
                y = (A * p + E * vt) / (A * q + E)
                no2 = jnp.maximum(w + o, kt)
                A2 = jnp.exp(w + o - no2)
                E2 = jnp.exp(kt - no2)
                return ((A2 * p + E2 * vt, A2 * q + E2, no2), y)
            init = (jnp.zeros((Bn, Cn), k.dtype), jnp.zeros((Bn, Cn), k.dtype), jnp.full((Bn, Cn), NEG_INF, k.dtype))
            kT = jnp.moveaxis(k, 1, 0)
            vT = jnp.moveaxis(v, 1, 0)
            _, yT = jax.lax.scan(step, init, (kT, vT))
            return jnp.moveaxis(yT, 0, 1)
        return _wkv(w, u, k, v)

    def _L1_ffn_ref(x, w1, w2):
        import jax, jax.numpy as jnp
        import numpy as np
        DIM = 256
        INNER = 4 * DIM
        EPS = 1e-05

        def simple_rms_norm(x):
            d = x.shape[-1]
            n = jnp.linalg.norm(x, axis=-1, keepdims=True)
            return x / jnp.maximum(n, 1e-12) * jnp.sqrt(jnp.asarray(d, x.dtype))

        def activation_quant(x):
            scale = 127.0 / jnp.clip(jnp.max(jnp.abs(x), axis=-1, keepdims=True), EPS)
            return jnp.clip(jnp.round(x * scale), -128, 127) / scale

        def weight_quant(w):
            scale = 1.0 / jnp.clip(jnp.mean(jnp.abs(w)), EPS)
            return jnp.clip(jnp.round(w * scale), -1, 1) / scale

        def ste(x, q):
            return x + jax.lax.stop_gradient(q - x)

        def bitlinear158(x, w):
            xn = simple_rms_norm(x)
            xq = ste(xn, activation_quant(xn))
            wq = ste(w, weight_quant(w))
            return jnp.einsum('bsi,oi->bso', xq, wq)
        h = jax.nn.gelu(bitlinear158(x, w1), approximate=False)
        h = jax.nn.gelu(h, approximate=False)
        return bitlinear158(h, w2)
    x = x + _L0_attn_ref(_layernorm(x, axis=-1), L0_attn_w_query, L0_attn_wkv_a, L0_attn_wkv_b, L0_attn_kv_norm_w, L0_attn_out_proj_w)
    x = x + _L0_xattn_ref(_layernorm(x, axis=-1), ctx_2048, itok_BxS_0_1023, L0_xattn_W_kvc, L0_xattn_W_dq, L0_xattn_W_uq, L0_xattn_W_qr, L0_xattn_W_uk, L0_xattn_W_kr, L0_xattn_W_uv, L0_xattn_W_o)
    x = x + _L0_ffn_ref(_layernorm(x, axis=-1), L0_ffn_gate_w, L0_ffn_gate_b, L0_ffn_w_gate, L0_ffn_b_gate, L0_ffn_w_up, L0_ffn_b_up, L0_ffn_w_down, L0_ffn_b_down)
    x = x + _L1_attn_ref(_layernorm(x, axis=-1), L1_attn_norm_w, L1_attn_in_proj_w, L1_attn_conv_w, L1_attn_conv_b, L1_attn_x_proj_w, L1_attn_dt_w, L1_attn_dt_b, L1_attn_A_log, L1_attn_D_param, L1_attn_out_proj_w)
    x = x + _L1_xattn_ref(8, 128, 256, L1_xattn_w, L1_xattn_u, _layernorm(x, axis=-1), ctx_2048)
    x = x + _L1_ffn_ref(_layernorm(x, axis=-1), L1_ffn_w1, L1_ffn_w2)
    return x

_drawn_inputs = setup_inputs


def setup_inputs(seed=0):
    import zlib

    import numpy as np

    out = dict(_drawn_inputs(seed))
    spreads = {'L0_attn_kv_norm_w': (1.0, 0.6),
     'L0_ffn_gate_b': (0.0, 0.292),
     'L0_ffn_b_gate': (0.0, 0.8),
     'L0_ffn_b_up': (0.0, 0.8),
     'L0_ffn_b_down': (0.0, 0.1),
     'L1_attn_norm_w': (1.0, 0.6),
     'L1_attn_conv_b': (0.0, 0.8),
     'L1_attn_dt_b': (0.0, 0.8),
     'L1_attn_D_param': (1.0, 0.6)}
    factors = {'L0_attn_w_query': 2.683,
     'L0_ffn_w_gate': 3.076,
     'L0_ffn_w_up': 7.241,
     'L0_ffn_w_down': 2.878,
     'L1_attn_in_proj_w': 8.0,
     'L1_attn_conv_w': 8.0,
     'L1_attn_x_proj_w': 8.0,
     'L1_attn_dt_w': 8.0,
     'L1_attn_A_log': 8.0,
     'L1_attn_out_proj_w': 8.0,
     'L1_xattn_w': 64.0,
     'L1_xattn_u': 64.0,
     'L1_ffn_w1': 50.405,
     'L1_ffn_w2': 43.061}
    for name, (base, spread) in spreads.items():
        noise = np.random.default_rng([zlib.crc32(name.encode()), seed]).standard_normal(out[name].shape)
        drawn = base * np.exp(spread * noise) if base else spread * noise
        out[name] = jnp.asarray(drawn.astype(out[name].dtype))
    for name, factor in factors.items():
        out[name] = (out[name] * factor).astype(out[name].dtype)
    return out
```

```python
import concourse.bass as bass
from concourse import mybir
from contextlib import ExitStack

fp32 = mybir.dt.float32
bf16 = mybir.dt.bfloat16
i32 = mybir.dt.int32
u32 = mybir.dt.uint32
ALU = mybir.AluOpType
ACT = mybir.ActivationFunctionType
AX = mybir.AxisListType

P = 128
NB = 8
D = 256
DC = D // P
T = NB * P
H = 16
R = 64
GH = 4
NG = H // GH
QC = 96
VH = 128
E = 32
TOPK = 4
I = 128
NBLK = 64
DI = 512
CT = DI // P
ST = 16
KCONV = 4
PAD = KCONV - 1
INNER = 1024
IC = INNER // P
NEG = -1.0e30
MAGIC = 12582912.0
LN_EPS = 1e-5


class Chain:

    def __init__(self, eng, sem):
        self.eng, self.sem, self.base, self.n = eng, sem, 0, 0

    def mark(self, ins):
        ins.then_inc(self.sem, 1)
        self.n += 1

    def wait(self):
        self.eng.wait_ge(self.sem, self.base + self.n)

    def link(self, ins):
        self.mark(ins)
        self.wait()

    def enter(self, i, per):
        self.before, self.per = self.n, per
        self.base, self.n = self.n + i * per, 0

    def leave(self, rounds):
        assert self.n == self.per, (self.n, self.per)
        self.base, self.n = 0, self.before + rounds * self.per


def decoder(nc, a, out):
    ctx = ExitStack()
    with ctx:
        def sem(name):
            return nc.alloc_semaphore(name=name)

        WORDS = 53200

        arena = ctx.enter_context(nc.sbuf_tensor("arena", [P, WORDS], fp32))
        ps = ctx.enter_context(nc.psum_tensor("ps", [P, 8, 512], fp32))
        first_layer = ExitStack()
        first_layer.enter_context(nc.cleanup_on_exit())

        psb = ps[:, :, :].bitcast(bf16)

        def view(at, n, pat=None, dt=fp32, parts=P, **dims):
            assert at + n <= WORDS, (at, n)
            v = arena[0:parts, at:at + n]
            if dt is not fp32:
                v = v.bitcast(dt)
            return v.rearrange(pat, **dims) if pat else v

        x = view(0, 2048, "p (b f) -> p b f", b=NB)
        hT = view(2048, 2048, "p (c t) -> p c t", c=DC)
        h = view(4096, 2048, "p (b f) -> p b f", b=NB)
        ctxT0 = view(4096, 2048, "p (c t) -> p c t", c=DC)
        at = 6144
        ident = view(at, P); at += P
        ones = view(at, P); at += P
        maskA = view(at, P); at += P
        maskX = view(at, 1024, "p (b t) -> p b t", b=NB); at += 1024
        rope = {}
        for name in "AX":
            rope[name] = (view(at, 256, "p (e t) -> p e t", e=2), view(at + 256, P)); at += 384
        tri_b = view(at, 64, dt=bf16); at += 64
        ones_b = view(at, 64, dt=bf16); at += 64
        ident_b = view(at, 64, dt=bf16); at += 64
        stats = view(at, NB * 6, "p (b k) -> p b k", b=NB); at += NB * 6
        mv = view(at, NB * 2, "p (b k) -> p b k", b=NB); at += NB * 2
        var_eps = view(at, NB); at += NB
        rstd = view(at, NB); at += NB
        sumsq = view(at, NB); at += NB
        neg_half = view(at, 1); at += 1
        kv_norm = view(at, 1); at += 1
        small = view(at, 256); at += 256
        zeros = view(at, 256); at += 256
        assert at <= 9216
        W0 = 9216
        A0 = W0 + 16384
        X0 = A0 + 11520
        K0 = X0 + 9728
        assert K0 + 5504 <= WORDS, K0

        layer = {}
        for name, base, kc, cw in (("A", A0, P, DC), ("X", X0, QC, 1)):
            o = base
            L = {"kc": kc, "chunks": cw}
            L["wq"] = view(o, cw * 2048, "p (c h m) -> p c h m", c=cw, h=H); o += cw * 2048
            L["wqs"] = view(o, cw * 1024, "p (c h m) -> p c h m", c=cw, h=H // 2); o += cw * 1024
            L["wvo"] = view(o, 2048, "p (h m) -> p h m", h=H // 2); o += 2048
            L["wkv"] = view(o, 768, "p (e c m) -> p e c m", e=3, c=DC); o += 768
            L["key"] = view(o, 2048, "p (e t) -> p e t", e=2); o += 2048
            L["kvn"] = view(o, 512, "p (b r) -> p b r", b=NB); o += 512
            if name == "X":
                L["wdq"] = view(o, 192, "p (c m) -> p c m", c=DC); o += 192
                L["qc"] = view(o, 1024); o += 1024
            L["cos"], L["sin"] = rope[name]
            layer[name] = L
            assert o <= (X0 if name == "A" else K0), o
        rawA = W0
        wqnT = view(rawA, 4096, "p (h f) -> p h f", h=H)
        kbT = view(rawA + 4096, 1024, "p (h r) -> p h r", h=H)
        wvT = {"A": view(rawA + 5120, 2048, "p (h r) -> p h r", h=H)}
        wo = {"A": view(rawA + 7168, 4096, "p (h f) -> p h f", h=H)}
        rawX = rawA + 11264
        wuqT = view(rawX, 1536, "p (h q) -> p h q", h=H)
        wukT = view(rawX + 1536, 1024, "p (h r) -> p h r", h=H)
        wvT["X"] = view(rawX + 2560, 2048, "p (h r) -> p h r", h=H)
        wkvcT = view(rawX + 4608, 256)
        wkr2 = view(rawX + 4864, 128)
        wo["X"] = view(K0, 4096, "p (h f) -> p h f", h=H)
        o = K0 + 4096
        keytmp = view(o, 1024, "p (e t) -> p e t", e=2)
        o = K0
        q = view(o, 1024, "p (d h s) -> p d h s", d=2, h=GH); o += 1024
        qsw = view(o, 512, "p (d h s) -> p d h s", d=2, h=GH // 2); o += 512
        sm = view(o, 1024, "p (d h t) -> p d h t", d=2, h=GH); o += 1024
        pr = view(o, 1024, "p (d h t) -> p d h t", d=2, h=GH); o += 1024
        prT = view(o, 1024, "p (d m) -> p d m", d=2); o += 1024
        uT = view(o, 512, "p (d h s) -> p d h s", d=2, h=GH // 2); o += 512
        kvn2 = view(o, 128); o += 128
        mx = view(o, 8, "p (d h) -> p d h", d=2); o += 8
        negm = view(o, 8, "p (d h) -> p d h", d=2); o += 8
        rsum = view(o, 8, "p (d h) -> p d h", d=2); o += 8
        rinv = view(o, 8, "p (d h) -> p d h", d=2); o += 8
        assert o <= WORDS

        class Norm:

            def __init__(self, tag, rms=False):
                self.rms = rms
                if rms:
                    self.ln_ready = sem(tag + "_ln_ready")
                    self.sumsq_ready = sem(tag + "_sumsq")
                    self.added = sem(tag + "_ln_added")
                self.stats_in = sem(tag + "_stats_in")
                self.var_ready = sem(tag + "_var_ready")
                self.rstd_ready = sem(tag + "_rstd_ready")
                self.h_ready = sem(tag + "_h_ready")
                self.hT_done = sem(tag + "_hT_done")
                self.hT_ready = sem(tag + "_hT_ready")

            def dve(self, eng):
                for b in range(NB):
                    eng.bn_stats(stats[:, b, :], x[:, b, :]).then_inc(self.stats_in, 1)
                eng.wait_ge(self.stats_in, NB)
                for b in range(NB):
                    eng.bn_aggr(mv[:, b, :], stats[:, b, :]).then_inc(self.var_ready, 1)
                eng.wait_ge(self.rstd_ready, 2)
                eng.wait_ge(self.var_ready, NB)
                for b in range(NB):
                    eng.tensor_scalar(h[:, b, :], x[:, b, :], mv[:, b, 0:1], rstd[:, b:b + 1], ALU.subtract,
                                      ALU.mult).then_inc(self.ln_ready if self.rms else self.h_ready, 1)
                if self.rms:
                    for b in range(NB):
                        eng.wait_ge(self.ln_ready, b + 1)
                        eng.tensor_tensor(x[:, b, :], x[:, b, :], h[:, b, :], ALU.add).then_inc(self.added, 1)
                    eng.wait_ge(self.rstd_ready, 4)
                    for b in range(NB):
                        eng.wait_ge(self.added, b + 1)
                        eng.tensor_scalar(h[:, b, :], h[:, b, :], rstd[:, b:b + 1], None,
                                          ALU.mult).then_inc(self.h_ready, 1)

            def pool(self, eng):
                eng.wait_ge(self.var_ready, NB)
                eng.tensor_scalar(var_eps, mv[:, :, 1], LN_EPS, None, ALU.add).then_inc(self.rstd_ready, 1)
                eng.wait_ge(self.rstd_ready, 1)
                eng.tensor_tensor(rstd, var_eps, neg_half.to_broadcast([P, NB]), ALU.pow).then_inc(self.rstd_ready, 1)
                if self.rms:
                    eng.wait_ge(self.sumsq_ready, NB)
                    eng.wait_ge(self.ln_ready, NB)
                    eng.wait_ge(self.rstd_ready, 2)
                    eng.tensor_scalar(var_eps, sumsq, 1.0 / D, LN_EPS, ALU.mult, ALU.add).then_inc(self.rstd_ready, 1)
                    eng.wait_ge(self.rstd_ready, 3)
                    eng.tensor_tensor(rstd, var_eps, neg_half.to_broadcast([P, NB]), ALU.pow).then_inc(self.rstd_ready, 1)

            def pe(self, eng):
                for b in range(NB):
                    eng.wait_ge(self.h_ready, b + 1)
                    if b % 2 == 0 and b >= 4:
                        eng.wait_ge(self.hT_ready, b // 2 - 1)
                    for c in range(DC):
                        at = (b % 2) * D + c * P
                        t = eng.transpose(ps[:, (b // 2) % 2, at:at + P], h[:, b, c * P:(c + 1) * P], ident)
                    if b % 2:
                        t.then_inc(self.hT_done, 1)

            def act(self, eng, scale=None):
                if self.rms:
                    for b in range(NB):
                        eng.wait_ge(self.ln_ready, b + 1)
                        if b:
                            eng.wait_ge(self.sumsq_ready, b)
                        eng.activation(zeros, h[:, b, :], ACT.Square,
                                       accum_out=sumsq[:, b:b + 1]).then_inc(self.sumsq_ready, 1)
                for k in range(NB // 2):
                    eng.wait_ge(self.hT_done, k + 1)
                    src = ps[:, k % 2, :].rearrange("p (b c t) -> p c b t", b=2, c=DC)
                    dst = hT[:, :, k * D:(k + 1) * D].rearrange("p c (b t) -> p c b t", b=2)
                    if scale is None:
                        eng.activation(dst, src, ACT.Copy).then_inc(self.hT_ready, 1)
                    else:
                        for c in range(DC):
                            t = eng.activation(dst[:, c], src[:, c], ACT.Copy, scale=scale[:, c:c + 1])
                        t.then_inc(self.hT_ready, 1)

        class Keys:

            def __init__(self, tag):
                self.raw = sem(tag + "_key_raw")
                self.scaled = sem(tag + "_key_scaled")
                self.rotated = sem(tag + "_key_rotated")
                self.sq = sem(tag + "_key_sq")
                self.ssq = sem(tag + "_key_ssq")
                self.inv = sem(tag + "_key_inv")
                self.tok_done = sem(tag + "_kvn_done")
                self.tok = sem(tag + "_kvn")

        def pe_keys(eng, L, K, src, rms):
            for half in range(2):
                ts = slice(half * 512, half * 512 + 512)
                if half:
                    eng.wait_ge(K.scaled, 3)
                for e in range(3):
                    for c in range(DC):
                        t = eng.matmul(ps[:, 5 + e, :], L["wkv"][:, e, c, :], src[:, c, ts],
                                       start=c == 0, stop=c == DC - 1)
                t.then_inc(K.raw, 1)
                if rms:
                    eng.wait_ge(K.sq, half + 1)
                    eng.matmul(ps[:, 4, :], ones[0:R, :], keytmp[0:R, 1, :], start=True, stop=True).then_inc(K.ssq, 1)
            eng.wait_ge(K.rotated, 2)
            for b in range(NB):
                t = eng.transpose(ps[:, 4, b * R:(b + 1) * R], L["key"][0:R, 0, b * P:(b + 1) * P], ident[0:R, 0:R])
            t.then_inc(K.tok_done, 1)

        def dve_keys(eng, ch, L, K, rms):
            for half in range(2):
                ts = slice(half * 512, half * 512 + 512)
                t4 = "p (b t) -> p b t"
                eng.wait_ge(K.raw, half + 1)
                for e in range(2):
                    tab = L["cos"][:, e, :].unsqueeze(1).to_broadcast([P, 4, P])
                    eng.tensor_tensor(L["key"][:, e, ts].rearrange(t4, b=4), ps[:, 5 + e, :].rearrange(t4, b=4),
                                      tab, ALU.mult).then_inc(K.scaled, 1)
                tab = L["sin"].unsqueeze(1).to_broadcast([P, 4, P])
                eng.tensor_tensor(keytmp[:, 0, :].rearrange(t4, b=4), ps[:, 7, :].rearrange(t4, b=4),
                                  tab, ALU.mult).then_inc(K.scaled, 1)
                eng.wait_ge(K.scaled, 3 * half + 3)
                ch.mark(eng.tensor_tensor(L["key"][R:P, 0, ts], L["key"][R:P, 0, ts], keytmp[R:P, 0, :], ALU.add))
                last = eng.tensor_tensor(L["key"][0:R, 1, ts], L["key"][0:R, 1, ts], keytmp[0:R, 0, :], ALU.add)
                if rms:
                    ch.mark(last)
                    eng.wait_ge(K.ssq, half + 1)
                    eng.tensor_scalar(keytmp[:, 1, :], ps[:, 4, :], 1.0 / R, 1e-6, ALU.mult, ALU.add).then_inc(K.inv, 1)
                    eng.wait_ge(K.inv, 3 * half + 2)
                    eng.reciprocal(keytmp[:, 1, :], keytmp[:, 1, :]).then_inc(K.inv, 1)
                    eng.wait_ge(K.inv, 3 * half + 3)
                    ch.mark(eng.scalar_tensor_tensor(L["key"][0:R, 0, ts], L["key"][0:R, 0, ts], kv_norm[0:R, :],
                                                     keytmp[0:R, 1, :], ALU.mult, ALU.mult))
                    last = eng.scalar_tensor_tensor(L["key"][R:P, 1, ts], L["key"][R:P, 1, ts], kv_norm[R:P, :],
                                                    keytmp[R:P, 1, :], ALU.mult, ALU.mult)
                ch.wait()
                last.then_inc(K.rotated, 1)
                eng.wait_ge(K.rotated, half + 1)

        def act_keys(eng, L, K, rms):
            if rms:
                for half in range(2):
                    eng.wait_ge(K.scaled, 3 * half + 1)
                    if half:
                        eng.wait_ge(K.rotated, 1)
                    eng.activation(keytmp[0:R, 1, :], ps[0:R, 5, :], ACT.Square).then_inc(K.sq, 1)
                    eng.wait_ge(K.inv, 3 * half + 1)
                    eng.activation(keytmp[:, 1, :], keytmp[:, 1, :], ACT.Sqrt).then_inc(K.inv, 1)
            eng.wait_ge(K.tok_done, 1)
            eng.activation(L["kvn"], ps[:, 4, :].rearrange("p (b r) -> p b r", b=NB), ACT.Copy).then_inc(K.tok, 1)

        loads = {}

        def load(eng, name, dst, src):
            if name not in loads:
                loads[name] = [sem("ld_" + name), 0]
            loads[name][1] += 16
            eng.dma_start(dst, src).then_inc(loads[name][0], 16)

        def loaded(eng, *names):
            for n in names:
                eng.wait_ge(loads[n][0], loads[n][1])

        s_const = sem("const_step")
        s_seg = sem("mask_step")
        kr_done, kr_ready = sem("kr_done"), sem("kr_ready")
        absX_done, absX_ready = sem("absX_done"), sem("absX_ready")
        absA_done, absA_ready = sem("absA_done"), sem("absA_ready")
        vo_done, vo_even, vo_odd = sem("vo_done"), sem("vo_even"), sem("vo_odd")
        s_zero = sem("zeros_ready")
        keysX, keysA = Keys("X"), Keys("A")
        normA = Norm("nA")
        s_ch1 = sem("dve_chain1")
        LA, LX = layer["A"], layer["X"]
        NCONST = 6

        with nc.Block() as block:
            @block.sync
            def _(eng):
                load(eng, "ctx", ctxT0, a["ctxT"])
                load(eng, "kvX", wkvcT[0:R, :], a["X_kvcT"])
                load(eng, "kvX", wkr2[0:R, :], a["X_kr2"])
                load(eng, "kvX", LX["wkv"][:, 0, :, 0:R], a["X_kvc"])
                load(eng, "kvX", LX["wkv"][:, 1, :, R:P], a["X_kvc"])
                for name in "XA":
                    load(eng, "rope" + name, rope[name][0], a["cos" + name])
                    load(eng, "rope" + name, rope[name][1], a["sin" + name])
                load(eng, "x", x, a["x"])
                load(eng, "absX", wuqT, a["X_uqT"])
                load(eng, "absX", wukT, a["X_ukT"])
                load(eng, "kvA", LA["wkv"], a["A_wkv"])
                load(eng, "kvA", kv_norm, a["A_norm"])
                load(eng, "absA", wqnT[0:R], a["A_qnT"])
                load(eng, "absA", kbT[0:R], a["A_kbT"])
                load(eng, "voX", wvT["X"], a["X_vT"])
                load(eng, "voX", wo["X"], a["X_o"])
                load(eng, "voA", wvT["A"], a["A_vT"])
                load(eng, "voA", wo["A"], a["A_o"])
                load(eng, "qX", LX["wq"][0:QC, 0].rearrange("p (q e) m -> p q (e m)", e=2)[:, :, R:P + R], a["X_qr"])
                load(eng, "qX", LX["wqs"][0:QC, 0], a["X_qrs"])
                load(eng, "qX", LX["wdq"], a["X_dq"])
                for c in range(DC):
                    load(eng, "qA", LA["wq"][:, c].rearrange("p (q e) m -> p q (e m)", e=2)[:, :, R:P + R],
                         a["A_qr"][:, c])
                load(eng, "qA", LA["wqs"], a["A_qrs"])
                load(eng, "seg", small[:, 0:NB].bitcast(i32), a["seg"])

            @block.gpsimd
            def _(eng):
                eng.memset(zeros, 0.0).then_inc(s_zero, 1)
                eng.memset(ident, 0.0).then_inc(s_const, 1)
                eng.memset(maskA, 0.0).then_inc(s_const, 1)
                eng.memset(ones, 1.0).then_inc(s_const, 1)
                eng.memset(neg_half, -0.5).then_inc(s_const, 1)
                eng.wait_ge(s_const, 2)
                eng.affine_select(out=ident, in_=ident, compare_op=ALU.not_equal, fill=1.0, base=0,
                                  pattern=[[-1, P]], channel_multiplier=1).then_inc(s_const, 1)
                eng.affine_select(out=maskA, in_=maskA, compare_op=ALU.is_ge, fill=NEG, base=0,
                                  pattern=[[-1, P]], channel_multiplier=1).then_inc(s_const, 1)
                eng.memset(small[:, 128:256], 1.0).then_inc(s_const, 1)
                eng.wait_ge(s_const, 7)
                eng.affine_select(out=small[:, 128:256], in_=small[:, 128:256], compare_op=ALU.is_gt, fill=0.0, base=0,
                                  pattern=[[1, P]], channel_multiplier=-1).then_inc(s_const, 1)
                eng.wait_ge(s_const, 8)
                eng.tensor_copy(tri_b, small[:, 128:256]).then_inc(s_const, 1)
                eng.tensor_copy(ones_b, ones).then_inc(s_const, 1)
                eng.tensor_copy(ident_b, ident).then_inc(s_const, 1)
                eng.iota(maskX[:, :, :], pattern=[[0, NB], [1, P]], base=0, channel_multiplier=0,
                         allow_small_or_imprecise_dtypes=True).then_inc(s_const, 1)
                normA.pool(eng)

            @block.vector
            def _(eng):
                ch = Chain(eng, s_ch1)
                loaded(eng, "x")
                eng.wait_ge(s_const, 4)
                eng.wait_ge(kr_done, 1)
                src = ps[:, 0, 0:256].rearrange("p (c m) -> p c m", c=DC)
                for k, dst in enumerate((LX["wkv"][:, 0, :, R:P], LX["wkv"][:, 1, :, 0:R],
                                         LX["wkv"][:, 2, :, 0:R], LX["wkv"][:, 2, :, R:P])):
                    eng.tensor_copy(dst, src[:, :, R * (k // 2):R * (k // 2) + R]).then_inc(kr_ready, 1)
                loaded(eng, "ropeX")
                dve_keys(eng, ch, LX, keysX, False)
                eng.wait_ge(keysX.raw, 2)
                normA.dve(eng)
                loaded(eng, "seg")
                eng.wait_ge(s_const, 12)
                eng.tensor_copy(small[:, 16:16 + NB], small[:, 0:NB].bitcast(i32)).then_inc(s_seg, 1)
                eng.wait_ge(s_seg, 1)
                for b in range(NB):
                    eng.tensor_scalar(maskX[:, b, :], maskX[:, b, :], small[:, 16 + b:17 + b], None,
                                      ALU.subtract).then_inc(s_seg, 1)
                flat = maskX.rearrange("p b t -> p (b t)")
                late = view(rawA, 1024)
                eng.wait_ge(s_seg, 1 + NB)
                eng.wait_ge(absA_done, 4)
                eng.tensor_scalar(late, flat, 0.0, NEG, ALU.is_gt, ALU.mult).then_inc(s_seg, 1)
                eng.wait_ge(s_seg, 2 + NB)
                eng.tensor_scalar(flat, flat, -8.0, NEG, ALU.is_lt, ALU.mult).then_inc(s_seg, 1)
                eng.wait_ge(s_seg, 3 + NB)
                eng.tensor_tensor(flat, flat, late, ALU.add).then_inc(s_seg, 1)
                for n in range(H):
                    L, p = (LX, n) if n < 8 else (LA, n - 8)
                    eng.wait_ge(vo_done, n + 1)
                    eng.tensor_copy(L["wvo"][R:P, p, :], ps[R:P, 2 + n % 2, D:2 * D]).then_inc(vo_odd, 1)
                loaded(eng, "kvA", "ropeA")
                dve_keys(eng, ch, LA, keysA, True)

            @block.scalar
            def _(eng):
                for g in range(2):
                    eng.wait_ge(absX_done, g + 1)
                    for e in range(2):
                        dst = LX["wq"][0:QC, 0, 8 * g:8 * g + 8].rearrange("p (q e) m -> p q (e m)", e=2)
                        src = ps[0:QC, g, :].rearrange("p (q e r) -> p q e r", q=4, e=2)
                        t = eng.activation(dst[:, :, 192 * e:192 * e + R], src[:, :, e], ACT.Copy)
                    t.then_inc(absX_ready, 1)
                act_keys(eng, LX, keysX, False)
                for k in range(4):
                    c, g = k // 2, k % 2
                    eng.wait_ge(absA_done, k + 1)
                    for e in range(2):
                        dst = LA["wq"][:, c, 8 * g:8 * g + 8].rearrange("p (q e) m -> p q (e m)", e=2)
                        src = ps[:, k % 2, :].rearrange("p (q e r) -> p q e r", q=4, e=2)
                        t = eng.activation(dst[:, :, 192 * e:192 * e + R], src[:, :, e], ACT.Copy)
                    t.then_inc(absA_ready, 1)
                for n in range(H):
                    L, p = (LX, n) if n < 8 else (LA, n - 8)
                    eng.wait_ge(vo_done, n + 1)
                    eng.activation(L["wvo"][0:R, p, :], ps[0:R, 2 + n % 2, 0:D], ACT.Copy).then_inc(vo_even, 1)
                normA.act(eng)
                act_keys(eng, LA, keysA, True)

            @block.tensor
            def _(eng):
                loaded(eng, "kvX")
                for c in range(DC):
                    t = eng.matmul(ps[:, 0, c * P:(c + 1) * P], wkvcT[0:R, c * P:(c + 1) * P], wkr2[0:R, :],
                                   start=True, stop=True)
                t.then_inc(kr_done, 1)
                loaded(eng, "ctx")
                eng.wait_ge(kr_ready, 4)
                eng.wait_ge(s_const, 6)
                pe_keys_done = pe_keys(eng, LX, keysX, ctxT0, False)
                loaded(eng, "absX")
                for g in range(2):
                    for j in range(8):
                        hd = 8 * g + j
                        t = eng.matmul(ps[0:QC, g, j * R:(j + 1) * R], wuqT[:, hd, :], wukT[:, hd, :],
                                       start=True, stop=True)
                    t.then_inc(absX_done, 1)
                loaded(eng, "absA")
                for k in range(4):
                    c, g = k // 2, k % 2
                    if k < 2:
                        eng.wait_ge(absX_ready, k + 1)
                    else:
                        eng.wait_ge(absA_ready, k - 1)
                    for j in range(8):
                        hd = 8 * g + j
                        t = eng.matmul(ps[:, k % 2, j * R:(j + 1) * R], wqnT[0:R, hd, c * P:(c + 1) * P],
                                       kbT[0:R, hd, :], start=True, stop=True)
                    t.then_inc(absA_done, 1)
                loaded(eng, "voX", "voA")
                for n in range(H):
                    name, p = ("X", n) if n < 8 else ("A", n - 8)
                    if n >= 2:
                        eng.wait_ge(vo_even, n - 1)
                        eng.wait_ge(vo_odd, n - 1)
                    for e in range(2):
                        t = eng.matmul(ps[:, 2 + n % 2, e * D:(e + 1) * D], wvT[name][:, 2 * p + e, :],
                                       wo[name][:, 2 * p + e, :], start=True, stop=True)
                    t.then_inc(vo_done, 1)
                eng.wait_ge(absA_ready, 4)
                normA.pe(eng)
                eng.wait_ge(normA.hT_ready, 4)
                loaded(eng, "kvA")
                eng.wait_ge(keysX.tok, 1)
                pe_keys(eng, LA, keysA, hT, True)

        def near(b, g, off):
            g += off
            return (b - 1, g + 4) if g < 0 else (b + 1, g - 4) if g > 3 else (b, g)

        def four(stages, b, first, last):
            for g in range(4):
                for off, emit in stages:
                    if not ((first and g + off < 0) or (last and g + off > 3)):
                        emit(*near(b, g, off))

        def pipeline(eng, rounds, stages, ahead, behind):
            for off, emit in ahead:
                emit(0, off)
            four(stages, 0, True, False)
            with eng.Fori(1, rounds - 1) as b:
                four(stages, b, False, False)
            four(stages, rounds - 1, False, True)
            for off, emit in behind:
                emit(rounds - 1, off)

        def attention(tag, L, scale, mask, per_batch_mask, prefetch):
            q_done, q_scaled, q_roped = sem(tag + "_q_done"), sem(tag + "_q_scaled"), sem(tag + "_q_roped")
            sc_done, masked, negm_ready = sem(tag + "_scores_done"), sem(tag + "_masked"), sem(tag + "_negm_ready")
            mx_ready = sem(tag + "_mx_ready")
            exp_done, rinv_ready, pr_ready = sem(tag + "_exp_done"), sem(tag + "_rinv_ready"), sem(tag + "_pr_ready")
            prT_done, prT_ready = sem(tag + "_prT_done"), sem(tag + "_prT_ready")
            u_done, uT_ready, o_done = sem(tag + "_u_done"), sem(tag + "_uT_ready"), sem(tag + "_o_done")
            kvn_ready, res_ready = sem(tag + "_kvn_ready"), sem(tag + "_res_ready")
            kc, chunks = L["kc"], L["chunks"]
            psQ, psW, psS, psT, psU, psO = 0, 2, 3, 5, 6, 7
            src = hT if chunks == DC else L["qc"].unsqueeze(1)

            def tok(b):
                return bass.ds(b * P, P)

            def pe_queries(eng, b, g):
                d, s = g % 2, 4 * b + g
                if not (isinstance(b, int) and s < 1):
                    eng.wait_ge(q_scaled, s)
                for j in range(GH):
                    for c in range(chunks):
                        eng.matmul(ps[:, psQ + d, j * P:(j + 1) * P], L["wq"][0:kc, c, GH * g + j, :],
                                   src[0:kc, c, tok(b)], start=c == 0, stop=c == chunks - 1)
                for j in range(GH // 2):
                    for c in range(chunks):
                        t = eng.matmul(ps[:, psW, j * P:(j + 1) * P],
                                       L["wqs"][0:kc, c, GH // 2 * g + j, :], src[0:kc, c, tok(b)],
                                       start=c == 0, stop=c == chunks - 1)
                t.then_inc(q_done, 1)

            def pe_scores(eng, b, g):
                d, s = g % 2, 4 * b + g
                eng.wait_ge(q_roped, s + 1)
                if not (isinstance(b, int) and s < 2):
                    eng.wait_ge(masked, s - 1)
                for j in range(GH):
                    t = eng.matmul(ps[:, psS + d, j * P:(j + 1) * P], q[:, d, j, :],
                                   L["key"][:, j % 2, tok(b)], start=True, stop=True)
                t.then_inc(sc_done, 1)

            def pe_transpose(eng, b, g):
                d, s = g % 2, 4 * b + g
                eng.wait_ge(pr_ready, s + 1)
                if not (isinstance(b, int) and s < 1):
                    eng.wait_ge(prT_ready, s)
                for j in range(GH):
                    t = eng.transpose(ps[:, psT, j * P:(j + 1) * P], pr[:, d, j, :], ident)
                t.then_inc(prT_done, 1)

            def pe_values(eng, b, g):
                d, s = g % 2, 4 * b + g
                eng.wait_ge(prT_ready, s + 1)
                if not (isinstance(b, int) and s < 1):
                    eng.wait_ge(uT_ready, s)
                if g == 0:
                    eng.wait_ge(kvn_ready, b + 1)
                eng.matmul(ps[:, psU, :], kvn2, prT[:, d, :], start=True, stop=True).then_inc(u_done, 1)

            def pe_output(eng, b, g):
                d, s = g % 2, 4 * b + g
                eng.wait_ge(uT_ready, s + 1)
                if g == 0 and not (isinstance(b, int) and b < 1):
                    eng.wait_ge(res_ready, b)
                for j in range(GH // 2):
                    t = eng.matmul(ps[:, psO, 0:D], uT[:, d, j, :], L["wvo"][:, GH // 2 * g + j, :],
                                   start=g == 0 and j == 0, stop=g == NG - 1 and j == GH // 2 - 1)
                t.then_inc(o_done, 1)

            def dve_queries(eng, b, g):
                d, s = g % 2, 4 * b + g
                eng.wait_ge(q_done, s + 1)
                if not (isinstance(b, int) and s < 2):
                    eng.wait_ge(sc_done, s - 1)
                eng.tensor_tensor(q[:, d].rearrange("p (a e) s -> p a e s", e=2),
                                  ps[:, psQ + d, :].rearrange("p (a e s) -> p a e s", a=2, e=2),
                                  L["cos"].unsqueeze(1).to_broadcast([P, 2, 2, P]), ALU.mult)
                eng.tensor_tensor(qsw[:, d], ps[:, psW, 0:D].rearrange("p (a s) -> p a s", a=2),
                                  L["sin"].unsqueeze(1).to_broadcast([P, 2, P]), ALU.mult).then_inc(q_scaled, 1)
                eng.wait_ge(q_scaled, s + 1)
                qe = q[:, d].rearrange("p (a e) s -> p a e s", e=2)
                eng.tensor_tensor(qe[R:P, :, 0], qe[R:P, :, 0], qsw[R:P, d], ALU.add)
                eng.tensor_tensor(qe[0:R, :, 1], qe[0:R, :, 1], qsw[0:R, d], ALU.add).then_inc(q_roped, 1)

            def dve_softmax(eng, b, g):
                d, s = g % 2, 4 * b + g
                eng.wait_ge(sc_done, s + 1)
                if not (isinstance(b, int) and s < 2):
                    eng.wait_ge(exp_done, s - 1)
                m = mask[:, b, :] if per_batch_mask and isinstance(b, int) else (
                    mask[:, bass.ds(b, 1), :].rearrange("p a t -> p (a t)") if per_batch_mask else mask)
                eng.tensor_tensor(sm[:, d], ps[:, psS + d, :].rearrange("p (h t) -> p h t", h=GH),
                                  m.unsqueeze(1).to_broadcast([P, GH, P]), ALU.add).then_inc(masked, 1)
                eng.wait_ge(masked, s + 1)
                eng.tensor_reduce(mx[:, d], sm[:, d], AX.X, ALU.max).then_inc(mx_ready, 1)
                eng.wait_ge(mx_ready, s + 1)
                eng.tensor_scalar(negm[:, d], mx[:, d], -scale, None, ALU.mult).then_inc(negm_ready, 1)

            def dve_inverse(eng, b, g):
                d, s = g % 2, 4 * b + g
                eng.wait_ge(exp_done, s + 1)
                if not (isinstance(b, int) and s < 2):
                    eng.wait_ge(pr_ready, s - 1)
                eng.reciprocal(rinv[:, d], rsum[:, d]).then_inc(rinv_ready, 1)

            def dve_residual(eng, b):
                eng.wait_ge(o_done, 4 * b + 4)
                eng.tensor_tensor(x[:, bass.ds(b, 1), :].rearrange("p a f -> p (a f)"),
                                  x[:, bass.ds(b, 1), :].rearrange("p a f -> p (a f)"),
                                  ps[:, psO, 0:D], ALU.add).then_inc(res_ready, 1)

            def act_exp(eng, b, g):
                d, s = g % 2, 4 * b + g
                eng.wait_ge(negm_ready, s + 1)
                if not (isinstance(b, int) and s < 2):
                    eng.wait_ge(prT_done, s - 1)
                for j in range(GH):
                    t = eng.activation(pr[:, d, j, :], sm[:, d, j, :], ACT.Exp, bias=negm[:, d, j:j + 1],
                                       scale=scale, accum_out=rsum[:, d, j:j + 1])
                t.then_inc(exp_done, 1)

            def act_probs(eng, b, g):
                d, s = g % 2, 4 * b + g
                eng.wait_ge(prT_done, s + 1)
                if not (isinstance(b, int) and s < 2):
                    eng.wait_ge(u_done, s - 1)
                eng.activation(prT[:, d, :], ps[:, psT, :], ACT.Copy).then_inc(prT_ready, 1)

            def act_values(eng, b, g):
                d, s = g % 2, 4 * b + g
                eng.wait_ge(u_done, s + 1)
                if not (isinstance(b, int) and s < 2):
                    eng.wait_ge(o_done, s - 1)
                pu = ps[:, psU, :].rearrange("p (a e s) -> p a e s", a=2, e=2)
                eng.activation(uT[0:R, d], pu[0:R, :, 0], ACT.Copy)
                eng.activation(uT[R:P, d], pu[R:P, :, 1], ACT.Copy).then_inc(uT_ready, 1)

            def pool_norm(eng, b, g):
                d, s = g % 2, 4 * b + g
                eng.wait_ge(rinv_ready, s + 1)
                eng.tensor_tensor(pr[:, d], pr[:, d], rinv[:, d].unsqueeze(2).to_broadcast([P, GH, P]),
                                  ALU.mult).then_inc(pr_ready, 1)

            def pool_latents(eng, b):
                if not (isinstance(b, int) and b < 1):
                    eng.wait_ge(u_done, 4 * b)
                eng.tensor_copy(kvn2.rearrange("p (e r) -> p e r", e=2),
                                L["kvn"][:, bass.ds(b, 1), :].to_broadcast([P, 2, R])).then_inc(kvn_ready, 1)

            with nc.Block() as block:
                @block.tensor
                def _(eng):
                    Q = lambda b, g: pe_queries(eng, b, g)
                    S = lambda b, g: pe_scores(eng, b, g)
                    TR = lambda b, g: pe_transpose(eng, b, g)
                    U = lambda b, g: pe_values(eng, b, g)
                    O = lambda b, g: pe_output(eng, b, g)
                    pipeline(eng, NB, [(-2, O), (-1, U), (1, S), (2, Q), (0, TR)],
                                 [(0, Q), (1, Q), (0, S)], [(2, O), (3, U), (3, O)])

                @block.vector
                def _(eng):
                    SF = lambda b, g: dve_softmax(eng, b, g)
                    QS = lambda b, g: dve_queries(eng, b, g)
                    IN = lambda b, g: dve_inverse(eng, b, g)

                    def RS(b, g):
                        if g == NG - 1:
                            dve_residual(eng, b)
                    pipeline(eng, NB, [(0, IN), (-2, RS), (1, SF), (2, QS)],
                                 [(0, QS), (1, QS), (0, SF)], [(2, RS), (3, RS)])

                @block.scalar
                def _(eng):
                    EX = lambda b, g: act_exp(eng, b, g)
                    PT = lambda b, g: act_probs(eng, b, g)
                    UT = lambda b, g: act_values(eng, b, g)
                    pipeline(eng, NB, [(-1, UT), (0, PT), (1, EX)], [(0, EX)], [(3, UT)])

                @block.gpsimd
                def _(eng):
                    NO = lambda b, g: pool_norm(eng, b, g)

                    def LT(b, g):
                        if g == 0:
                            pool_latents(eng, b)
                    pipeline(eng, NB, [(0, NO), (0, LT)], [], [])

                @block.sync
                def _(eng):
                    prefetch(eng)

        wgu = view(W0, 16384, "p (c e m) -> p c e m", c=DC, e=E)
        xs = nc.dram_tensor("expert_in", (NBLK * P, D), fp32).ap()
        ys = nc.dram_tensor("expert_out", (NBLK * P, D), fp32).ap()

        def prefetch_up(eng):
            for e in range(0, E, 8):
                for c in range(DC):
                    load(eng, "wgu", wgu[:, c, e:e + 8], a["E_gu"][:, c, e:e + 8])
            eng.wait_ge(s_zero, 1)
            load(eng, "xs0", xs.rearrange("(p r) f -> p r f", p=P), zeros.unsqueeze(1).to_broadcast([P, NBLK, D]))

        attention("A", LA, float(P) ** -0.5, maskA, False, prefetch_up)

        normX = Norm("nX")
        qc_done, qc_ready = sem("qc_done"), sem("qc_ready")
        with nc.Block() as block:
            @block.vector
            def _(eng):
                normX.dve(eng)

            @block.gpsimd
            def _(eng):
                normX.pool(eng)

            @block.scalar
            def _(eng):
                normX.act(eng)
                for k in range(2):
                    eng.wait_ge(qc_done, k + 1)
                    eng.activation(LX["qc"][0:QC, k * 512:(k + 1) * 512], ps[0:QC, 2 + k, :], ACT.Copy).then_inc(qc_ready, 1)

            @block.tensor
            def _(eng):
                normX.pe(eng)
                for k in range(2):
                    eng.wait_ge(normX.hT_ready, 2 * k + 2)
                    for c in range(DC):
                        t = eng.matmul(ps[0:QC, 2 + k, :], LX["wdq"][:, c, :], hT[:, c, k * 512:(k + 1) * 512],
                                       start=c == 0, stop=c == DC - 1)
                    t.then_inc(qc_done, 1)
                loaded(eng, "qX")
                eng.wait_ge(qc_ready, 2)

        wdn = view(A0, 8192, "p (e m) -> p e m", e=E)
        sel = view(51104, 2048, "p (e m) -> p e m", dt=bf16, e=E)
        bias_f = view(A0 + 10240, 512)
        bias_b = view(A0 + 10752, 256, dt=bf16)
        gate_w = view(A0 + 11008, 64, "p (c e) -> p c e", c=DC)
        gate_b = view(A0 + 11072, 32)

        def prefetch_down(eng):
            load(eng, "wdn", wdn, a["E_dn"])
            load(eng, "gate", gate_w, a["E_gate"])
            load(eng, "gate", gate_b[0:1, :], a["E_gate_b"])
            load(eng, "bias", bias_f[0:3 * E, :], a["E_bias"])

        attention("X", LX, float(VH + R) ** -0.5, maskX, True, prefetch_down)

        o = X0
        logits = view(o, 256, "p (b e) -> p b e", b=NB); o += 256
        top = view(o, 64, "p (b k) -> p b k", b=NB); o += 64
        topi = view(o, 64, "p (b k) -> p b k", dt=u32, b=NB); o += 64
        idxf = view(o, 32, "p (b k) -> p b k", b=NB); o += 32
        gw = view(o, 32, "p (b k) -> p b k", b=NB); o += 32
        gsum = view(o, NB); o += NB
        iotaE = view(o, E); o += E
        iotaJ = view(o, NBLK); o += NBLK
        pick = view(o, 1024, "p (n e) -> p n e", e=E); o += 1024
        prod = view(o, 1024, "p (n e) -> p n e", e=E); o += 1024
        memb = view(o, 256, "p (b e) -> p b e", b=NB); o += 256
        cum = view(o, 288, "p (b e) -> p b e", b=NB + 1); o += 288
        memb_b = view(o, 128, dt=bf16); o += 128
        cum_b = view(o, 144, dt=bf16); o += 144
        nblk = view(o, E); o += E
        incl = view(o, E); o += E
        base = view(o, E); o += E
        place = view(o, 256, "p (b e) -> p b e", b=NB); o += 256
        slot = view(o, 32); o += 32
        slot_i = view(o, 32, dt=i32); o += 32
        cmp = view(o, NBLK * E, "p (j e) -> p j e", e=E); o += NBLK * E
        owner = view(o, NBLK); o += NBLK
        owner_i = view(o, NBLK, dt=i32); o += NBLK
        biastmp = view(o, 1024, "p (k m) -> p k m", k=2); o += 1024
        assert o <= K0
        normM = Norm("nM")
        s_iota, s_sel = sem("iota_ready"), sem("sel_ready")
        lg_done, pos_done = sem("logits_done"), sem("positions_done")
        s_route, w_exp = sem("route_step"), sem("gate_exp")
        memb_ready, slot_ready, owner_ready, bias_ready = (sem("memb_ready"), sem("slot_ready"), sem("owner_ready"),
                                                           sem("bias_ready"))
        gw_ready, s_top = sem("gate_weights_ready"), sem("top_step")
        neg_top = sem("neg_top")
        scattered = sem("scattered")

        def split3(eng, ch, dst, src, tmp):
            n = 3 * E
            ch.link(eng.tensor_copy(dst[0:n], src[0:n]))
            ch.link(eng.tensor_tensor(src[0:n], src[0:n], dst[0:n], ALU.subtract))
            ch.mark(eng.tensor_copy(dst[E:2 * E], src[E:2 * E]))
            ch.link(eng.tensor_copy(tmp[0:n], src[0:n]))
            ch.link(eng.tensor_tensor(src[2 * E:n], src[2 * E:n], tmp[2 * E:n], ALU.subtract))
            ch.link(eng.tensor_copy(dst[2 * E:n], src[2 * E:n]))

        with nc.Block() as block:
            @block.gpsimd
            def _(eng):
                eng.iota(iotaE, pattern=[[1, E]], base=0, channel_multiplier=0,
                         allow_small_or_imprecise_dtypes=True).then_inc(s_iota, 1)
                eng.iota(iotaJ, pattern=[[1, NBLK]], base=0, channel_multiplier=0,
                         allow_small_or_imprecise_dtypes=True).then_inc(s_iota, 1)
                normM.pool(eng)
                eng.memset(sel[0:3 * E], 0.0).then_inc(s_sel, 1)
                for m in range(3):
                    eng.wait_ge(s_sel, m + 1)
                    eng.affine_select(out=sel[0:3 * E], in_=sel[0:3 * E], compare_op=ALU.not_equal, fill=1.0,
                                      base=-E * m, pattern=[[-1, E], [0, P]], channel_multiplier=1).then_inc(s_sel, 1)
                loaded(eng, "xs0")
                eng.wait_ge(slot_ready, 1)
                for n in range(NB * TOPK):
                    eng.indirect_dma_start(xs, bass.IndirectOffsetOnAxis(ap=slot_i[:, n:n + 1].bitcast(u32), axis=0),
                                           h[:, n // TOPK, :], None).then_inc(scattered, 16)
                eng.wait_ge(scattered, 16 * NB * TOPK)

            @block.vector
            def _(eng):
                ch = Chain(eng, s_route)
                normM.dve(eng)
                loaded(eng, "bias")
                split3(eng, ch, bias_b, bias_f, biastmp[:, 0, :].bitcast(bf16)[:, 0:512])
                for b in range(NB):
                    if b % 4 == 0:
                        eng.wait_ge(lg_done, b // 4 + 1)
                        ch.link(eng.tensor_copy(logits[:, b:b + 4], ps[:, 2 + b // 4, 0:4 * E].rearrange("p (b e) -> p b e", b=4)))
                    eng.max(top[:, b], logits[:, b]).then_inc(s_top, 1)
                    eng.wait_ge(s_top, 2 * b + 1)
                    eng.max_index(topi[:, b], top[:, b], logits[:, b]).then_inc(s_top, 1)
                eng.wait_ge(s_top, 2 * NB)
                ch.mark(eng.tensor_copy(idxf, topi[:, :, 0:TOPK]))
                eng.tensor_tensor(gw, top[:, :, 0:TOPK], top[:, :, 0:1].to_broadcast([P, NB, TOPK]),
                                  ALU.subtract).then_inc(neg_top, 1)
                ch.wait()
                eng.wait_ge(s_iota, 2)
                pk = "p (b k) e -> p b k e"
                ch.link(eng.tensor_tensor(pick, idxf.rearrange("p b k -> p (b k)").unsqueeze(2).to_broadcast([P, 32, E]),
                                          iotaE.unsqueeze(1).to_broadcast([P, 32, E]), ALU.is_equal))
                ch.mark(eng.memset(cum[:, 0], 0.0))
                ch.link(eng.tensor_reduce(memb, pick.rearrange("p (b k) e -> p b e k", b=NB), AX.X, ALU.add))
                for b in range(NB):
                    ch.link(eng.tensor_tensor(cum[:, b + 1], cum[:, b], memb[:, b], ALU.add))
                ch.mark(eng.tensor_copy(memb_b, memb.rearrange("p b e -> p (b e)")))
                ch.link(eng.tensor_copy(cum_b, cum.rearrange("p b e -> p (b e)")))
                eng.tensor_copy(biastmp[:, 1, 0:1], iotaE[:, 0:1]).then_inc(memb_ready, 1)
                eng.wait_ge(pos_done, 1)
                ch.link(eng.tensor_scalar(nblk, ps[:, 4, 0:E], 1.0 / P, (P - 1.0) / P - 0.5 + 1.0 / 256, ALU.mult, ALU.add))
                ch.link(eng.tensor_scalar(nblk, nblk, MAGIC, None, ALU.add))
                ch.link(eng.tensor_scalar(nblk, nblk, -MAGIC, None, ALU.add))
                ch.link(eng.tensor_tensor_scan(incl, ones[:, 0:E], nblk, 0.0, ALU.mult, ALU.add))
                ch.link(eng.tensor_tensor(base, incl, nblk, ALU.subtract))
                ch.link(eng.scalar_tensor_tensor(place, base.unsqueeze(1).to_broadcast([P, NB, E]), float(P),
                                                 ps[:, 5, 0:256].rearrange("p (b e) -> p b e", b=NB), ALU.mult, ALU.add))
                ch.link(eng.tensor_tensor(prod.rearrange(pk, b=NB), pick.rearrange(pk, b=NB),
                                          place.unsqueeze(2).to_broadcast([P, NB, TOPK, E]), ALU.mult))
                ch.link(eng.tensor_reduce(slot, prod, AX.X, ALU.add))
                eng.tensor_copy(slot_i, slot).then_inc(slot_ready, 1)
                ch.link(eng.tensor_tensor(cmp, incl.unsqueeze(1).to_broadcast([P, NBLK, E]),
                                          iotaJ.unsqueeze(2).to_broadcast([P, NBLK, E]), ALU.is_le))
                ch.link(eng.tensor_reduce(owner, cmp, AX.X, ALU.add))
                ch.link(eng.tensor_scalar(owner, owner, E - 1.0, None, ALU.min))
                eng.tensor_copy(owner_i, owner).then_inc(owner_ready, 1)
                eng.wait_ge(w_exp, 1)
                ch.link(eng.tensor_reduce(gsum, gw, AX.X, ALU.add))
                ch.link(eng.reciprocal(gsum, gsum))
                eng.tensor_tensor(gw, gw, gsum.unsqueeze(2).to_broadcast([P, NB, TOPK]), ALU.mult).then_inc(gw_ready, 1)

            @block.scalar
            def _(eng):
                normM.act(eng)
                eng.wait_ge(neg_top, 1)
                eng.activation(gw, gw, ACT.Exp).then_inc(w_exp, 1)

            @block.tensor
            def _(eng):
                normM.pe(eng)
                loaded(eng, "gate")
                for b in range(NB):
                    if b % 2 == 0:
                        eng.wait_ge(normM.hT_ready, b // 2 + 1)
                    dst = ps[:, 2 + b // 4, (b % 4) * E:(b % 4 + 1) * E]
                    for c in range(DC):
                        eng.matmul(dst, hT[:, c, b * P:(b + 1) * P], gate_w[:, c, :], start=c == 0, stop=False)
                    t = eng.matmul(dst, ones[0:1, :], gate_b[0:1, :], start=False, stop=True)
                    if b % 4 == 3:
                        t.then_inc(lg_done, 1)
                eng.wait_ge(memb_ready, 1)
                eng.matmul(ps[:, 4, 0:E], ones_b, cum_b[:, NB * E:(NB + 1) * E], start=True, stop=True)
                eng.matmul(ps[:, 5, 0:256], ones_b, cum_b[:, 0:256], start=True, stop=False)
                eng.matmul(ps[:, 5, 0:256], tri_b, memb_b, start=False, stop=True).then_inc(pos_done, 1)

        o = K0
        xin = view(o, 1024, "p (u f) -> p u f", u=4); o += 1024
        xinT = view(o, 512, "p (d c t) -> p d c t", d=2, c=DC); o += 512
        gate = view(o, 256, "p (d m) -> p d m", d=2); o += 256
        sig = view(o, 256, "p (d m) -> p d m", d=2); o += 256
        up = view(o, 256, "p (d m) -> p d m", d=2); o += 256
        act_ = view(o, 256, "p (d m) -> p d m", d=2); o += 256
        actT = view(o, 256, "p (d m) -> p d m", d=2); o += 256
        yout = view(o, 1024, "p (u f) -> p u f", u=4); o += 1024
        x_in = [sem(f"block_in{u}") for u in range(4)]
        y_out = [sem(f"block_out{u}") for u in range(4)]
        xT_done, xT_ready, gu_done, gate_ready = sem("xT_done"), sem("xT_ready"), sem("gu_done"), sem("gate_ready")
        up_ready, sig_ready, gs_ready, act_ready = sem("up_ready"), sem("sig_ready"), sem("gs_ready"), sem("act_ready")
        aT_done, aT_ready, dn_done, y_ready = sem("aT_done"), sem("aT_ready"), sem("dn_done"), sem("y_ready")

        def early(b, n, s):
            return isinstance(b, int) and s < n

        with nc.Block() as block:
            @block.sync
            def _(eng):
                def LD(i, u):
                    s = 4 * i + u
                    if not early(i, 4, s):
                        eng.wait_ge(xT_done, s - 3)
                    eng.dma_start(xin[:, u], xs[bass.ds(s * P, P), :]).then_inc(x_in[u], 16)

                def SR(i, u):
                    s = 4 * i + u
                    eng.wait_ge(y_ready, s + 1)
                    eng.dma_start(ys[bass.ds(s * P, P), :], yout[:, u]).then_inc(y_out[u], 16)

                pipeline(eng, NBLK // 4, [(4, LD), (-3, SR)], [(u, LD) for u in range(4)],
                         [(u, SR) for u in range(1, 4)])
                for u in range(4):
                    eng.wait_ge(y_out[u], 16 * (NBLK // 4))

            @block.tensor
            def _(eng):
                loaded(eng, "wgu", "wdn")

                def TX(i, u):
                    s, d = 4 * i + u, u % 2
                    eng.wait_ge(x_in[u], 16 * i + 16)
                    if not early(i, 2, s):
                        eng.wait_ge(xT_ready, s - 1)
                    for c in range(DC):
                        t = eng.transpose(ps[:, d, c * P:(c + 1) * P], xin[:, u, c * P:(c + 1) * P], ident)
                    t.then_inc(xT_done, 1)

                e_up, e_mid, e_down = (eng.alloc_register(n) for n in ("e_up", "e_mid", "e_down"))

                def OW(i, u):
                    eng.reg_load(e_up, owner_i[0:1, bass.ds(4 * i + u, 1)])

                def SH(i, u):
                    eng.reg_mov(e_down, e_mid)
                    eng.reg_mov(e_mid, e_up)

                eng.reg_mov(e_mid, 0)

                def GU(i, u):
                    s, d = 4 * i + u, u % 2
                    e = eng.snap(e_up, min_val=0, max_val=E - 1)
                    eng.wait_ge(xT_ready, s + 1)
                    if not early(i, 2, s):
                        eng.wait_ge(gate_ready, s - 1)
                        eng.wait_ge(up_ready, s - 1)
                    for c in range(DC):
                        eng.matmul(ps[:, 2 + d, 0:2 * I], xinT[:, d, c, :],
                                   wgu[:, c, bass.ds(e, 1), :].rearrange("p a m -> p (a m)"), start=c == 0, stop=False)
                    eng.matmul(ps[:, 2 + d, 0:2 * I], sel[0:3 * E, bass.ds(e, 1), :].rearrange("p a m -> p (a m)"),
                               bias_b[0:3 * E, 0:2 * I], start=False, stop=True).then_inc(gu_done, 1)

                def TA(i, u):
                    s, d = 4 * i + u, u % 2
                    eng.wait_ge(act_ready, s + 1)
                    if not early(i, 2, s):
                        eng.wait_ge(aT_ready, s - 1)
                    eng.transpose(ps[:, 4 + d, 0:P], act_[:, d], ident).then_inc(aT_done, 1)

                def DN(i, u):
                    s, d = 4 * i + u, u % 2
                    e = eng.snap(e_down, min_val=0, max_val=E - 1)
                    eng.wait_ge(aT_ready, s + 1)
                    if not early(i, 2, s):
                        eng.wait_ge(y_ready, s - 1)
                    eng.matmul(ps[:, 6 + d, 0:D], actT[:, d], wdn[:, bass.ds(e, 1), :].rearrange("p a m -> p (a m)"),
                               start=True, stop=False)
                    eng.matmul(ps[:, 6 + d, 0:D], sel[0:3 * E, bass.ds(e, 1), :].rearrange("p a m -> p (a m)"),
                               bias_b[0:3 * E, 2 * I:2 * I + D], start=False, stop=True).then_inc(dn_done, 1)

                pipeline(eng, NBLK // 4, [(2, TX), (-1, DN), (1, GU), (0, SH), (2, OW), (0, TA)],
                         [(0, OW), (0, TX), (1, TX), (0, GU), (0, SH), (1, OW)], [(3, DN)])

            @block.scalar
            def _(eng):
                def XT(i, u):
                    s, d = 4 * i + u, u % 2
                    eng.wait_ge(xT_done, s + 1)
                    if not early(i, 2, s):
                        eng.wait_ge(gu_done, s - 1)
                    eng.activation(xinT[:, d], ps[:, d, 0:D].rearrange("p (c t) -> p c t", c=DC),
                                   ACT.Copy).then_inc(xT_ready, 1)

                def SG(i, u):
                    s, d = 4 * i + u, u % 2
                    eng.wait_ge(gate_ready, s + 1)
                    if not early(i, 2, s):
                        eng.wait_ge(gs_ready, s - 1)
                    eng.activation(sig[:, d], gate[:, d], ACT.Sigmoid, scale=1.702).then_inc(sig_ready, 1)

                def AT(i, u):
                    s, d = 4 * i + u, u % 2
                    eng.wait_ge(aT_done, s + 1)
                    if not early(i, 2, s):
                        eng.wait_ge(dn_done, s - 1)
                    eng.activation(actT[:, d], ps[:, 4 + d, 0:P], ACT.Copy).then_inc(aT_ready, 1)

                pipeline(eng, NBLK // 4, [(2, XT), (1, SG), (0, AT)], [(0, XT), (1, XT), (0, SG)], [])

            @block.vector
            def _(eng):
                def GL(i, u):
                    s, d = 4 * i + u, u % 2
                    eng.wait_ge(gu_done, s + 1)
                    eng.tensor_scalar(gate[:, d], ps[:, 2 + d, 0:I], 7.0, None, ALU.min).then_inc(gate_ready, 1)
                    eng.tensor_scalar(up[:, d], ps[:, 2 + d, I:2 * I], 1.0, 8.0, ALU.add, ALU.min).then_inc(up_ready, 1)
                    eng.wait_ge(sig_ready, s + 1)
                    eng.tensor_tensor(gate[:, d], gate[:, d], sig[:, d], ALU.mult).then_inc(gs_ready, 1)
                    eng.wait_ge(gs_ready, s + 1)
                    if not early(i, 2, s):
                        eng.wait_ge(aT_done, s - 1)
                    eng.scalar_tensor_tensor(act_[:, d], up[:, d], -6.0, gate[:, d], ALU.max,
                                             ALU.mult).then_inc(act_ready, 1)

                def YO(i, u):
                    s = 4 * i + u
                    eng.wait_ge(dn_done, s + 1)
                    if not early(i, 4, s):
                        eng.wait_ge(y_out[u], 16 * i)
                    eng.tensor_copy(yout[:, u], ps[:, 6 + u % 2, 0:D]).then_inc(y_ready, 1)

                pipeline(eng, NBLK // 4, [(-1, YO), (1, GL)], [(0, GL)], [(3, YO)])

        yg = view(W0, 8192, "p (n f) -> p n f", f=D)
        gathered = [sem(f"gathered{b}") for b in range(NB)]
        s_comb = sem("combine_step")
        with nc.Block() as block:
            @block.gpsimd
            def _(eng):
                for n in range(NB * TOPK):
                    eng.indirect_dma_start(yg[:, n, :], None, ys,
                                           bass.IndirectOffsetOnAxis(ap=slot_i[:, n:n + 1].bitcast(u32), axis=0)
                                           ).then_inc(gathered[n // TOPK], 16)

            @block.vector
            def _(eng):
                ch = Chain(eng, s_comb)
                for b in range(NB):
                    eng.wait_ge(gathered[b], 16 * TOPK)
                    for k in range(TOPK):
                        ch.link(eng.scalar_tensor_tensor(x[:, b], yg[:, b * TOPK + k], gw[:, b, k:k + 1], x[:, b],
                                                         ALU.mult, ALU.add))

        first_layer.close()

        o = W0
        xc = view(o, 4096, "p (c t) -> p c t", c=CT); o += 4096
        zs = view(o, 4096, "p (c t) -> p c t", c=CT); o += 4096
        dts = view(o, 4096, "p (c t) -> p c t", c=CT); o += 4096
        dtu = view(o, 4096, "p (c t) -> p c t", c=CT); o += 4096
        yg = view(o, 4096, "p (c t) -> p c t", c=CT); o += 4096
        room = [o + 1024 * k for k in range(4)] + [35840 + 1024 * k for k in range(7)] + [45568 + 1024 * k for k in range(5)]
        B_ = [view(r, 1024) for r in room]
        w_in = view(33792, 2048, "p (k m) -> p k m", k=DC)
        bc3 = view(43008, 512, dt=bf16)
        o = 43520
        w_bc = view(o, 384, "p (k m) -> p k m", k=CT); o += 384
        w_dt = view(o, 512, "p (k m) -> p k m", k=CT); o += 512
        w_out = view(o, 1024, "p (k m) -> p k m", k=CT); o += 1024
        vecs = view(o, 128)
        cw, cb, dtw, dtb, Dp = vecs[:, 0:16], vecs[:, 16:20], vecs[:, 20:24], vecs[:, 24:28], vecs[:, 28:32]
        nw, negA = vecs[:, 32:34], vecs[:, 34:98]
        padded = [view(room[4], 1048, "p (b t) -> p b t", b=NB), view(room[4] + 1048, 1048, "p (b t) -> p b t", b=NB)]
        conv = [B_[7], B_[8]]
        bcf, bct = B_[9], B_[10].bitcast(bf16)[:, 0:1024]
        zz, ez, eabs = [B_[0], B_[1]], [B_[11], B_[12]], [B_[2], B_[3]]
        normS = Norm("nS", True)
        in_done, xi_ready, z_ready = sem("in_done"), sem("xi_ready"), sem("z_ready")
        conv_ready, xc_ready, pad_ready = sem("conv_ready"), sem("xc_ready"), sem("pad_ready")
        bc_done, dt_done, bc_ready, s_split = sem("bc_done"), sem("dt_done"), sem("bc_ready"), sem("split_step")
        zz_ready, sp_ready, dt_ready, dtu_ready = sem("zz_ready"), sem("sp_ready"), sem("dt_ready"), sem("dtu_ready")
        s_actm, s_negA = sem("act_step_m"), sem("negA_step")
        t8 = "p (b t) -> p b t"

        with nc.Block() as block:
            @block.sync
            def _(eng):
                load(eng, "w_in", w_in, a["M_in"])
                load(eng, "w_bc", w_bc[:, :, :], a["M_bc"])
                load(eng, "w_bc", w_dt, a["M_dt"])
                load(eng, "vecs", vecs[:, 0:98], a["M_vec"])
                load(eng, "w_out", w_out, a["M_out"])

            @block.gpsimd
            def _(eng):
                for k in range(2):
                    eng.memset(padded[k][:, :, 0:PAD], 0.0).then_inc(pad_ready, 1)
                normS.pool(eng)
                for c in range(CT):
                    eng.wait_ge(dt_ready, c + 1)
                    eng.tensor_tensor(dtu[:, c], dts[:, c], xc[:, c], ALU.mult).then_inc(dtu_ready, 1)

            @block.tensor
            def _(eng):
                normS.pe(eng)
                loaded(eng, "w_in")
                eng.wait_ge(normS.hT_ready, 4)
                for m in range(2 * CT):
                    r = 2 * (m % 4)
                    if m >= 4:
                        eng.wait_ge(xi_ready, m - 3)
                    for half in range(2):
                        for k in range(DC):
                            t = eng.matmul(ps[:, r + half, :], w_in[:, k, m * P:(m + 1) * P],
                                           hT[:, k, half * 512:(half + 1) * 512], start=k == 0, stop=k == DC - 1)
                    t.then_inc(in_done, 1)
                loaded(eng, "w_bc")
                eng.wait_ge(xc_ready, CT)
                eng.wait_ge(z_ready, 2)
                for half in range(2):
                    for c in range(CT):
                        t = eng.matmul(ps[0:3 * E, half, :], w_bc[:, c, :], xc[:, c, half * 512:(half + 1) * 512],
                                       start=c == 0, stop=c == CT - 1)
                t.then_inc(bc_done, 1)
                for half in range(2):
                    for c in range(CT):
                        t = eng.matmul(ps[:, 2 + half, :], w_dt[:, c, :], xc[:, c, half * 512:(half + 1) * 512],
                                       start=c == 0, stop=c == CT - 1)
                t.then_inc(dt_done, 1)

            @block.scalar
            def _(eng):
                loaded(eng, "vecs")
                normS.act(eng, nw)
                for c in range(CT):
                    eng.wait_ge(in_done, c + 1)
                    if c < 2:
                        eng.wait_ge(pad_ready, c + 1)
                    else:
                        eng.wait_ge(conv_ready, c - 1)
                    r = 2 * c
                    eng.activation(padded[c % 2][:, :, PAD:], ps[:, r:r + 2, :].rearrange("p k (b t) -> p (k b) t", b=4),
                                   ACT.Copy).then_inc(xi_ready, 1)
                for c in range(CT):
                    eng.wait_ge(in_done, CT + c + 1)
                    eng.activation(zs[:, c], ps[:, 2 * c:2 * c + 2, :].rearrange("p k m -> p (k m)"),
                                   ACT.Silu).then_inc(z_ready, 1)
                    eng.wait_ge(conv_ready, c + 1)
                    eng.activation(xc[:, c], conv[c % 2], ACT.Silu).then_inc(xc_ready, 1)
                eng.activation(negA, negA, ACT.Exp).then_inc(s_negA, 1)
                for c in range(CT):
                    d = c % 2
                    eng.wait_ge(zz_ready, c + 1)
                    eng.activation(ez[d], zz[d], ACT.Abs).then_inc(s_actm, 1)
                    eng.wait_ge(s_actm, 2 * c + 1)
                    if c >= 2:
                        eng.wait_ge(dt_ready, c - 1)
                    eng.activation(eabs[d], ez[d], ACT.Exp, scale=-1.0).then_inc(s_actm, 1)
                    eng.wait_ge(s_actm, 2 * c + 2)
                    eng.activation(ez[d], eabs[d], ACT.Ln, bias=1.0).then_inc(sp_ready, 1)

            @block.vector
            def _(eng):
                ch = Chain(eng, s_split)
                normS.dve(eng)
                for c in range(CT):
                    d = c % 2
                    acc = conv[d].rearrange(t8, b=NB)
                    eng.wait_ge(xi_ready, c + 1)
                    if c >= 2:
                        eng.wait_ge(xc_ready, c - 1)
                    ch.link(eng.tensor_scalar(acc, padded[d][:, :, 0:P], cw[:, 4 * c:4 * c + 1], cb[:, c:c + 1],
                                              ALU.mult, ALU.add))
                    for k in range(1, KCONV):
                        t = eng.scalar_tensor_tensor(acc, padded[d][:, :, k:k + P], cw[:, 4 * c + k:4 * c + k + 1],
                                                     acc, ALU.mult, ALU.add)
                        if k < KCONV - 1:
                            ch.link(t)
                        else:
                            t.then_inc(conv_ready, 1)
                eng.wait_ge(bc_done, 1)
                ch.link(eng.tensor_copy(bcf[0:3 * E], ps[0:3 * E, 0:2, :].rearrange("p k m -> p (k m)")))
                eng.wait_ge(dt_done, 1)
                for c in range(2):
                    eng.tensor_scalar(zz[c], ps[:, 2:4, :].rearrange("p k m -> p (k m)"), dtw[:, c:c + 1],
                                      dtb[:, c:c + 1], ALU.mult, ALU.add).then_inc(zz_ready, 1)
                split3(eng, ch, bc3, bcf, bct)
                eng.wait_ge(s_negA, 1)
                ch.mark(eng.tensor_scalar(negA, negA, -1.0, None, ALU.mult))
                for c in range(CT):
                    d = c % 2
                    eng.wait_ge(sp_ready, c + 1)
                    eng.wait_ge(zz_ready, c + 1)
                    eng.scalar_tensor_tensor(dts[:, c], zz[d], 0.0, ez[d], ALU.max, ALU.add).then_inc(dt_ready, 1)
                    if c + 2 < CT:
                        eng.wait_ge(dt_ready, c + 1)
                        eng.tensor_scalar(zz[d], ps[:, 2:4, :].rearrange("p k m -> p (k m)"), dtw[:, c + 2:c + 3],
                                          dtb[:, c + 2:c + 3], ALU.mult, ALU.add).then_inc(zz_ready, 1)

        dA = [B_[k] for k in range(4)]
        dBu = [B_[4], B_[5]]
        hst = [B_[6], B_[7], B_[8], B_[9]]
        hC = [B_[10], B_[11], B_[12], B_[13]]
        Csb = [B_[14], B_[15]]

        def scan(cp):
            tag = f"scan{cp}"
            B_done, C_done, C_ready = sem(tag + "_B"), sem(tag + "_C"), sem(tag + "_C_sbuf")
            dA_ready, dBu_ready, h_ready, hC_ready = sem(tag + "_dA"), sem(tag + "_dBu"), sem(tag + "_h"), sem(tag + "_hC")
            y_done, dA_zero, y_ready = sem(tag + "_y"), sem(tag + "_dA_zero"), sem(tag + "_gated")
            rounds = ST // 2
            psB, psC = ps[:, 4:6, :].rearrange("p k m -> p (k m)"), ps[:, 6:8, :].rearrange("p k m -> p (k m)")

            with nc.Block() as block:
                @block.tensor
                def _(eng):
                    def BC(i, u):
                        if u % 2:
                            return
                        s, n = 4 * i + u, 2 * i + u // 2
                        if not early(i, 1, s):
                            eng.wait_ge(dBu_ready, s)
                        for half in range(2):
                            t = eng.matmul(ps[:, 4 + half, :], sel[0:3 * E, bass.ds(n, 1), :].rearrange("p a m -> p (a m)"),
                                           bc3[0:3 * E, half * 512:(half + 1) * 512], start=True, stop=True)
                        t.then_inc(B_done, 1)
                        if not early(i, 1, s):
                            eng.wait_ge(C_ready, n)
                        for half in range(2):
                            t = eng.matmul(ps[:, 6 + half, :],
                                           sel[0:3 * E, bass.ds(n + ST, 1), :].rearrange("p a m -> p (a m)"),
                                           bc3[0:3 * E, half * 512:(half + 1) * 512], start=True, stop=True)
                        t.then_inc(C_done, 1)

                    def Y(i, u):
                        s = 4 * i + u
                        eng.wait_ge(hC_ready, s + 1)
                        for half in range(2):
                            t = eng.matmul(ps[:, 2 * (u % 2) + half, :], ident, hC[u][:, half * 512:(half + 1) * 512],
                                           start=early(i, 2, s), stop=isinstance(i, int) and s >= 2 * ST - 2)
                        t.then_inc(y_done, 1)

                    pipeline(eng, rounds, [(2, BC), (-1, Y)], [(0, BC)], [(3, Y)])

                @block.scalar
                def _(eng):
                    def CS(i, u):
                        if u % 2:
                            return
                        n = 2 * i + u // 2
                        eng.wait_ge(C_done, n + 1)
                        if not early(i, 2, n):
                            eng.wait_ge(hC_ready, 2 * n - 2)
                        eng.activation(Csb[u // 2], psC, ACT.Copy).then_inc(C_ready, 1)

                    def DA(i, u):
                        s, n, c = 4 * i + u, 2 * i + u // 2, 2 * cp + u % 2
                        if early(i, 4, s):
                            eng.wait_ge(dA_zero, u + 1)
                        else:
                            eng.wait_ge(h_ready, s - 3)
                        eng.activation(dA[u].rearrange(t8, b=NB)[:, :, 1:P], dts[:, c].rearrange(t8, b=NB)[:, :, 1:P],
                                       ACT.Exp, scale=negA[:, bass.ds(ST * c + n, 1)]).then_inc(dA_ready, 1)

                    pipeline(eng, rounds, [(2, DA), (1, CS)], [(0, DA), (1, DA), (0, CS)], [])

                @block.vector
                def _(eng):
                    def DB(i, u):
                        s, n, c = 4 * i + u, 2 * i + u // 2, 2 * cp + u % 2
                        eng.wait_ge(B_done, n + 1)
                        if not early(i, 2, s):
                            eng.wait_ge(h_ready, s - 1)
                        eng.tensor_tensor(dBu[u % 2], dtu[:, c], psB, ALU.mult).then_inc(dBu_ready, 1)

                    def SC(i, u):
                        s = 4 * i + u
                        eng.wait_ge(dA_ready, s + 1)
                        eng.wait_ge(dBu_ready, s + 1)
                        if not early(i, 4, s):
                            eng.wait_ge(hC_ready, s - 3)
                        eng.tensor_tensor_scan(hst[u], dA[u], dBu[u % 2], 0.0, ALU.mult, ALU.add).then_inc(h_ready, 1)

                    pipeline(eng, rounds, [(1, DB), (0, SC)], [(0, DB)], [])
                    for k in range(2):
                        c = 2 * cp + k
                        eng.wait_ge(y_done, 2 * ST - 1 + k)
                        eng.scalar_tensor_tensor(yg[:, c], xc[:, c], Dp[:, c:c + 1],
                                                 ps[:, 2 * k:2 * k + 2, :].rearrange("p k m -> p (k m)"),
                                                 ALU.mult, ALU.add).then_inc(y_ready, 1)
                    for k in range(2):
                        c = 2 * cp + k
                        eng.wait_ge(y_ready, k + 1)
                        eng.tensor_tensor(yg[:, c], yg[:, c], zs[:, c], ALU.mult).then_inc(y_ready, 1)

                @block.gpsimd
                def _(eng):
                    for u in range(4):
                        eng.memset(dA[u].rearrange(t8, b=NB)[:, :, 0:1], 0.0).then_inc(dA_zero, 1)

                    def HC(i, u):
                        s, n = 4 * i + u, 2 * i + u // 2
                        eng.wait_ge(h_ready, s + 1)
                        eng.wait_ge(C_ready, n + 1)
                        if not early(i, 4, s):
                            eng.wait_ge(y_done, s - 3)
                        eng.tensor_tensor(hC[u], hst[u], Csb[u // 2], ALU.mult).then_inc(hC_ready, 1)

                    pipeline(eng, rounds, [(0, HC)], [], [])

        scan(0)
        scan(1)

        op_done, op_ready = sem("out_proj_done"), sem("out_proj_added")
        with nc.Block() as block:
            @block.tensor
            def _(eng):
                loaded(eng, "w_out")
                for b in range(NB):
                    if b >= 4:
                        eng.wait_ge(op_ready, b - 3)
                    for c in range(CT):
                        t = eng.matmul(ps[:, b % 4, 0:D], yg[:, c, b * P:(b + 1) * P], w_out[:, c, :],
                                       start=c == 0, stop=c == CT - 1)
                    t.then_inc(op_done, 1)

            @block.vector
            def _(eng):
                for b in range(NB):
                    eng.wait_ge(op_done, b + 1)
                    eng.tensor_tensor(x[:, b], x[:, b], ps[:, b % 4, 0:D], ALU.add).then_inc(op_ready, 1)

        TP = P + 1
        o = W0
        vT = view(o, 2048, "p (c t) -> p c t", c=DC); o += 2048
        wkv_u = view(o, 2); o += 2
        wkv_w = view(o, 2); o += 2
        names = ("kp", "wp", "op", "no", "a1", "e1", "a2", "e2", "ev", "pp", "qp", "num", "den", "tmp")
        W = {n: [view(o + NB * TP * (2 * k + c), NB * TP, "p (b t) -> p b t", b=NB) for c in range(DC)]
             for k, n in enumerate(names)}
        o += NB * TP * 2 * len(names)
        assert o <= 51104
        flat = lambda v: v.rearrange("p b t -> p (b t)")
        normW = Norm("nW")
        s_w, w_act, w_pool = sem("wkv_step"), sem("wkv_exp"), sem("wkv_pool")
        kp_ready, pre_ready, sc_ready, yw_ready = sem("kp_ready"), sem("wkv_pre"), sem("wkv_scan"), sem("wkv_y")
        yT_done, xw_ready = sem("wkv_T_done"), sem("wkv_added")
        BIG = -1.0e38

        with nc.Block() as block:
            @block.sync
            def _(eng):
                load(eng, "vT", vT, a["ctxT"])
                load(eng, "uw", wkv_u, a["W_u"])
                load(eng, "uw", wkv_w, a["W_w"])

            @block.gpsimd
            def _(eng):
                for c in range(DC):
                    eng.memset(W["kp"][c][:, :, 0:1], BIG).then_inc(w_pool, 1)
                    for n in ("a2", "e2", "ev"):
                        eng.memset(W[n][c][:, :, 0:1], 0.0).then_inc(w_pool, 1)
                normW.pool(eng)
                loaded(eng, "vT")
                for c in range(DC):
                    v = vT[:, c].rearrange(t8, b=NB)
                    eng.wait_ge(w_act, 4 * c + 4)
                    eng.tensor_tensor(W["ev"][c][:, :, 1:], W["e2"][c][:, :, 1:], v, ALU.mult).then_inc(w_pool, 1)
                    eng.tensor_tensor(W["tmp"][c][:, :, 1:], W["e1"][c][:, :, 1:], v, ALU.mult).then_inc(w_pool, 1)

            @block.scalar
            def _(eng):
                normW.act(eng)
                eng.wait_ge(normW.hT_ready, 4)
                for c in range(DC):
                    eng.activation(W["kp"][c][:, :, 1:], hT[:, c].rearrange(t8, b=NB), ACT.Copy).then_inc(kp_ready, 1)
                for c in range(DC):
                    for k, n in enumerate(("e2", "a2", "e1", "a1")):
                        eng.wait_ge(pre_ready, 4 * c + k + 1)
                        if k == 0:
                            eng.wait_ge(w_pool, 4 * DC)
                        eng.activation(W[n][c][:, :, 1:], W[n][c][:, :, 1:], ACT.Exp).then_inc(w_act, 1)

            @block.vector
            def _(eng):
                ch = Chain(eng, s_w)
                normW.dve(eng)
                loaded(eng, "uw")
                for c in range(DC):
                    w = {n: W[n][c] for n in names}
                    u_, w_ = wkv_u[:, c:c + 1], wkv_w[:, c:c + 1]
                    k, o_prev, o_now = w["kp"][:, :, 1:], w["op"][:, :, 0:P], w["op"][:, :, 1:]
                    eng.wait_ge(kp_ready, c + 1)
                    eng.wait_ge(w_pool, 4 * DC)
                    ch.link(eng.tensor_scalar(w["wp"][:, :, 1:], k, 0.0, w_, ALU.mult, ALU.add))
                    ch.link(eng.memset(w["wp"][:, :, 0:1], BIG))
                    ch.link(eng.tensor_tensor_scan(flat(w["op"]), flat(w["wp"]), flat(w["kp"]), BIG, ALU.add, ALU.max))
                    eng.tensor_tensor(w["e2"][:, :, 1:], k, o_now, ALU.subtract).then_inc(pre_ready, 1)
                    eng.scalar_tensor_tensor(w["a2"][:, :, 1:], o_prev, w_, o_now, ALU.add, ALU.subtract).then_inc(pre_ready, 1)
                    ch.link(eng.scalar_tensor_tensor(w["no"][:, :, 1:], k, u_, o_prev, ALU.add, ALU.max))
                    eng.scalar_tensor_tensor(w["e1"][:, :, 1:], k, u_, w["no"][:, :, 1:], ALU.add, ALU.subtract).then_inc(pre_ready, 1)
                    eng.tensor_tensor(w["a1"][:, :, 1:], o_prev, w["no"][:, :, 1:], ALU.subtract).then_inc(pre_ready, 1)
                for c in range(DC):
                    w = {n: W[n][c] for n in names}
                    eng.wait_ge(w_act, 4 * c + 2)
                    ch.link(eng.tensor_tensor_scan(flat(w["qp"]), flat(w["a2"]), flat(w["e2"]), 0.0, ALU.mult, ALU.add))
                    eng.wait_ge(w_pool, 4 * DC + 2 * c + 1)
                    ch.link(eng.tensor_tensor_scan(flat(w["pp"]), flat(w["a2"]), flat(w["ev"]), 0.0, ALU.mult, ALU.add))
                    eng.wait_ge(w_act, 4 * c + 4)
                    num, den = w["num"][:, :, 0:P], w["den"][:, :, 0:P]
                    ch.mark(eng.tensor_tensor(num, w["a1"][:, :, 1:], w["pp"][:, :, 0:P], ALU.mult))
                    ch.link(eng.tensor_tensor(den, w["a1"][:, :, 1:], w["qp"][:, :, 0:P], ALU.mult))
                    eng.wait_ge(w_pool, 4 * DC + 2 * c + 2)
                    ch.mark(eng.tensor_tensor(num, num, w["tmp"][:, :, 1:], ALU.add))
                    ch.link(eng.tensor_tensor(den, den, w["e1"][:, :, 1:], ALU.add))
                    ch.link(eng.reciprocal(den, den))
                    eng.tensor_tensor(num, num, den, ALU.mult).then_inc(yw_ready, 1)
                for b in range(NB):
                    eng.wait_ge(yT_done, b + 1)
                    eng.tensor_tensor(x[:, b], x[:, b], ps[:, 2 + b % 4, 0:D], ALU.add).then_inc(xw_ready, 1)

            @block.tensor
            def _(eng):
                normW.pe(eng)
                eng.wait_ge(yw_ready, DC)
                for b in range(NB):
                    if b >= 4:
                        eng.wait_ge(xw_ready, b - 3)
                    for c in range(DC):
                        t = eng.transpose(ps[:, 2 + b % 4, c * P:(c + 1) * P], W["num"][c][:, b, 0:P], ident)
                    t.then_inc(yT_done, 1)

        o = W0
        w1 = view(o, 2048, "p (k m) -> p k m", k=DC); o += 2048
        w2 = view(o, 2048, "p (k m) -> p k m", k=IC); o += 2048
        w1q = view(o, 1024, "p (k m) -> p k m", dt=bf16, k=DC); o += 1024
        w2q = view(o, 1024, "p (k m) -> p k m", dt=bf16, k=IC); o += 1024
        wab = view(o, 2); o += 2
        wcl = view(o, 2); o += 2
        wsc = view(o, 2); o += 2
        hq = view(o, 1024, "p (b f) -> p b f", dt=bf16, b=NB); o += 1024
        hqT = view(o, 256, "p (d k t) -> p d k t", dt=bf16, d=2, k=DC); o += 256
        g1 = view(o, 2048, "p (d f) -> p d f", d=2); o += 2048
        g2 = view(o, 2048, "p (d f) -> p d f", d=2); o += 2048
        gq = view(o, 1024, "p (d f) -> p d f", dt=bf16, d=2); o += 1024
        gqT = view(o, 1024, "p (d k t) -> p d k t", dt=bf16, d=2, k=IC); o += 1024
        junk = view(o, 1024); o += 1024
        tv = view(o, 64, "p (n b) -> p n b", b=NB); o += 64
        hn = view(o, 256); o += 256
        ss1, am1, r1, sc1, f1 = (tv[:, k] for k in range(5))
        tv2 = view(o, 64, "p (n b) -> p n b", b=NB); o += 64
        ss2, am2, r2, sc2, f2 = (tv2[:, k] for k in range(5))
        normF = Norm("nF")
        s_f, wab_ready, wsum_done = sem("ffn_step"), sem("wab_ready"), sem("wsum_done")
        wq_ready, ss1_ready, r1_ready, hq_ready = sem("wq_ready"), sem("ss1_ready"), sem("r1_ready"), sem("hq_ready")
        hqT_done, hqT_ready, up_done = sem("hqT_done"), sem("hqT_ready"), sem("up_done")
        g1_ready, g2_ready, ss2_ready, r2_ready, gq_ready = (sem("g1_ready"), sem("g2_ready"), sem("ss2_ready"),
                                                             sem("r2_ready"), sem("gq_ready"))
        gqT_done, gqT_ready, down_done, x_ready, stored = (sem("gqT_done"), sem("gqT_ready"), sem("down_done"),
                                                           sem("x_ready"), sem("out_stored"))

        def quant_scales(eng, ch, am, r, sc, f, w_clip):
            ch.link(eng.tensor_tensor(f, am, r, ALU.mult))
            ch.link(eng.tensor_scalar(f, f, 1e-5, 1.0 / 127.0, ALU.max, ALU.mult))
            ch.link(eng.reciprocal(sc, f))
            ch.link(eng.tensor_scalar(f, f, w_clip, None, ALU.mult))

        def quantise(eng, ch, dst, src, tmp, r, sc):
            ch.link(eng.tensor_scalar(tmp, src, r, sc, ALU.mult, ALU.mult))
            ch.link(eng.tensor_scalar(tmp, tmp, MAGIC, MAGIC + 127.0, ALU.add, ALU.min))
            return eng.tensor_scalar(dst, tmp, -MAGIC, -128.0, ALU.add, ALU.max)

        with nc.Block() as block:
            @block.sync
            def _(eng):
                load(eng, "w12", w1, a["F_w1"])
                load(eng, "w12", w2, a["F_w2"])
                for b in range(NB):
                    eng.wait_ge(x_ready, b + 1)
                    eng.dma_start(out[:, b], x[:, b]).then_inc(stored, 16)
                eng.wait_ge(stored, 16 * NB)

            @block.gpsimd
            def _(eng):
                normF.pool(eng)
                eng.wait_ge(ss1_ready, NB)
                eng.wait_ge(normF.rstd_ready, 2)
                eng.tensor_scalar(ss1, ss1, 1e-24, 1.0 / D, ALU.max, ALU.mult).then_inc(r1_ready, 1)
                eng.wait_ge(r1_ready, 1)
                eng.tensor_tensor(r1, ss1, neg_half.to_broadcast([P, NB]), ALU.pow).then_inc(r1_ready, 1)
                for b in range(NB):
                    eng.wait_ge(ss2_ready, b + 1)
                    eng.tensor_scalar(ss2[:, b:b + 1], ss2[:, b:b + 1], 1e-24, 1.0 / INNER, ALU.max, ALU.mult).then_inc(r2_ready, 1)
                    eng.wait_ge(r2_ready, 2 * b + 1)
                    eng.tensor_tensor(r2[:, b:b + 1], ss2[:, b:b + 1], neg_half, ALU.pow).then_inc(r2_ready, 1)

            @block.vector
            def _(eng):
                ch = Chain(eng, s_f)
                normF.dve(eng)
                loaded(eng, "w12")
                for k, w in enumerate((w1, w2)):
                    t = eng.tensor_reduce(wab[:, k:k + 1], w.rearrange("p k m -> p (k m)"), AX.X, ALU.add,
                                          apply_absolute_value=True).then_inc(wab_ready, 1)
                eng.wait_ge(normF.h_ready, NB)
                ch.link(eng.tensor_reduce(am1, h, AX.X, ALU.max, apply_absolute_value=True))
                eng.wait_ge(wsum_done, 1)
                ch.link(eng.tensor_scalar(wcl, ps[:, 7, 0:2], 1.0 / (D * INNER), 1e-5, ALU.mult, ALU.max))
                ch.link(eng.reciprocal(wsc, wcl))
                eng.wait_ge(r1_ready, 2)
                quant_scales(eng, ch, am1, r1, sc1, f1, wcl[:, 0:1])
                for b in range(NB):
                    quantise(eng, ch, hq[:, b], h[:, b], hn, r1[:, b:b + 1], sc1[:, b:b + 1]).then_inc(hq_ready, 1)
                    eng.wait_ge(hq_ready, b + 1)
                for k, (w, wq) in enumerate(((w1, w1q), (w2, w2q))):
                    ch.link(eng.tensor_scalar(w, w, wsc[:, k:k + 1], MAGIC, ALU.mult, ALU.add))
                    ch.link(eng.tensor_scalar(w, w, -MAGIC, -1.0, ALU.add, ALU.max))
                    eng.tensor_scalar(wq, w, 1.0, None, ALU.min).then_inc(wq_ready, 1)
                for b in range(NB):
                    d = b % 2
                    one = slice(b, b + 1)
                    eng.wait_ge(g2_ready, b + 1)
                    ch.link(eng.tensor_reduce(am2[:, one], g2[:, d], AX.X, ALU.max, apply_absolute_value=True))
                    eng.wait_ge(r2_ready, 2 * b + 2)
                    quant_scales(eng, ch, am2[:, one], r2[:, one], sc2[:, one], f2[:, one], wcl[:, 1:2])
                    if b >= 2:
                        eng.wait_ge(gqT_done, b - 1)
                    quantise(eng, ch, gq[:, d], g2[:, d], g2[:, d], r2[:, one], sc2[:, one]).then_inc(gq_ready, 1)
                    if b:
                        eng.wait_ge(down_done, b)
                        eng.scalar_tensor_tensor(x[:, b - 1], ps[:, 7, 0:D], f2[:, b - 1:b], x[:, b - 1], ALU.mult,
                                                 ALU.add).then_inc(x_ready, 1)
                eng.wait_ge(down_done, NB)
                eng.scalar_tensor_tensor(x[:, NB - 1], ps[:, 7, 0:D], f2[:, NB - 1:NB], x[:, NB - 1], ALU.mult,
                                         ALU.add).then_inc(x_ready, 1)

            @block.scalar
            def _(eng):
                for b in range(NB):
                    eng.wait_ge(normF.h_ready, b + 1)
                    if b:
                        eng.wait_ge(ss1_ready, b)
                    eng.activation(junk[:, 0:D], h[:, b], ACT.Square, accum_out=ss1[:, b:b + 1]).then_inc(ss1_ready, 1)
                for b in range(NB):
                    d = b % 2
                    eng.wait_ge(hqT_done, b + 1)
                    if b >= 2:
                        eng.wait_ge(up_done, b - 1)
                    eng.activation(hqT[:, d], psb[:, d, 0:D].rearrange("p (k t) -> p k t", k=DC), ACT.Copy).then_inc(hqT_ready, 1)
                    eng.wait_ge(up_done, b + 1)
                    eng.activation(g1[:, d], ps[:, 2 + 2 * d:4 + 2 * d, :].rearrange("p k m -> p (k m)"), ACT.Gelu,
                                   scale=f1[:, b:b + 1]).then_inc(g1_ready, 1)
                    eng.wait_ge(g1_ready, b + 1)
                    if b >= 2:
                        eng.wait_ge(gq_ready, b - 1)
                    eng.activation(g2[:, d], g1[:, d], ACT.Gelu).then_inc(g2_ready, 1)
                    eng.wait_ge(g2_ready, b + 1)
                    eng.activation(g1[:, d], g2[:, d], ACT.Square, accum_out=ss2[:, b:b + 1]).then_inc(ss2_ready, 1)
                    eng.wait_ge(gqT_done, b + 1)
                    if b >= 2:
                        eng.wait_ge(down_done, b - 1)
                    eng.activation(gqT[:, d], psb[:, 6, :].rearrange("p (k t) -> p k t", k=IC), ACT.Copy).then_inc(gqT_ready, 1)

            @block.tensor
            def _(eng):
                eng.wait_ge(wab_ready, 2)
                eng.matmul(ps[:, 7, 0:2], ones, wab, start=True, stop=True).then_inc(wsum_done, 1)

                def up_(b):
                    d = b % 2
                    eng.wait_ge(hq_ready, b + 1)
                    if b >= 2:
                        eng.wait_ge(hqT_ready, b - 1)
                    for k in range(DC):
                        t = eng.transpose(psb[:, d, k * P:(k + 1) * P], hq[:, b, k * P:(k + 1) * P], ident_b)
                    t.then_inc(hqT_done, 1)
                    eng.wait_ge(hqT_ready, b + 1)
                    if b == 0:
                        eng.wait_ge(wq_ready, 2)
                    if b >= 2:
                        eng.wait_ge(g1_ready, b - 1)
                    for half in range(2):
                        for k in range(DC):
                            t = eng.matmul(ps[:, 2 + 2 * d + half, :], hqT[:, d, k], w1q[:, k, half * 512:(half + 1) * 512],
                                           start=k == 0, stop=k == DC - 1)
                    t.then_inc(up_done, 1)

                up_(0)
                for b in range(NB):
                    d = b % 2
                    eng.wait_ge(gq_ready, b + 1)
                    if b:
                        eng.wait_ge(gqT_ready, b)
                    for k in range(IC):
                        t = eng.transpose(psb[:, 6, k * P:(k + 1) * P], gq[:, d, k * P:(k + 1) * P], ident_b)
                    t.then_inc(gqT_done, 1)
                    if b + 1 < NB:
                        up_(b + 1)
                    eng.wait_ge(gqT_ready, b + 1)
                    if b:
                        eng.wait_ge(x_ready, b)
                    for k in range(IC):
                        t = eng.matmul(ps[:, 7, 0:D], gqT[:, d, k], w2q[:, k, :], start=k == 0, stop=k == IC - 1)
                    t.then_inc(down_done, 1)


def kernel(**inputs):
    import numpy as np
    import concourse.bacc as _bacc
    from concourse import mybir as _mybir
    from concourse.bass_utils import run_bass_kernel_spmd as _run

    g = {k: np.asarray(v) for k, v in inputs.items()}
    arrays = {}

    def put(name, v):
        arrays[name] = np.ascontiguousarray(v)

    def chunked(w, parts=P):
        return w.reshape(-1, parts, w.shape[-1]).transpose(1, 0, 2)

    pos = np.arange(P, dtype=np.float32)
    fA = (1.0 / np.float32(10000.0) ** (np.arange(0, R, 2, dtype=np.float32) / np.float32(R))).astype(np.float32)
    fX = (1.0 / np.float32(10000.0) ** (np.arange(R // 2, dtype=np.float32) / np.float32(R // 2))).astype(np.float32)
    iA, iX = np.arange(R) // 2, np.arange(R) % (R // 2)
    swA, swX = np.arange(R) ^ 1, (np.arange(R) + R // 2) % R
    sgA, sgX = np.where(np.arange(R) % 2 == 0, -1.0, 1.0), np.where(np.arange(R) < R // 2, -1.0, 1.0)
    for name, f, idx, sign in (("A", fA, iA, sgA), ("X", fX, iX, sgX)):
        ang = (pos[None, :] * f[idx][:, None]).astype(np.float32).astype(np.float64)
        c, s = np.cos(ang).astype(np.float32), (np.sin(ang) * sign[:, None]).astype(np.float32)
        one = np.ones_like(c)
        put("cos" + name, np.stack([np.concatenate([one, c]), np.concatenate([c, one])], 1))
        put("sin" + name, np.concatenate([s, s]))

    put("x", g["x"].transpose(1, 0, 2))
    put("ctxT", chunked(g["ctx_2048"].reshape(T, D).T))
    put("seg", g["itok_BxS_0_1023"].T)
    wq = g["L0_attn_w_query"].reshape(D, H, 2, R)
    put("A_qnT", wq[:, :, 0].transpose(2, 1, 0))
    pe = wq[:, :, 1].reshape(DC, P, H, R).transpose(1, 0, 2, 3)
    put("A_qr", pe.reshape(P, DC, H // 2, 2 * R))
    put("A_qrs", pe[..., swA].reshape(P, DC, H // 2, 2, R)[:, :, :, ::-1].reshape(P, DC, H // 2, 2 * R))
    wkvb = g["L0_attn_wkv_b"].reshape(R, H, R + VH)
    put("A_kbT", wkvb[:, :, :R].transpose(2, 1, 0))
    vT = wkvb[:, :, R:].transpose(2, 1, 0)
    put("A_vT", np.concatenate([vT, vT], -1))
    put("A_o", g["L0_attn_out_proj_w"].reshape(H, VH, D).transpose(1, 0, 2))
    kva = chunked(g["L0_attn_wkv_a"])
    kc, kp = kva[..., :R], kva[..., R:]
    put("A_wkv", np.stack([np.concatenate([kc, kp], -1), np.concatenate([kp, kc], -1),
                           np.concatenate([kp[..., swA]] * 2, -1)], 1))
    put("A_norm", np.concatenate([g["L0_attn_kv_norm_w"]] * 2).reshape(P, 1))
    put("X_kvcT", g["L0_xattn_W_kvc"].T)
    put("X_kr2", np.concatenate([g["L0_xattn_W_kr"], g["L0_xattn_W_kr"][:, swX]], -1))
    put("X_kvc", chunked(g["L0_xattn_W_kvc"]))
    put("X_uqT", g["L0_xattn_W_uq"].reshape(QC, H, VH).transpose(2, 1, 0))
    put("X_ukT", g["L0_xattn_W_uk"].reshape(R, H, VH).transpose(2, 1, 0))
    vT = g["L0_xattn_W_uv"].reshape(R, H, VH).transpose(2, 1, 0)
    put("X_vT", np.concatenate([vT, vT], -1))
    put("X_o", g["L0_xattn_W_o"].reshape(H, VH, D).transpose(1, 0, 2))
    qr = g["L0_xattn_W_qr"].reshape(QC, H, R)
    put("X_qr", qr.reshape(QC, H // 2, 2 * R))
    put("X_qrs", qr[..., swX].reshape(QC, H // 2, 2, R)[:, :, ::-1].reshape(QC, H // 2, 2 * R))
    put("X_dq", chunked(g["L0_xattn_W_dq"]))

    gu = np.concatenate([g["L0_ffn_w_gate"], g["L0_ffn_w_up"]], -1)
    put("E_gu", gu.reshape(E, DC, P, 2 * I).transpose(2, 1, 0, 3))
    put("E_dn", g["L0_ffn_w_down"].transpose(1, 0, 2))
    put("E_gate", chunked(g["L0_ffn_gate_w"].T))
    put("E_gate_b", g["L0_ffn_gate_b"].reshape(1, E))
    bias = np.concatenate([g["L0_ffn_b_gate"], g["L0_ffn_b_up"], g["L0_ffn_b_down"]], -1)
    put("E_bias", np.concatenate([bias] * 3))

    put("M_in", chunked(g["L1_attn_in_proj_w"].T))
    xp = g["L1_attn_x_proj_w"].T
    put("M_bc", chunked(np.concatenate([xp[:, :2 * ST]] * 3, -1)))
    put("M_dt", chunked(np.repeat(xp[:, 2 * ST:], P, -1)))
    put("M_out", chunked(g["L1_attn_out_proj_w"].T))
    col = lambda v: v.reshape(-1, P).T
    put("M_vec", np.concatenate([chunked(g["L1_attn_conv_w"].reshape(DI, KCONV)).reshape(P, CT * KCONV),
                                 col(g["L1_attn_conv_b"]), col(g["L1_attn_dt_w"]), col(g["L1_attn_dt_b"]),
                                 col(g["L1_attn_D_param"]), col(g["L1_attn_norm_w"]),
                                 chunked(g["L1_attn_A_log"]).reshape(P, CT * ST)], -1))
    put("W_u", col(g["L1_xattn_u"]))
    put("W_w", col(g["L1_xattn_w"]))
    put("F_w1", chunked(g["L1_ffn_w1"].T))
    put("F_w2", chunked(g["L1_ffn_w2"].T))

    nc = _bacc.Bacc("TRN2", target_bir_lowering=False, num_devices=1)
    aps = {n: nc.dram_tensor("in_" + n, v.shape, _mybir.dt.from_np(v.dtype), kind="ExternalInput").ap()
           for n, v in arrays.items()}
    out = nc.dram_tensor("out_x", (P, NB, D), fp32, kind="ExternalOutput").ap()
    decoder(nc, aps, out)
    r = _run(nc, [{"in_" + n: v for n, v in arrays.items()}], core_ids=[0])
    return r.results[0]["out_x"].transpose(1, 0, 2)
```

```python
import concourse.bass as bass
from concourse import mybir
from contextlib import ExitStack

fp32 = mybir.dt.float32
bf16 = mybir.dt.bfloat16
i32 = mybir.dt.int32
u32 = mybir.dt.uint32
ALU = mybir.AluOpType
ACT = mybir.ActivationFunctionType
AX = mybir.AxisListType

P = 128
NB = 8
D = 256
DC = D // P
T = NB * P
H = 16
R = 64
GH = 4
NG = H // GH
QC = 96
VH = 128
E = 32
TOPK = 4
I = 128
NBLK = 64
DI = 512
CT = DI // P
ST = 16
KCONV = 4
PAD = KCONV - 1
INNER = 1024
IC = INNER // P
NEG = -1.0e30
MAGIC = 12582912.0
LN_EPS = 1e-5


class Chain:

    def __init__(self, eng, sem):
        self.eng, self.sem, self.base, self.n = eng, sem, 0, 0

    def mark(self, ins):
        ins.then_inc(self.sem, 1)
        self.n += 1

    def wait(self):
        self.eng.wait_ge(self.sem, self.base + self.n)

    def link(self, ins):
        self.mark(ins)
        self.wait()

    def enter(self, i, per):
        self.before, self.per = self.n, per
        self.base, self.n = self.n + i * per, 0

    def leave(self, rounds):
        assert self.n == self.per, (self.n, self.per)
        self.base, self.n = 0, self.before + rounds * self.per


def decoder(nc, a, out):
    ctx = ExitStack()
    with ctx:
        def sem(name):
            return nc.alloc_semaphore(name=name)

        WORDS = 53200

        arena = ctx.enter_context(nc.sbuf_tensor("arena", [P, WORDS], fp32))
        ps = ctx.enter_context(nc.psum_tensor("ps", [P, 8, 512], fp32))
        first_layer = ExitStack()
        first_layer.enter_context(nc.cleanup_on_exit())

        psb = ps[:, :, :].bitcast(bf16)

        def view(at, n, pat=None, dt=fp32, parts=P, **dims):
            assert at + n <= WORDS, (at, n)
            v = arena[0:parts, at:at + n]
            if dt is not fp32:
                v = v.bitcast(dt)
            return v.rearrange(pat, **dims) if pat else v

        x = view(0, 2048, "p (b f) -> p b f", b=NB)
        hT = view(2048, 2048, "p (c t) -> p c t", c=DC)
        h = view(4096, 2048, "p (b f) -> p b f", b=NB)
        ctxT0 = view(4096, 2048, "p (c t) -> p c t", c=DC)
        at = 6144
        ident = view(at, P); at += P
        ones = view(at, P); at += P
        maskA = view(at, P); at += P
        maskX = view(at, 1024, "p (b t) -> p b t", b=NB); at += 1024
        rope = {}
        for name in "AX":
            rope[name] = (view(at, 256, "p (e t) -> p e t", e=2), view(at + 256, P)); at += 384
        small = view(at, 256); at += 256
        tri_b = view(at, 64, dt=bf16); at += 64
        ones_b = view(at, 64, dt=bf16); at += 64
        ident_b = view(at, 64, dt=bf16); at += 64
        stats = view(at, NB * 6, "p (b k) -> p b k", b=NB); at += NB * 6
        mv = view(at, NB * 2, "p (b k) -> p b k", b=NB); at += NB * 2
        var_eps = view(at, NB); at += NB
        rstd = view(at, NB); at += NB
        sumsq = view(at, NB); at += NB
        neg_half = view(at, 1); at += 1
        kv_norm = view(at, 1); at += 1
        zeros = view(at, 256); at += 256
        assert at <= 9216
        W0 = 9216
        A0 = W0 + 16384
        X0 = A0 + 11520
        K0 = X0 + 8704
        assert K0 + 6688 <= WORDS, K0

        layer = {}
        for name, base, kc, cw in (("A", A0, P, DC), ("X", X0, QC, 1)):
            o = base
            L = {"kc": kc, "chunks": cw}
            L["wq"] = view(o, cw * 2048, "p (c h m) -> p c h m", c=cw, h=H); o += cw * 2048
            L["wvo"] = view(o, 2048, "p (h m) -> p h m", h=H // 2); o += 2048
            L["wkv"] = view(o, 768, "p (e c m) -> p e c m", e=3, c=DC); o += 768
            L["key"] = view(o, 2048, "p (e t) -> p e t", e=2); o += 2048
            L["kvn"] = view(o, 512, "p (b r) -> p b r", b=NB); o += 512
            if name == "X":
                L["wdq"] = view(o, 192, "p (c m) -> p c m", c=DC); o += 192
                L["qc"] = view(o, 1024); o += 1024
            L["cos"], L["sin"] = rope[name]
            layer[name] = L
            assert o <= (X0 if name == "A" else K0), o
        rawA = W0
        wqnT = view(rawA, 4096, "p (h f) -> p h f", h=H)
        kbT = view(rawA + 4096, 1024, "p (h r) -> p h r", h=H)
        wvT = {"A": view(rawA + 5120, 2048, "p (h r) -> p h r", h=H)}
        wo = {"A": view(rawA + 7168, 4096, "p (h f) -> p h f", h=H)}
        rawX = rawA + 11264
        wuqT = view(rawX, 1536, "p (h q) -> p h q", h=H)
        wukT = view(rawX + 1536, 1024, "p (h r) -> p h r", h=H)
        wvT["X"] = view(rawX + 2560, 2048, "p (h r) -> p h r", h=H)
        wkvcT = view(rawX + 4608, 256)
        wkr2 = view(rawX + 4864, 128)
        wo["X"] = view(K0, 4096, "p (h f) -> p h f", h=H)
        o = K0 + 4096
        keytmp = view(o, 1024, "p (e t) -> p e t", e=2)
        o = K0
        q = view(o, 2048, "p (d h s) -> p d h s", d=NG, h=GH); o += 2048
        qsw = view(o, 512, "p (d h s) -> p d h s", d=2, h=GH // 2); o += 512
        sm = view(o, 1024, "p (d h t) -> p d h t", d=2, h=GH); o += 1024
        pr = view(o, 1024, "p (d h t) -> p d h t", d=2, h=GH); o += 1024
        prT = view(o, 1024, "p (d m) -> p d m", d=2); o += 1024
        uT = view(o, 512, "p (d h s) -> p d h s", d=2, h=GH // 2); o += 512
        un = view(o, 512, "p (d h r) -> p d h r", d=2, h=GH); o += 512
        mx = view(o, 8, "p (d h) -> p d h", d=2); o += 8
        negm = view(o, 8, "p (d h) -> p d h", d=2); o += 8
        rsum = view(o, 8, "p (d h) -> p d h", d=2); o += 8
        rinv = view(o, 8, "p (d h) -> p d h", d=2); o += 8
        assert o <= WORDS

        class Norm:

            def __init__(self, tag, rms=False):
                self.rms = rms
                if rms:
                    self.ln_ready = sem(tag + "_ln_ready")
                    self.sumsq_ready = sem(tag + "_sumsq")
                    self.added = sem(tag + "_ln_added")
                self.stats_in = sem(tag + "_stats_in")
                self.var_ready = sem(tag + "_var_ready")
                self.rstd_ready = sem(tag + "_rstd_ready")
                self.h_ready = sem(tag + "_h_ready")
                self.hT_done = sem(tag + "_hT_done")
                self.hT_ready = sem(tag + "_hT_ready")

            def dve_stats(self, eng, b):
                eng.bn_stats(stats[:, b, :], x[:, b, :]).then_inc(self.stats_in, 1)

            def dve_variance(self, eng):
                eng.wait_ge(self.stats_in, NB)
                for b in range(NB):
                    eng.bn_aggr(mv[:, b, :], stats[:, b, :]).then_inc(self.var_ready, 1)

            def dve(self, eng, begun=False):
                if not begun:
                    for b in range(NB):
                        self.dve_stats(eng, b)
                    self.dve_variance(eng)
                eng.wait_ge(self.rstd_ready, 2)
                eng.wait_ge(self.var_ready, NB)
                for b in range(NB):
                    eng.tensor_scalar(h[:, b, :], x[:, b, :], mv[:, b, 0:1], rstd[:, b:b + 1], ALU.subtract,
                                      ALU.mult).then_inc(self.ln_ready if self.rms else self.h_ready, 1)
                if self.rms:
                    for b in range(NB):
                        eng.wait_ge(self.ln_ready, b + 1)
                        eng.tensor_tensor(x[:, b, :], x[:, b, :], h[:, b, :], ALU.add).then_inc(self.added, 1)
                    eng.wait_ge(self.rstd_ready, 4)
                    for b in range(NB):
                        eng.wait_ge(self.added, b + 1)
                        eng.tensor_scalar(h[:, b, :], h[:, b, :], rstd[:, b:b + 1], None,
                                          ALU.mult).then_inc(self.h_ready, 1)

            def pool(self, eng):
                eng.wait_ge(self.var_ready, NB)
                eng.tensor_scalar(var_eps, mv[:, :, 1], LN_EPS, None, ALU.add).then_inc(self.rstd_ready, 1)
                eng.wait_ge(self.rstd_ready, 1)
                eng.tensor_tensor(rstd, var_eps, neg_half.to_broadcast([P, NB]), ALU.pow).then_inc(self.rstd_ready, 1)
                if self.rms:
                    eng.wait_ge(self.sumsq_ready, NB)
                    eng.wait_ge(self.ln_ready, NB)
                    eng.wait_ge(self.rstd_ready, 2)
                    eng.tensor_scalar(var_eps, sumsq, 1.0 / D, LN_EPS, ALU.mult, ALU.add).then_inc(self.rstd_ready, 1)
                    eng.wait_ge(self.rstd_ready, 3)
                    eng.tensor_tensor(rstd, var_eps, neg_half.to_broadcast([P, NB]), ALU.pow).then_inc(self.rstd_ready, 1)

            def pe(self, eng):
                for b in range(NB):
                    eng.wait_ge(self.h_ready, b + 1)
                    if b % 2 == 0 and b >= 4:
                        eng.wait_ge(self.hT_ready, b // 2 - 1)
                    for c in range(DC):
                        at = (b % 2) * D + c * P
                        t = eng.transpose(ps[:, (b // 2) % 2, at:at + P], h[:, b, c * P:(c + 1) * P], ident)
                    if b % 2:
                        t.then_inc(self.hT_done, 1)

            def act(self, eng, scale=None):
                if self.rms:
                    for b in range(NB):
                        eng.wait_ge(self.ln_ready, b + 1)
                        if b:
                            eng.wait_ge(self.sumsq_ready, b)
                        eng.activation(zeros, h[:, b, :], ACT.Square,
                                       accum_out=sumsq[:, b:b + 1]).then_inc(self.sumsq_ready, 1)
                for k in range(NB // 2):
                    eng.wait_ge(self.hT_done, k + 1)
                    src = ps[:, k % 2, :].rearrange("p (b c t) -> p c b t", b=2, c=DC)
                    dst = hT[:, :, k * D:(k + 1) * D].rearrange("p c (b t) -> p c b t", b=2)
                    if scale is None:
                        eng.activation(dst, src, ACT.Copy).then_inc(self.hT_ready, 1)
                    else:
                        for c in range(DC):
                            t = eng.activation(dst[:, c], src[:, c], ACT.Copy, scale=scale[:, c:c + 1])
                        t.then_inc(self.hT_ready, 1)

        class Keys:

            def __init__(self, tag):
                self.raw = sem(tag + "_key_raw")
                self.scaled = sem(tag + "_key_scaled")
                self.rotated = sem(tag + "_key_rotated")
                self.sq = sem(tag + "_key_sq")
                self.ssq = sem(tag + "_key_ssq")
                self.inv = sem(tag + "_key_inv")
                self.tok_done = sem(tag + "_kvn_done")
                self.tok = sem(tag + "_kvn")

        def pe_keys(eng, L, K, src, rms):
            for half in range(2):
                ts = slice(half * 512, half * 512 + 512)
                if half:
                    eng.wait_ge(K.scaled, 3)
                for e in range(3):
                    for c in range(DC):
                        t = eng.matmul(ps[:, 5 + e, :], L["wkv"][:, e, c, :], src[:, c, ts],
                                       start=c == 0, stop=c == DC - 1)
                t.then_inc(K.raw, 1)
                if rms:
                    eng.wait_ge(K.sq, half + 1)
                    eng.matmul(ps[:, 4, :], ones[0:R, :], keytmp[0:R, 1, :], start=True, stop=True).then_inc(K.ssq, 1)
            eng.wait_ge(K.rotated, 2)
            for b in range(NB):
                t = eng.transpose(ps[:, 4, b * R:(b + 1) * R], L["key"][0:R, 0, b * P:(b + 1) * P], ident[0:R, 0:R])
            t.then_inc(K.tok_done, 1)

        def dve_keys(eng, ch, L, K, rms):
            for half in range(2):
                ts = slice(half * 512, half * 512 + 512)
                t4 = "p (b t) -> p b t"
                eng.wait_ge(K.raw, half + 1)
                for e in range(2):
                    tab = L["cos"][:, e, :].unsqueeze(1).to_broadcast([P, 4, P])
                    eng.tensor_tensor(L["key"][:, e, ts].rearrange(t4, b=4), ps[:, 5 + e, :].rearrange(t4, b=4),
                                      tab, ALU.mult).then_inc(K.scaled, 1)
                tab = L["sin"].unsqueeze(1).to_broadcast([P, 4, P])
                eng.tensor_tensor(keytmp[:, 0, :].rearrange(t4, b=4), ps[:, 7, :].rearrange(t4, b=4),
                                  tab, ALU.mult).then_inc(K.scaled, 1)
                eng.wait_ge(K.scaled, 3 * half + 3)
                ch.mark(eng.tensor_tensor(L["key"][R:P, 0, ts], L["key"][R:P, 0, ts], keytmp[R:P, 0, :], ALU.add))
                last = eng.tensor_tensor(L["key"][0:R, 1, ts], L["key"][0:R, 1, ts], keytmp[0:R, 0, :], ALU.add)
                if rms:
                    ch.mark(last)
                    eng.wait_ge(K.ssq, half + 1)
                    eng.tensor_scalar(keytmp[:, 1, :], ps[:, 4, :], 1.0 / R, 1e-6, ALU.mult, ALU.add).then_inc(K.inv, 1)
                    eng.wait_ge(K.inv, 3 * half + 2)
                    eng.reciprocal(keytmp[:, 1, :], keytmp[:, 1, :]).then_inc(K.inv, 1)
                    eng.wait_ge(K.inv, 3 * half + 3)
                    ch.mark(eng.scalar_tensor_tensor(L["key"][0:R, 0, ts], L["key"][0:R, 0, ts], kv_norm[0:R, :],
                                                     keytmp[0:R, 1, :], ALU.mult, ALU.mult))
                    last = eng.scalar_tensor_tensor(L["key"][R:P, 1, ts], L["key"][R:P, 1, ts], kv_norm[R:P, :],
                                                    keytmp[R:P, 1, :], ALU.mult, ALU.mult)
                ch.wait()
                last.then_inc(K.rotated, 1)
                eng.wait_ge(K.rotated, half + 1)

        def act_keys(eng, L, K, rms):
            if rms:
                for half in range(2):
                    eng.wait_ge(K.scaled, 3 * half + 1)
                    if half:
                        eng.wait_ge(K.rotated, 1)
                    eng.activation(keytmp[0:R, 1, :], ps[0:R, 5, :], ACT.Square).then_inc(K.sq, 1)
                    eng.wait_ge(K.inv, 3 * half + 1)
                    eng.activation(keytmp[:, 1, :], keytmp[:, 1, :], ACT.Sqrt).then_inc(K.inv, 1)
            eng.wait_ge(K.tok_done, 1)
            eng.activation(L["kvn"], ps[:, 4, :].rearrange("p (b r) -> p b r", b=NB), ACT.Copy).then_inc(K.tok, 1)

        loads = {}

        def load(eng, name, dst, src):
            if name not in loads:
                loads[name] = [sem("ld_" + name), 0]
            loads[name][1] += 16
            eng.dma_start(dst, src).then_inc(loads[name][0], 16)

        def loaded(eng, *names):
            for n in names:
                eng.wait_ge(loads[n][0], loads[n][1])

        s_const = sem("const_step")
        s_seg = sem("mask_step")
        kr_done, kr_ready = sem("kr_done"), sem("kr_ready")
        absX_done, absX_ready = sem("absX_done"), sem("absX_ready")
        absA_done, absA_ready = sem("absA_done"), sem("absA_ready")
        vo_done, vo_even, vo_odd = sem("vo_done"), sem("vo_even"), sem("vo_odd")
        s_zero = sem("zeros_ready")
        keysX, keysA = Keys("X"), Keys("A")
        normA = Norm("nA")
        s_ch1 = sem("dve_chain1")
        LA, LX = layer["A"], layer["X"]
        NCONST = 6

        with nc.Block() as block:
            @block.sync
            def _(eng):
                load(eng, "ctx", ctxT0, a["ctxT"])
                load(eng, "kvX", wkvcT[0:R, :], a["X_kvcT"])
                load(eng, "kvX", wkr2[0:R, :], a["X_kr2"])
                load(eng, "kvX", LX["wkv"][:, 0, :, 0:R], a["X_kvc"])
                load(eng, "kvX", LX["wkv"][:, 1, :, R:P], a["X_kvc"])
                for name in "XA":
                    load(eng, "rope" + name, rope[name][0], a["cos" + name])
                    load(eng, "rope" + name, rope[name][1], a["sin" + name])
                load(eng, "x", x, a["x"])
                load(eng, "absX", wuqT, a["X_uqT"])
                load(eng, "absX", wukT, a["X_ukT"])
                load(eng, "kvA", LA["wkv"], a["A_wkv"])
                load(eng, "kvA", kv_norm, a["A_norm"])
                load(eng, "absA", wqnT[0:R], a["A_qnT"])
                load(eng, "absA", kbT[0:R], a["A_kbT"])
                load(eng, "voX", wvT["X"], a["X_vT"])
                load(eng, "voX", wo["X"], a["X_o"])
                load(eng, "voA", wvT["A"], a["A_vT"])
                load(eng, "voA", wo["A"], a["A_o"])
                load(eng, "qX", LX["wq"][0:QC, 0].rearrange("p (q e) m -> p q (e m)", e=2)[:, :, R:P + R], a["X_qr"])
                load(eng, "qX", LX["wdq"], a["X_dq"])
                for c in range(DC):
                    load(eng, "qA", LA["wq"][:, c].rearrange("p (q e) m -> p q (e m)", e=2)[:, :, R:P + R],
                         a["A_qr"][:, c])
                load(eng, "seg", small[:, 0:NB].bitcast(i32), a["seg"])

            @block.gpsimd
            def _(eng):
                eng.memset(zeros, 0.0).then_inc(s_zero, 1)
                eng.memset(ident, 0.0).then_inc(s_const, 1)
                eng.memset(maskA, 0.0).then_inc(s_const, 1)
                eng.memset(ones, 1.0).then_inc(s_const, 1)
                eng.memset(neg_half, -0.5).then_inc(s_const, 1)
                eng.wait_ge(s_const, 2)
                eng.affine_select(out=ident, in_=ident, compare_op=ALU.not_equal, fill=1.0, base=0,
                                  pattern=[[-1, P]], channel_multiplier=1).then_inc(s_const, 1)
                eng.affine_select(out=maskA, in_=maskA, compare_op=ALU.is_ge, fill=NEG, base=0,
                                  pattern=[[-1, P]], channel_multiplier=1).then_inc(s_const, 1)
                eng.memset(small[:, 128:256], 1.0).then_inc(s_const, 1)
                eng.wait_ge(s_const, 7)
                eng.affine_select(out=small[:, 128:256], in_=small[:, 128:256], compare_op=ALU.is_gt, fill=0.0, base=0,
                                  pattern=[[1, P]], channel_multiplier=-1).then_inc(s_const, 1)
                eng.wait_ge(s_const, 8)
                eng.tensor_copy(tri_b, small[:, 128:256]).then_inc(s_const, 1)
                eng.tensor_copy(ones_b, ones).then_inc(s_const, 1)
                eng.tensor_copy(ident_b, ident).then_inc(s_const, 1)
                eng.iota(maskX[:, :, :], pattern=[[0, NB], [1, P]], base=0, channel_multiplier=0,
                         allow_small_or_imprecise_dtypes=True).then_inc(s_const, 1)
                normA.pool(eng)

            @block.vector
            def _(eng):
                ch = Chain(eng, s_ch1)
                loaded(eng, "x")
                eng.wait_ge(s_const, 4)
                eng.wait_ge(kr_done, 1)
                src = ps[:, 0, 0:256].rearrange("p (c m) -> p c m", c=DC)
                for k, dst in enumerate((LX["wkv"][:, 0, :, R:P], LX["wkv"][:, 1, :, 0:R],
                                         LX["wkv"][:, 2, :, 0:R], LX["wkv"][:, 2, :, R:P])):
                    eng.tensor_copy(dst, src[:, :, R * (k // 2):R * (k // 2) + R]).then_inc(kr_ready, 1)
                loaded(eng, "ropeX")
                dve_keys(eng, ch, LX, keysX, False)
                eng.wait_ge(keysX.raw, 2)
                normA.dve(eng)
                loaded(eng, "seg")
                eng.wait_ge(s_const, 12)
                eng.tensor_copy(small[:, 16:16 + NB], small[:, 0:NB].bitcast(i32)).then_inc(s_seg, 1)
                eng.wait_ge(s_seg, 1)
                for b in range(NB):
                    eng.tensor_scalar(maskX[:, b, :], maskX[:, b, :], small[:, 16 + b:17 + b], None,
                                      ALU.subtract).then_inc(s_seg, 1)
                flat = maskX.rearrange("p b t -> p (b t)")
                late = view(rawA, 1024)
                eng.wait_ge(s_seg, 1 + NB)
                eng.wait_ge(absA_done, 4)
                eng.tensor_scalar(late, flat, 0.0, NEG, ALU.is_gt, ALU.mult).then_inc(s_seg, 1)
                eng.wait_ge(s_seg, 2 + NB)
                eng.tensor_scalar(flat, flat, -8.0, NEG, ALU.is_lt, ALU.mult).then_inc(s_seg, 1)
                eng.wait_ge(s_seg, 3 + NB)
                eng.tensor_tensor(flat, flat, late, ALU.add).then_inc(s_seg, 1)
                for n in range(H):
                    L, p = (LX, n) if n < 8 else (LA, n - 8)
                    eng.wait_ge(vo_done, n + 1)
                    eng.tensor_copy(L["wvo"][R:P, p, :], ps[R:P, 2 + n % 2, D:2 * D]).then_inc(vo_odd, 1)
                loaded(eng, "kvA", "ropeA")
                dve_keys(eng, ch, LA, keysA, True)

            @block.scalar
            def _(eng):
                for g in range(2):
                    eng.wait_ge(absX_done, g + 1)
                    for e in range(2):
                        dst = LX["wq"][0:QC, 0, 8 * g:8 * g + 8].rearrange("p (q e) m -> p q (e m)", e=2)
                        src = ps[0:QC, g, :].rearrange("p (q e r) -> p q e r", q=4, e=2)
                        t = eng.activation(dst[:, :, 192 * e:192 * e + R], src[:, :, e], ACT.Copy)
                    t.then_inc(absX_ready, 1)
                act_keys(eng, LX, keysX, False)
                for k in range(4):
                    c, g = k // 2, k % 2
                    eng.wait_ge(absA_done, k + 1)
                    for e in range(2):
                        dst = LA["wq"][:, c, 8 * g:8 * g + 8].rearrange("p (q e) m -> p q (e m)", e=2)
                        src = ps[:, k % 2, :].rearrange("p (q e r) -> p q e r", q=4, e=2)
                        t = eng.activation(dst[:, :, 192 * e:192 * e + R], src[:, :, e], ACT.Copy)
                    t.then_inc(absA_ready, 1)
                for n in range(H):
                    L, p = (LX, n) if n < 8 else (LA, n - 8)
                    eng.wait_ge(vo_done, n + 1)
                    eng.activation(L["wvo"][0:R, p, :], ps[0:R, 2 + n % 2, 0:D], ACT.Copy).then_inc(vo_even, 1)
                normA.act(eng)
                act_keys(eng, LA, keysA, True)

            @block.tensor
            def _(eng):
                loaded(eng, "kvX")
                for c in range(DC):
                    t = eng.matmul(ps[:, 0, c * P:(c + 1) * P], wkvcT[0:R, c * P:(c + 1) * P], wkr2[0:R, :],
                                   start=True, stop=True)
                t.then_inc(kr_done, 1)
                loaded(eng, "ctx")
                eng.wait_ge(kr_ready, 4)
                eng.wait_ge(s_const, 6)
                pe_keys_done = pe_keys(eng, LX, keysX, ctxT0, False)
                loaded(eng, "absX")
                for g in range(2):
                    for j in range(8):
                        hd = 8 * g + j
                        t = eng.matmul(ps[0:QC, g, j * R:(j + 1) * R], wuqT[:, hd, :], wukT[:, hd, :],
                                       start=True, stop=True)
                    t.then_inc(absX_done, 1)
                loaded(eng, "absA")
                for k in range(4):
                    c, g = k // 2, k % 2
                    if k < 2:
                        eng.wait_ge(absX_ready, k + 1)
                    else:
                        eng.wait_ge(absA_ready, k - 1)
                    for j in range(8):
                        hd = 8 * g + j
                        t = eng.matmul(ps[:, k % 2, j * R:(j + 1) * R], wqnT[0:R, hd, c * P:(c + 1) * P],
                                       kbT[0:R, hd, :], start=True, stop=True)
                    t.then_inc(absA_done, 1)
                loaded(eng, "voX", "voA")
                for n in range(H):
                    name, p = ("X", n) if n < 8 else ("A", n - 8)
                    if n >= 2:
                        eng.wait_ge(vo_even, n - 1)
                        eng.wait_ge(vo_odd, n - 1)
                    for e in range(2):
                        t = eng.matmul(ps[:, 2 + n % 2, e * D:(e + 1) * D], wvT[name][:, 2 * p + e, :],
                                       wo[name][:, 2 * p + e, :], start=True, stop=True)
                    t.then_inc(vo_done, 1)
                eng.wait_ge(absA_ready, 4)
                normA.pe(eng)
                eng.wait_ge(normA.hT_ready, 4)
                loaded(eng, "kvA")
                eng.wait_ge(keysX.tok, 1)
                pe_keys(eng, LA, keysA, hT, True)

        def near(b, g, off):
            g += off
            return (b - 1, g + 4) if g < 0 else (b + 1, g - 4) if g > 3 else (b, g)

        def four(stages, b, first, last):
            for g in range(4):
                for off, emit in stages:
                    if not ((first and g + off < 0) or (last and g + off > 3)):
                        emit(*near(b, g, off))

        def pipeline(eng, rounds, stages, ahead, behind):
            for off, emit in ahead:
                emit(0, off)
            four(stages, 0, True, False)
            with eng.Fori(1, rounds - 1) as b:
                four(stages, b, False, False)
            four(stages, rounds - 1, False, True)
            for off, emit in behind:
                emit(rounds - 1, off)

        swap_pairs = [k ^ 1 for k in range(32)]

        def attention(tag, L, scale, mask, per_batch_mask, prefetch):
            q_done, q_scaled, q_roped = sem(tag + "_q_done"), sem(tag + "_q_scaled"), sem(tag + "_q_roped")
            sc_done, masked, negm_ready = sem(tag + "_scores_done"), sem(tag + "_masked"), sem(tag + "_negm_ready")
            mx_ready = sem(tag + "_mx_ready")
            exp_done, rinv_ready = sem(tag + "_exp_done"), sem(tag + "_rinv_ready")
            prT_done, prT_ready = sem(tag + "_prT_done"), sem(tag + "_prT_ready")
            u_done, un_ready, v_done = sem(tag + "_u_done"), sem(tag + "_un_ready"), sem(tag + "_v_done")
            uT_ready, o_done, res_ready = sem(tag + "_uT_ready"), sem(tag + "_o_done"), sem(tag + "_res_ready")
            rotation = sem(tag + "_rotation")
            kc, chunks = L["kc"], L["chunks"]
            psQ, psS, psT, psU, psV, psO = 0, 2, 4, 5, 6, 7
            src = hT if chunks == DC else L["qc"].unsqueeze(1)

            def tok(b):
                return bass.ds(b * P, P)

            def pe_queries(eng, b, g):
                d, s = g % 2, 4 * b + g
                if not (isinstance(b, int) and s < 2):
                    eng.wait_ge(q_scaled, s - 1)
                for j in range(GH):
                    for c in range(chunks):
                        t = eng.matmul(ps[:, psQ + d, j * P:(j + 1) * P], L["wq"][0:kc, c, GH * g + j, :],
                                       src[0:kc, c, tok(b)], start=c == 0, stop=c == chunks - 1)
                t.then_inc(q_done, 1)

            def pe_scores(eng, b, g):
                d, s = g % 2, 4 * b + g
                eng.wait_ge(q_roped, s + 1)
                if not (isinstance(b, int) and s < 2):
                    eng.wait_ge(masked, s - 1)
                for j in range(GH):
                    t = eng.matmul(ps[:, psS + d, j * P:(j + 1) * P], q[:, g, j, :],
                                   L["key"][:, j % 2, tok(b)], start=True, stop=True)
                t.then_inc(sc_done, 1)

            def pe_transpose(eng, b, g):
                d, s = g % 2, 4 * b + g
                eng.wait_ge(exp_done, s + 1)
                if not (isinstance(b, int) and s < 1):
                    eng.wait_ge(prT_ready, s)
                for j in range(GH):
                    t = eng.transpose(ps[:, psT, j * P:(j + 1) * P], pr[:, d, j, :], ident)
                t.then_inc(prT_done, 1)

            def pe_values(eng, b, g):
                d, s = g % 2, 4 * b + g
                eng.wait_ge(prT_ready, s + 1)
                if not (isinstance(b, int) and s < 1):
                    eng.wait_ge(un_ready, s)
                for j in range(GH):
                    t = eng.matmul(ps[:, psU, j * R:(j + 1) * R], prT[:, d, j * P:(j + 1) * P],
                                   L["kvn"][:, bass.ds(b, 1), :].rearrange("p a r -> p (a r)"), start=True, stop=True)
                t.then_inc(u_done, 1)

            def pe_turn(eng, b, g):
                d, s = g % 2, 4 * b + g
                eng.wait_ge(un_ready, s + 1)
                if not (isinstance(b, int) and s < 1):
                    eng.wait_ge(uT_ready, s)
                for j in range(GH // 2):
                    t = eng.transpose(ps[:, psV, j * P:(j + 1) * P],
                                      un[:, d, 2 * j:2 * j + 2].rearrange("p h r -> p (h r)"), ident)
                t.then_inc(v_done, 1)

            def pe_output(eng, b, g):
                d, s = g % 2, 4 * b + g
                eng.wait_ge(uT_ready, s + 1)
                if g == 0 and not (isinstance(b, int) and b < 1):
                    eng.wait_ge(res_ready, b)
                for j in range(GH // 2):
                    t = eng.matmul(ps[:, psO, 0:D], uT[:, d, j, :], L["wvo"][:, GH // 2 * g + j, :],
                                   start=g == 0 and j == 0, stop=g == NG - 1 and j == GH // 2 - 1)
                t.then_inc(o_done, 1)

            def dve_queries(eng, b, g):
                d, s = g % 2, 4 * b + g
                eng.wait_ge(q_done, s + 1)
                if not (isinstance(b, int) and s < 2):
                    eng.wait_ge(q_roped, s - 1)
                if not (isinstance(b, int) and s < NG):
                    eng.wait_ge(sc_done, s - 3)
                pq = ps[:, psQ + d, :].rearrange("p (a e s) -> p a e s", a=2, e=2)
                eng.tensor_tensor(q[:, g].rearrange("p (a e) s -> p a e s", e=2), pq,
                                  L["cos"].unsqueeze(1).to_broadcast([P, 2, 2, P]), ALU.mult)
                eng.stream_shuffle(qsw[R:P, d], pq[R:P, :, 0], swap_pairs)
                eng.stream_shuffle(qsw[0:R, d], pq[0:R, :, 1], swap_pairs).then_inc(q_scaled, 1)

            def pool_rotate(eng, b, g):
                d, s = g % 2, 4 * b + g
                eng.wait_ge(q_scaled, s + 1)
                eng.tensor_tensor(qsw[:, d], qsw[:, d], L["sin"].unsqueeze(1).to_broadcast([P, 2, P]),
                                  ALU.mult).then_inc(rotation, 1)
                eng.wait_ge(rotation, 2 * s + 1)
                qe = q[:, g].rearrange("p (a e) s -> p a e s", e=2)
                eng.tensor_tensor(qe[R:P, :, 0], qe[R:P, :, 0], qsw[R:P, d], ALU.add).then_inc(rotation, 1)
                eng.wait_ge(rotation, 2 * s + 2)
                eng.tensor_tensor(qe[0:R, :, 1], qe[0:R, :, 1], qsw[0:R, d], ALU.add).then_inc(q_roped, 1)

            def dve_softmax(eng, b, g):
                d, s = g % 2, 4 * b + g
                eng.wait_ge(sc_done, s + 1)
                if not (isinstance(b, int) and s < 2):
                    eng.wait_ge(exp_done, s - 1)
                m = mask[:, b, :] if per_batch_mask and isinstance(b, int) else (
                    mask[:, bass.ds(b, 1), :].rearrange("p a t -> p (a t)") if per_batch_mask else mask)
                eng.tensor_tensor(sm[:, d], ps[:, psS + d, :].rearrange("p (h t) -> p h t", h=GH),
                                  m.unsqueeze(1).to_broadcast([P, GH, P]), ALU.add).then_inc(masked, 1)
                eng.wait_ge(masked, s + 1)
                eng.tensor_reduce(mx[:, d], sm[:, d], AX.X, ALU.max).then_inc(mx_ready, 1)
                eng.wait_ge(mx_ready, s + 1)
                eng.tensor_scalar(negm[:, d], mx[:, d], -scale, None, ALU.mult).then_inc(negm_ready, 1)

            def dve_inverse(eng, b, g):
                d, s = g % 2, 4 * b + g
                eng.wait_ge(exp_done, s + 1)
                eng.reciprocal(rinv[:, d], rsum[:, d]).then_inc(rinv_ready, 1)

            def dve_normalise(eng, b, g):
                d, s = g % 2, 4 * b + g
                eng.wait_ge(rinv_ready, s + 1)
                eng.wait_ge(u_done, s + 1)
                if not (isinstance(b, int) and s < 2):
                    eng.wait_ge(v_done, s - 1)
                eng.tensor_tensor(un[:, d], ps[:, psU, 0:GH * R].rearrange("p (h r) -> p h r", h=GH),
                                  rinv[:, d].unsqueeze(2).to_broadcast([P, GH, R]), ALU.mult).then_inc(un_ready, 1)

            def dve_residual(eng, b):
                eng.wait_ge(o_done, 4 * b + 4)
                eng.tensor_tensor(x[:, bass.ds(b, 1), :].rearrange("p a f -> p (a f)"),
                                  x[:, bass.ds(b, 1), :].rearrange("p a f -> p (a f)"),
                                  ps[:, psO, 0:D], ALU.add).then_inc(res_ready, 1)

            def act_exp(eng, b, g):
                d, s = g % 2, 4 * b + g
                eng.wait_ge(negm_ready, s + 1)
                if not (isinstance(b, int) and s < 2):
                    eng.wait_ge(prT_done, s - 1)
                    eng.wait_ge(rinv_ready, s - 1)
                for j in range(GH):
                    t = eng.activation(pr[:, d, j, :], sm[:, d, j, :], ACT.Exp, bias=negm[:, d, j:j + 1],
                                       scale=scale, accum_out=rsum[:, d, j:j + 1])
                t.then_inc(exp_done, 1)

            def act_probs(eng, b, g):
                d, s = g % 2, 4 * b + g
                eng.wait_ge(prT_done, s + 1)
                if not (isinstance(b, int) and s < 2):
                    eng.wait_ge(u_done, s - 1)
                eng.activation(prT[:, d, :], ps[:, psT, :], ACT.Copy).then_inc(prT_ready, 1)

            def act_values(eng, b, g):
                d, s = g % 2, 4 * b + g
                eng.wait_ge(v_done, s + 1)
                if not (isinstance(b, int) and s < 2):
                    eng.wait_ge(o_done, s - 1)
                eng.activation(uT[:, d], ps[:, psV, 0:D].rearrange("p (a s) -> p a s", a=2),
                               ACT.Copy).then_inc(uT_ready, 1)

            with nc.Block() as block:
                @block.tensor
                def _(eng):
                    Q = lambda b, g: pe_queries(eng, b, g)
                    S = lambda b, g: pe_scores(eng, b, g)
                    TR = lambda b, g: pe_transpose(eng, b, g)
                    U = lambda b, g: pe_values(eng, b, g)
                    O = lambda b, g: pe_output(eng, b, g)
                    V = lambda b, g: pe_turn(eng, b, g)
                    pipeline(eng, NB, [(-3, O), (-2, V), (-1, U), (1, S), (3, Q), (0, TR)],
                             [(0, Q), (1, Q), (2, Q), (0, S)], [(1, O), (2, V), (3, U), (2, O), (3, V), (3, O)])

                @block.vector
                def _(eng):
                    SF = lambda b, g: dve_softmax(eng, b, g)
                    QS = lambda b, g: dve_queries(eng, b, g)
                    IN = lambda b, g: dve_inverse(eng, b, g)
                    UN = lambda b, g: dve_normalise(eng, b, g)

                    def RS(b, g):
                        if g == NG - 1:
                            dve_residual(eng, b)
                    pipeline(eng, NB, [(-3, RS), (-1, IN), (-1, UN), (1, SF), (3, QS)],
                             [(0, QS), (1, QS), (2, QS), (0, SF)], [(3, IN), (3, UN), (3, RS)])

                @block.scalar
                def _(eng):
                    EX = lambda b, g: act_exp(eng, b, g)
                    PT = lambda b, g: act_probs(eng, b, g)
                    UT = lambda b, g: act_values(eng, b, g)
                    pipeline(eng, NB, [(-2, UT), (0, PT), (1, EX)], [(0, EX)], [(2, UT), (3, UT)])

                @block.gpsimd
                def _(eng):
                    RO = lambda b, g: pool_rotate(eng, b, g)
                    pipeline(eng, NB, [(3, RO)], [(0, RO), (1, RO), (2, RO)], [])

                @block.sync
                def _(eng):
                    prefetch(eng)

        wgu = view(W0, 16384, "p (c e m) -> p c e m", c=DC, e=E)
        hd = nc.dram_tensor("tokens", (T, D), fp32).ap()
        ys = nc.dram_tensor("expert_out", (NBLK * P, D), fp32).ap()

        def prefetch_up(eng):
            for e in range(0, E, 8):
                for c in range(DC):
                    load(eng, "wgu", wgu[:, c, e:e + 8], a["E_gu"][:, c, e:e + 8])

        attention("A", LA, float(P) ** -0.5, maskA, False, prefetch_up)

        normX = Norm("nX")
        qc_done, qc_ready = sem("qc_done"), sem("qc_ready")
        with nc.Block() as block:
            @block.vector
            def _(eng):
                normX.dve(eng)

            @block.gpsimd
            def _(eng):
                normX.pool(eng)

            @block.scalar
            def _(eng):
                normX.act(eng)
                for k in range(2):
                    eng.wait_ge(qc_done, k + 1)
                    eng.activation(LX["qc"][0:QC, k * 512:(k + 1) * 512], ps[0:QC, 2 + k, :], ACT.Copy).then_inc(qc_ready, 1)

            @block.tensor
            def _(eng):
                normX.pe(eng)
                for k in range(2):
                    eng.wait_ge(normX.hT_ready, 2 * k + 2)
                    for c in range(DC):
                        t = eng.matmul(ps[0:QC, 2 + k, :], LX["wdq"][:, c, :], hT[:, c, k * 512:(k + 1) * 512],
                                       start=c == 0, stop=c == DC - 1)
                    t.then_inc(qc_done, 1)
                loaded(eng, "qX")
                eng.wait_ge(qc_ready, 2)

        wdn = view(A0, 8192, "p (e m) -> p e m", e=E)
        sel = view(51104, 2048, "p (e m) -> p e m", dt=bf16, e=E)
        bias_f = view(A0 + 10240, 512)
        bias_b = view(A0 + 10752, 256, dt=bf16)
        gate_w = view(A0 + 11008, 64, "p (c e) -> p c e", c=DC)
        gate_b = view(A0 + 11072, 32)

        def prefetch_down(eng):
            load(eng, "wdn", wdn, a["E_dn"])
            load(eng, "gate", gate_w, a["E_gate"])
            load(eng, "gate", gate_b[0:1, :], a["E_gate_b"])
            load(eng, "bias", bias_f[0:3 * E, :], a["E_bias"])

        attention("X", LX, float(VH + R) ** -0.5, maskX, True, prefetch_down)

        o = X0
        logits = view(o, 256, "p (b e) -> p b e", b=NB); o += 256
        top = view(o, 64, "p (b k) -> p b k", b=NB); o += 64
        topi = view(o, 64, "p (b k) -> p b k", dt=u32, b=NB); o += 64
        idxf = view(o, 32, "p (b k) -> p b k", b=NB); o += 32
        gw = view(o, 32, "p (b k) -> p b k", b=NB); o += 32
        gsum = view(o, NB); o += NB
        iotaE = view(o, E); o += E
        iotaJ = view(o, NBLK); o += NBLK
        pick = view(o, 1024, "p (n e) -> p n e", e=E); o += 1024
        prod = view(o, 1024, "p (n e) -> p n e", e=E); o += 1024
        memb = view(o, 256, "p (b e) -> p b e", b=NB); o += 256
        cum = view(o, 288, "p (b e) -> p b e", b=NB + 1); o += 288
        memb_b = view(o, 128, dt=bf16); o += 128
        cum_b = view(o, 144, dt=bf16); o += 144
        nblk = view(o, E); o += E
        incl = view(o, E); o += E
        base = view(o, E); o += E
        place = view(o, 256, "p (b e) -> p b e", b=NB); o += 256
        slot = view(o, 32); o += 32
        slot_i = view(o, 32, dt=i32); o += 32
        cmp = view(o, E); o += E
        owner = view(o, 1); o += 1
        owner_i = view(o, NBLK, dt=i32); o += NBLK
        biastmp = view(o, 1024, "p (k m) -> p k m", k=2); o += 1024
        assert o <= K0
        o = K0
        at_pos = view(o, 2048, "p (m t) -> p m t", dt=bf16, m=NB * TOPK); o += 2048
        at_blk = view(o, 1024, "p (m j) -> p m j", dt=bf16, m=NB * TOPK); o += 1024
        id_blk = view(o, 2048, "p (e m j) -> p e m j", dt=bf16, e=2, m=NB * TOPK); o += 2048
        tok_lo = view(o, NBLK); o += NBLK
        blk = view(o, 32); o += 32
        assert o <= 51104
        tok_i = small[:, 0:NBLK + 1].bitcast(i32)
        iotaT, iotaP = small[:, 64:65], small[:, 128:256]
        tok_u = small[:, 68:72].bitcast(i32)
        normM = Norm("nM")
        s_iota, s_sel = sem("iota_ready"), sem("sel_ready")
        lg_done, pos_done = sem("logits_done"), sem("positions_done")
        s_route, w_exp = sem("route_step"), sem("gate_exp")
        memb_ready, slot_ready, owner_ready, bias_ready = (sem("memb_ready"), sem("slot_ready"), sem("owner_ready"),
                                                           sem("bias_ready"))
        gw_ready, s_top = sem("gate_weights_ready"), sem("top_step")
        neg_top = sem("neg_top")
        tokens_out, map_in, map_done, map_ready = sem("tokens_out"), sem("map_in"), sem("map_done"), sem("map_ready")

        def split3(eng, ch, dst, src, tmp):
            n = 3 * E
            ch.link(eng.tensor_copy(dst[0:n], src[0:n]))
            ch.link(eng.tensor_tensor(src[0:n], src[0:n], dst[0:n], ALU.subtract))
            ch.mark(eng.tensor_copy(dst[E:2 * E], src[E:2 * E]))
            ch.link(eng.tensor_copy(tmp[0:n], src[0:n]))
            ch.link(eng.tensor_tensor(src[2 * E:n], src[2 * E:n], tmp[2 * E:n], ALU.subtract))
            ch.link(eng.tensor_copy(dst[2 * E:n], src[2 * E:n]))

        with nc.Block() as block:
            @block.sync
            def _(eng):
                for b in range(NB):
                    eng.wait_ge(normM.h_ready, b + 1)
                    eng.dma_start(hd[b * P:(b + 1) * P], h[:, b]).then_inc(tokens_out, 16)
                eng.wait_ge(tokens_out, 16 * NB)

            @block.gpsimd
            def _(eng):
                eng.iota(iotaE, pattern=[[1, E]], base=0, channel_multiplier=0,
                         allow_small_or_imprecise_dtypes=True).then_inc(s_iota, 1)
                eng.iota(iotaJ, pattern=[[1, NBLK]], base=0, channel_multiplier=0,
                         allow_small_or_imprecise_dtypes=True).then_inc(s_iota, 1)
                eng.iota(iotaP, pattern=[[1, P]], base=0, channel_multiplier=0,
                         allow_small_or_imprecise_dtypes=True).then_inc(s_iota, 1)
                eng.iota(iotaT, pattern=[[0, 1]], base=0, channel_multiplier=1,
                         allow_small_or_imprecise_dtypes=True).then_inc(s_iota, 1)
                normM.pool(eng)
                eng.memset(sel[0:3 * E], 0.0).then_inc(s_sel, 1)
                for m in range(3):
                    eng.wait_ge(s_sel, m + 1)
                    eng.affine_select(out=sel[0:3 * E], in_=sel[0:3 * E], compare_op=ALU.not_equal, fill=1.0,
                                      base=-E * m, pattern=[[-1, E], [0, P]], channel_multiplier=1).then_inc(s_sel, 1)

            @block.vector
            def _(eng):
                ch = Chain(eng, s_route)
                normM.dve(eng)
                loaded(eng, "bias")
                split3(eng, ch, bias_b, bias_f, biastmp[:, 0, :].bitcast(bf16)[:, 0:512])
                for b in range(NB):
                    if b % 4 == 0:
                        eng.wait_ge(lg_done, b // 4 + 1)
                        ch.link(eng.tensor_copy(logits[:, b:b + 4], ps[:, 2 + b // 4, 0:4 * E].rearrange("p (b e) -> p b e", b=4)))
                    eng.max(top[:, b], logits[:, b]).then_inc(s_top, 1)
                    eng.wait_ge(s_top, 2 * b + 1)
                    eng.max_index(topi[:, b], top[:, b], logits[:, b]).then_inc(s_top, 1)
                eng.wait_ge(s_top, 2 * NB)
                ch.mark(eng.tensor_copy(idxf, topi[:, :, 0:TOPK]))
                eng.tensor_tensor(gw, top[:, :, 0:TOPK], top[:, :, 0:1].to_broadcast([P, NB, TOPK]),
                                  ALU.subtract).then_inc(neg_top, 1)
                ch.wait()
                eng.wait_ge(s_iota, 4)
                pk = "p (b k) e -> p b k e"
                ch.link(eng.tensor_tensor(pick, idxf.rearrange("p b k -> p (b k)").unsqueeze(2).to_broadcast([P, 32, E]),
                                          iotaE.unsqueeze(1).to_broadcast([P, 32, E]), ALU.is_equal))
                ch.mark(eng.memset(cum[:, 0], 0.0))
                ch.link(eng.tensor_reduce(memb, pick.rearrange("p (b k) e -> p b e k", b=NB), AX.X, ALU.add))
                for b in range(NB):
                    ch.link(eng.tensor_tensor(cum[:, b + 1], cum[:, b], memb[:, b], ALU.add))
                ch.mark(eng.tensor_copy(memb_b, memb.rearrange("p b e -> p (b e)")))
                ch.link(eng.tensor_copy(cum_b, cum.rearrange("p b e -> p (b e)")))
                eng.tensor_copy(biastmp[:, 1, 0:1], iotaE[:, 0:1]).then_inc(memb_ready, 1)
                eng.wait_ge(pos_done, 1)
                ch.link(eng.tensor_scalar(nblk, ps[:, 4, 0:E], 1.0 / P, (P - 1.0) / P - 0.5 + 1.0 / 256, ALU.mult, ALU.add))
                ch.link(eng.tensor_scalar(nblk, nblk, MAGIC, None, ALU.add))
                ch.link(eng.tensor_scalar(nblk, nblk, -MAGIC, None, ALU.add))
                ch.link(eng.tensor_tensor_scan(incl, ones[:, 0:E], nblk, 0.0, ALU.mult, ALU.add))
                ch.link(eng.tensor_tensor(base, incl, nblk, ALU.subtract))
                ch.link(eng.scalar_tensor_tensor(place, base.unsqueeze(1).to_broadcast([P, NB, E]), float(P),
                                                 ps[:, 5, 0:256].rearrange("p (b e) -> p b e", b=NB), ALU.mult, ALU.add))
                ch.link(eng.tensor_tensor(prod.rearrange(pk, b=NB), pick.rearrange(pk, b=NB),
                                          place.unsqueeze(2).to_broadcast([P, NB, TOPK, E]), ALU.mult))
                ch.link(eng.tensor_reduce(slot, prod, AX.X, ALU.add))
                eng.tensor_copy(slot_i, slot).then_inc(slot_ready, 1)
                ch.link(eng.tensor_scalar(blk, slot, 1.0 / P, 1.0 / 256 - 0.5, ALU.mult, ALU.add))
                ch.link(eng.tensor_scalar(blk, blk, MAGIC, None, ALU.add))
                ch.link(eng.tensor_scalar(blk, blk, -MAGIC, None, ALU.add))
                ch.link(eng.scalar_tensor_tensor(slot, blk, -float(P), slot, ALU.mult, ALU.add))
                ch.mark(eng.tensor_tensor(at_blk, blk.unsqueeze(2).to_broadcast([P, NB * TOPK, NBLK]),
                                          iotaJ.unsqueeze(1).to_broadcast([P, NB * TOPK, NBLK]), ALU.is_equal))
                eng.tensor_tensor(at_pos, slot.unsqueeze(2).to_broadcast([P, NB * TOPK, P]),
                                  iotaP.unsqueeze(1).to_broadcast([P, NB * TOPK, P]), ALU.is_equal).then_inc(map_in, 1)
                ch.wait()
                eng.tensor_scalar(id_blk[:, 0], at_blk, iotaT, None, ALU.mult).then_inc(map_in, 1)
                for b in range(NB):
                    ns = slice(b * TOPK, (b + 1) * TOPK)
                    eng.tensor_scalar(id_blk[:, 1, ns], at_blk[:, ns], float(b), None, ALU.mult).then_inc(map_in, 1)
                ch.link(eng.tensor_scalar(cmp, incl, iotaT, None, ALU.is_le))
                ch.link(eng.tensor_reduce(owner, cmp, AX.X, ALU.add))
                eng.tensor_scalar(owner, owner, E - 1.0, None, ALU.min).then_inc(owner_ready, 1)
                eng.wait_ge(w_exp, 1)
                ch.link(eng.tensor_reduce(gsum, gw, AX.X, ALU.add))
                ch.link(eng.reciprocal(gsum, gsum))
                eng.tensor_tensor(gw, gw, gsum.unsqueeze(2).to_broadcast([P, NB, TOPK]), ALU.mult).then_inc(gw_ready, 1)
                eng.wait_ge(map_done, 2)
                eng.tensor_copy(owner_i[0:1, :], ps[0:1, 7, 0:NBLK]).then_inc(map_ready, 1)
                ch.link(eng.tensor_copy(tok_lo, ps[:, 6, 0:NBLK]))
                eng.scalar_tensor_tensor(tok_i[:, 0:NBLK], ps[:, 6, NBLK:2 * NBLK], float(P), tok_lo, ALU.mult,
                                         ALU.add).then_inc(map_ready, 1)
                eng.wait_ge(map_ready, 2)

            @block.scalar
            def _(eng):
                normM.act(eng)
                eng.wait_ge(neg_top, 1)
                eng.activation(gw, gw, ACT.Exp).then_inc(w_exp, 1)

            @block.tensor
            def _(eng):
                normM.pe(eng)
                loaded(eng, "gate")
                for b in range(NB):
                    if b % 2 == 0:
                        eng.wait_ge(normM.hT_ready, b // 2 + 1)
                    dst = ps[:, 2 + b // 4, (b % 4) * E:(b % 4 + 1) * E]
                    for c in range(DC):
                        eng.matmul(dst, hT[:, c, b * P:(b + 1) * P], gate_w[:, c, :], start=c == 0, stop=False)
                    t = eng.matmul(dst, ones[0:1, :], gate_b[0:1, :], start=False, stop=True)
                    if b % 4 == 3:
                        t.then_inc(lg_done, 1)
                eng.wait_ge(memb_ready, 1)
                eng.matmul(ps[:, 4, 0:E], ones_b, cum_b[:, NB * E:(NB + 1) * E], start=True, stop=True)
                eng.matmul(ps[:, 5, 0:256], ones_b, cum_b[:, 0:256], start=True, stop=False)
                eng.matmul(ps[:, 5, 0:256], tri_b, memb_b, start=False, stop=True).then_inc(pos_done, 1)
                eng.wait_ge(map_in, 2 + NB)
                for n in range(NB * TOPK):
                    t = eng.matmul(ps[:, 6, 0:2 * NBLK], at_pos[:, n], id_blk[:, :, n],
                                   start=n == 0, stop=n == NB * TOPK - 1)
                t.then_inc(map_done, 1)
                eng.wait_ge(owner_ready, 1)
                eng.matmul(ps[0:1, 7, 0:NBLK], owner, ident[:, 0:NBLK], start=True, stop=True).then_inc(map_done, 1)

        o = K0
        xin = view(o, 1024, "p (u f) -> p u f", u=4); o += 1024
        xinT = view(o, 512, "p (d c t) -> p d c t", d=2, c=DC); o += 512
        gate = view(o, 256, "p (d m) -> p d m", d=2); o += 256
        sig = view(o, 256, "p (d m) -> p d m", d=2); o += 256
        up = view(o, 256, "p (d m) -> p d m", d=2); o += 256
        act_ = view(o, 256, "p (d m) -> p d m", d=2); o += 256
        actT = view(o, 256, "p (d m) -> p d m", d=2); o += 256
        yout = view(o, 1024, "p (u f) -> p u f", u=4); o += 1024
        x_in = [sem(f"block_in{u}") for u in range(4)]
        tok_ready = sem("block_tokens")
        y_out = [sem(f"block_out{u}") for u in range(4)]
        xT_done, xT_ready, gu_done, gate_ready = sem("xT_done"), sem("xT_ready"), sem("gu_done"), sem("gate_ready")
        up_ready, sig_ready, gs_ready, act_ready = sem("up_ready"), sem("sig_ready"), sem("gs_ready"), sem("act_ready")
        aT_done, aT_ready, dn_done, y_ready = sem("aT_done"), sem("aT_ready"), sem("dn_done"), sem("y_ready")

        def early(b, n, s):
            return isinstance(b, int) and s < n

        with nc.Block() as block:
            @block.gpsimd
            def _(eng):
                def LD(i, u):
                    s, (i1, v) = 4 * i + u, near(i, u, 1)
                    if not early(i1, 4, s + 1):
                        eng.wait_ge(x_in[v], 16 * i1)
                    if not early(i, 4, s):
                        eng.wait_ge(xT_done, s - 3)
                    eng.wait_ge(tok_ready, s + 1)
                    eng.tensor_copy(tok_u[:, v:v + 1], tok_i[:, bass.ds(s + 1, 1)]).then_inc(tok_ready, 1)
                    eng.indirect_dma_start(xin[:, u], None, hd,
                                           bass.IndirectOffsetOnAxis(ap=tok_u[:, u:u + 1].bitcast(u32), axis=0)
                                           ).then_inc(x_in[u], 16)

                eng.tensor_copy(tok_u[:, 0:1], tok_i[:, 0:1]).then_inc(tok_ready, 1)
                pipeline(eng, NBLK // 4, [(4, LD)], [(u, LD) for u in range(4)], [])

            @block.sync
            def _(eng):
                def SR(i, u):
                    s = 4 * i + u
                    eng.wait_ge(y_ready, s + 1)
                    eng.dma_start(ys[bass.ds(s * P, P), :], yout[:, u]).then_inc(y_out[u], 16)

                pipeline(eng, NBLK // 4, [(-3, SR)], [], [(u, SR) for u in range(1, 4)])
                for u in range(4):
                    eng.wait_ge(y_out[u], 16 * (NBLK // 4))

            @block.tensor
            def _(eng):
                loaded(eng, "wgu", "wdn")

                def TX(i, u):
                    s, d = 4 * i + u, u % 2
                    eng.wait_ge(x_in[u], 16 * i + 16)
                    if not early(i, 2, s):
                        eng.wait_ge(xT_ready, s - 1)
                    for c in range(DC):
                        t = eng.transpose(ps[:, d, c * P:(c + 1) * P], xin[:, u, c * P:(c + 1) * P], ident)
                    t.then_inc(xT_done, 1)

                e_up, e_mid, e_low, e_down = (eng.alloc_register(n) for n in ("e_up", "e_mid", "e_low", "e_down"))

                def OW(i, u):
                    eng.reg_load(e_up, owner_i[0:1, bass.ds(4 * i + u, 1)])

                def SH(i, u):
                    eng.reg_mov(e_down, e_low)
                    eng.reg_mov(e_low, e_mid)
                    eng.reg_mov(e_mid, e_up)

                eng.reg_mov(e_mid, 0)
                eng.reg_mov(e_low, 0)

                def GU(i, u):
                    s, d = 4 * i + u, u % 2
                    e = eng.snap(e_up, min_val=0, max_val=E - 1)
                    eng.wait_ge(xT_ready, s + 1)
                    if not early(i, 2, s):
                        eng.wait_ge(gate_ready, s - 1)
                        eng.wait_ge(up_ready, s - 1)
                    for c in range(DC):
                        eng.matmul(ps[:, 2 + d, 0:2 * I], xinT[:, d, c, :],
                                   wgu[:, c, bass.ds(e, 1), :].rearrange("p a m -> p (a m)"), start=c == 0, stop=False)
                    eng.matmul(ps[:, 2 + d, 0:2 * I], sel[0:3 * E, bass.ds(e, 1), :].rearrange("p a m -> p (a m)"),
                               bias_b[0:3 * E, 0:2 * I], start=False, stop=True).then_inc(gu_done, 1)

                def TA(i, u):
                    s, d = 4 * i + u, u % 2
                    eng.wait_ge(act_ready, s + 1)
                    if not early(i, 2, s):
                        eng.wait_ge(aT_ready, s - 1)
                    eng.transpose(ps[:, 4 + d, 0:P], act_[:, d], ident).then_inc(aT_done, 1)

                def DN(i, u):
                    s, d = 4 * i + u, u % 2
                    e = eng.snap(e_down, min_val=0, max_val=E - 1)
                    eng.wait_ge(aT_ready, s + 1)
                    if not early(i, 2, s):
                        eng.wait_ge(y_ready, s - 1)
                    eng.matmul(ps[:, 6 + d, 0:D], actT[:, d], wdn[:, bass.ds(e, 1), :].rearrange("p a m -> p (a m)"),
                               start=True, stop=False)
                    eng.matmul(ps[:, 6 + d, 0:D], sel[0:3 * E, bass.ds(e, 1), :].rearrange("p a m -> p (a m)"),
                               bias_b[0:3 * E, 2 * I:2 * I + D], start=False, stop=True).then_inc(dn_done, 1)

                pipeline(eng, NBLK // 4, [(2, TX), (-2, DN), (1, GU), (0, SH), (2, OW), (0, TA)],
                         [(0, OW), (0, TX), (1, TX), (0, GU), (0, SH), (1, OW)], [(2, DN), (3, SH), (3, DN)])

            @block.scalar
            def _(eng):
                def XT(i, u):
                    s, d = 4 * i + u, u % 2
                    eng.wait_ge(xT_done, s + 1)
                    if not early(i, 2, s):
                        eng.wait_ge(gu_done, s - 1)
                    eng.activation(xinT[:, d], ps[:, d, 0:D].rearrange("p (c t) -> p c t", c=DC),
                                   ACT.Copy).then_inc(xT_ready, 1)

                def SG(i, u):
                    s, d = 4 * i + u, u % 2
                    eng.wait_ge(gate_ready, s + 1)
                    if not early(i, 2, s):
                        eng.wait_ge(gs_ready, s - 1)
                    eng.activation(sig[:, d], gate[:, d], ACT.Sigmoid, scale=1.702).then_inc(sig_ready, 1)

                def AT(i, u):
                    s, d = 4 * i + u, u % 2
                    eng.wait_ge(aT_done, s + 1)
                    if not early(i, 2, s):
                        eng.wait_ge(dn_done, s - 1)
                    eng.activation(actT[:, d], ps[:, 4 + d, 0:P], ACT.Copy).then_inc(aT_ready, 1)

                pipeline(eng, NBLK // 4, [(2, XT), (1, SG), (0, AT)], [(0, XT), (1, XT), (0, SG)], [])

            @block.vector
            def _(eng):
                def GL(i, u):
                    s, d = 4 * i + u, u % 2
                    eng.wait_ge(gu_done, s + 1)
                    eng.tensor_scalar(gate[:, d], ps[:, 2 + d, 0:I], 7.0, None, ALU.min).then_inc(gate_ready, 1)
                    eng.tensor_scalar(up[:, d], ps[:, 2 + d, I:2 * I], 1.0, 8.0, ALU.add, ALU.min).then_inc(up_ready, 1)

                def GS(i, u):
                    s, d = 4 * i + u, u % 2
                    eng.wait_ge(sig_ready, s + 1)
                    eng.tensor_tensor(gate[:, d], gate[:, d], sig[:, d], ALU.mult).then_inc(gs_ready, 1)
                    eng.wait_ge(gs_ready, s + 1)
                    if not early(i, 2, s):
                        eng.wait_ge(aT_done, s - 1)
                    eng.scalar_tensor_tensor(act_[:, d], up[:, d], -6.0, gate[:, d], ALU.max,
                                             ALU.mult).then_inc(act_ready, 1)

                def YO(i, u):
                    s = 4 * i + u
                    eng.wait_ge(dn_done, s + 1)
                    if not early(i, 4, s):
                        eng.wait_ge(y_out[u], 16 * i)
                    eng.tensor_copy(yout[:, u], ps[:, 6 + u % 2, 0:D]).then_inc(y_ready, 1)

                pipeline(eng, NBLK // 4, [(1, GL), (-2, YO), (1, GS)], [(0, GL), (0, GS)], [(2, YO), (3, YO)])

        first_layer.close()

        yg = view(W0, 8192, "p (n f) -> p n f", f=D)
        gathered = [sem(f"gathered{b}") for b in range(NB)]
        s_comb = sem("combine_step")
        w1 = view(A0, 2048, "p (k m) -> p k m", k=DC)
        w2 = view(A0 + 2048, 2048, "p (k m) -> p k m", k=IC)
        o = 6144 + 2 * P
        w1q = view(o, 1024, "p (k m) -> p k m", dt=bf16, k=DC); o += 1024
        w2q = view(o, 1024, "p (k m) -> p k m", dt=bf16, k=IC); o += 1024
        wab, wcl, wsc = view(o, 2), view(o + 2, 2), view(o + 4, 2)
        wab_ready, wsum_done, s_wq = sem("wab_ready"), sem("wsum_done"), sem("ternary_step")
        normS = Norm("nS", True)
        with nc.Block() as block:
            @block.sync
            def _(eng):
                load(eng, "w1", w1, a["F_w1"])
                load(eng, "w2", w2, a["F_w2"])

            @block.tensor
            def _(eng):
                eng.wait_ge(wab_ready, 2)
                eng.matmul(ps[:, 7, 0:2], ones, wab, start=True, stop=True).then_inc(wsum_done, 1)

            @block.gpsimd
            def _(eng):
                for n in range(NB * TOPK):
                    eng.indirect_dma_start(yg[:, n, :], None, ys,
                                           bass.IndirectOffsetOnAxis(ap=slot_i[:, n:n + 1].bitcast(u32), axis=0)
                                           ).then_inc(gathered[n // TOPK], 16)

            @block.vector
            def _(eng):
                ch = Chain(eng, s_comb)
                cw_ = Chain(eng, s_wq)

                def mean_abs(k, w):
                    loaded(eng, f"w{k + 1}")
                    eng.tensor_reduce(wab[:, k:k + 1], w.rearrange("p k m -> p (k m)"), AX.X, ALU.add,
                                      apply_absolute_value=True).then_inc(wab_ready, 1)

                def scales():
                    eng.wait_ge(wsum_done, 1)
                    cw_.link(eng.tensor_scalar(wcl, ps[:, 7, 0:2], 1.0 / (D * INNER), 1e-5, ALU.mult, ALU.max))
                    cw_.link(eng.reciprocal(wsc, wcl))

                def ternary(k, w, wq):
                    cw_.link(eng.tensor_scalar(w, w, wsc[:, k:k + 1], MAGIC, ALU.mult, ALU.add))
                    cw_.link(eng.tensor_scalar(w, w, -MAGIC, -1.0, ALU.add, ALU.max))
                    cw_.mark(eng.tensor_scalar(wq, w, 1.0, None, ALU.min))

                meanwhile = {3: lambda: mean_abs(0, w1), 4: lambda: mean_abs(1, w2), 5: scales,
                             6: lambda: ternary(0, w1, w1q), 7: lambda: ternary(1, w2, w2q)}
                for b in range(NB):
                    if b in meanwhile:
                        meanwhile[b]()
                    eng.wait_ge(gathered[b], 16 * TOPK)
                    for k in range(TOPK):
                        ch.link(eng.scalar_tensor_tensor(x[:, b], yg[:, b * TOPK + k], gw[:, b, k:k + 1], x[:, b],
                                                         ALU.mult, ALU.add))
                    normS.dve_stats(eng, b)
                normS.dve_variance(eng)
                cw_.wait()

        o = W0
        xc = view(o, 4096, "p (c t) -> p c t", c=CT); o += 4096
        zs = view(o, 4096, "p (c t) -> p c t", c=CT); o += 4096
        dts = view(o, 4096, "p (c t) -> p c t", c=CT); o += 4096
        dtu = view(o, 4096, "p (c t) -> p c t", c=CT); o += 4096
        yg = view(o, 4096, "p (c t) -> p c t", c=CT); o += 4096
        room = [o + 1024 * k for k in range(4)] + [35840 + 1024 * k for k in range(7)] + [45568 + 1024 * k for k in range(5)]
        B_ = [view(r, 1024) for r in room]
        w_in = view(33792, 2048, "p (k m) -> p k m", k=DC)
        bc3 = view(43008, 512, dt=bf16)
        o = 43520
        w_bc = view(o, 384, "p (k m) -> p k m", k=CT); o += 384
        w_dt = view(o, 512, "p (k m) -> p k m", k=CT); o += 512
        w_out = view(o, 1024, "p (k m) -> p k m", k=CT); o += 1024
        vecs = view(o, 128)
        cw, cb, dtw, dtb, Dp = vecs[:, 0:16], vecs[:, 16:20], vecs[:, 20:24], vecs[:, 24:28], vecs[:, 28:32]
        nw, negA = vecs[:, 32:34], vecs[:, 34:98]
        padded = [view(room[4], 1048, "p (b t) -> p b t", b=NB), view(room[4] + 1048, 1048, "p (b t) -> p b t", b=NB)]
        conv = [B_[7], B_[8]]
        bcf, bct = B_[9], B_[10].bitcast(bf16)[:, 0:1024]
        zz, ez, eabs = [B_[0], B_[1]], [B_[11], B_[12]], [B_[2], B_[3]]
        in_done, xi_ready, z_ready = sem("in_done"), sem("xi_ready"), sem("z_ready")
        conv_ready, xc_ready, pad_ready = sem("conv_ready"), sem("xc_ready"), sem("pad_ready")
        bc_done, dt_done, bc_ready, s_split = sem("bc_done"), sem("dt_done"), sem("bc_ready"), sem("split_step")
        zz_ready, sp_ready, dt_ready, dtu_ready = sem("zz_ready"), sem("sp_ready"), sem("dt_ready"), sem("dtu_ready")
        s_actm, s_negA = sem("act_step_m"), sem("negA_step")
        t8 = "p (b t) -> p b t"

        with nc.Block() as block:
            @block.sync
            def _(eng):
                load(eng, "w_in", w_in, a["M_in"])
                load(eng, "w_bc", w_bc[:, :, :], a["M_bc"])
                load(eng, "w_bc", w_dt, a["M_dt"])
                load(eng, "vecs", vecs[:, 0:98], a["M_vec"])
                load(eng, "w_out", w_out, a["M_out"])

            @block.gpsimd
            def _(eng):
                for k in range(2):
                    eng.memset(padded[k][:, :, 0:PAD], 0.0).then_inc(pad_ready, 1)
                normS.pool(eng)
                for c in range(CT):
                    eng.wait_ge(dt_ready, c + 1)
                    eng.tensor_tensor(dtu[:, c], dts[:, c], xc[:, c], ALU.mult).then_inc(dtu_ready, 1)

            @block.tensor
            def _(eng):
                normS.pe(eng)
                loaded(eng, "w_in")
                eng.wait_ge(normS.hT_ready, 4)
                for m in range(2 * CT):
                    r = 2 * (m % 4)
                    if m >= 4:
                        eng.wait_ge(xi_ready, m - 3)
                    for half in range(2):
                        for k in range(DC):
                            t = eng.matmul(ps[:, r + half, :], w_in[:, k, m * P:(m + 1) * P],
                                           hT[:, k, half * 512:(half + 1) * 512], start=k == 0, stop=k == DC - 1)
                    t.then_inc(in_done, 1)
                loaded(eng, "w_bc")
                eng.wait_ge(xc_ready, CT)
                eng.wait_ge(z_ready, 2)
                for half in range(2):
                    for c in range(CT):
                        t = eng.matmul(ps[0:3 * E, half, :], w_bc[:, c, :], xc[:, c, half * 512:(half + 1) * 512],
                                       start=c == 0, stop=c == CT - 1)
                t.then_inc(bc_done, 1)
                for half in range(2):
                    for c in range(CT):
                        t = eng.matmul(ps[:, 2 + half, :], w_dt[:, c, :], xc[:, c, half * 512:(half + 1) * 512],
                                       start=c == 0, stop=c == CT - 1)
                t.then_inc(dt_done, 1)

            @block.scalar
            def _(eng):
                loaded(eng, "vecs")
                normS.act(eng, nw)
                for c in range(CT):
                    eng.wait_ge(in_done, c + 1)
                    if c < 2:
                        eng.wait_ge(pad_ready, c + 1)
                    else:
                        eng.wait_ge(conv_ready, c - 1)
                    r = 2 * c
                    eng.activation(padded[c % 2][:, :, PAD:], ps[:, r:r + 2, :].rearrange("p k (b t) -> p (k b) t", b=4),
                                   ACT.Copy).then_inc(xi_ready, 1)
                for c in range(CT):
                    eng.wait_ge(in_done, CT + c + 1)
                    eng.activation(zs[:, c], ps[:, 2 * c:2 * c + 2, :].rearrange("p k m -> p (k m)"),
                                   ACT.Silu).then_inc(z_ready, 1)
                    eng.wait_ge(conv_ready, c + 1)
                    eng.activation(xc[:, c], conv[c % 2], ACT.Silu).then_inc(xc_ready, 1)
                eng.activation(negA, negA, ACT.Exp).then_inc(s_negA, 1)
                for c in range(CT):
                    d = c % 2
                    eng.wait_ge(zz_ready, c + 1)
                    eng.activation(ez[d], zz[d], ACT.Abs).then_inc(s_actm, 1)
                    eng.wait_ge(s_actm, 2 * c + 1)
                    if c >= 2:
                        eng.wait_ge(dt_ready, c - 1)
                    eng.activation(eabs[d], ez[d], ACT.Exp, scale=-1.0).then_inc(s_actm, 1)
                    eng.wait_ge(s_actm, 2 * c + 2)
                    eng.activation(ez[d], eabs[d], ACT.Ln, bias=1.0).then_inc(sp_ready, 1)

            @block.vector
            def _(eng):
                ch = Chain(eng, s_split)
                normS.dve(eng, True)
                for c in range(CT):
                    d = c % 2
                    acc = conv[d].rearrange(t8, b=NB)
                    eng.wait_ge(xi_ready, c + 1)
                    if c >= 2:
                        eng.wait_ge(xc_ready, c - 1)
                    ch.link(eng.tensor_scalar(acc, padded[d][:, :, 0:P], cw[:, 4 * c:4 * c + 1], cb[:, c:c + 1],
                                              ALU.mult, ALU.add))
                    for k in range(1, KCONV):
                        t = eng.scalar_tensor_tensor(acc, padded[d][:, :, k:k + P], cw[:, 4 * c + k:4 * c + k + 1],
                                                     acc, ALU.mult, ALU.add)
                        if k < KCONV - 1:
                            ch.link(t)
                        else:
                            t.then_inc(conv_ready, 1)
                eng.wait_ge(bc_done, 1)
                ch.link(eng.tensor_copy(bcf[0:3 * E], ps[0:3 * E, 0:2, :].rearrange("p k m -> p (k m)")))
                eng.wait_ge(dt_done, 1)
                for c in range(2):
                    eng.tensor_scalar(zz[c], ps[:, 2:4, :].rearrange("p k m -> p (k m)"), dtw[:, c:c + 1],
                                      dtb[:, c:c + 1], ALU.mult, ALU.add).then_inc(zz_ready, 1)
                split3(eng, ch, bc3, bcf, bct)
                eng.wait_ge(s_negA, 1)
                ch.mark(eng.tensor_scalar(negA, negA, -1.0, None, ALU.mult))
                for c in range(CT):
                    d = c % 2
                    eng.wait_ge(sp_ready, c + 1)
                    eng.wait_ge(zz_ready, c + 1)
                    eng.scalar_tensor_tensor(dts[:, c], zz[d], 0.0, ez[d], ALU.max, ALU.add).then_inc(dt_ready, 1)
                    if c + 2 < CT:
                        eng.wait_ge(dt_ready, c + 1)
                        eng.tensor_scalar(zz[d], ps[:, 2:4, :].rearrange("p k m -> p (k m)"), dtw[:, c + 2:c + 3],
                                          dtb[:, c + 2:c + 3], ALU.mult, ALU.add).then_inc(zz_ready, 1)

        dA = [B_[k] for k in range(4)]
        dBu = [B_[4], B_[5]]
        hst = [B_[6], B_[7], B_[8], B_[9]]
        hC = [B_[10], B_[11], B_[12], B_[13]]
        Csb = [B_[14], B_[15]]

        def scan(cp):
            tag = f"scan{cp}"
            B_done, C_done, C_ready = sem(tag + "_B"), sem(tag + "_C"), sem(tag + "_C_sbuf")
            dA_ready, dBu_ready, h_ready, hC_ready = sem(tag + "_dA"), sem(tag + "_dBu"), sem(tag + "_h"), sem(tag + "_hC")
            y_done, dA_zero, y_ready = sem(tag + "_y"), sem(tag + "_dA_zero"), sem(tag + "_gated")
            rounds = ST // 2
            psB, psC = ps[:, 4:6, :].rearrange("p k m -> p (k m)"), ps[:, 6:8, :].rearrange("p k m -> p (k m)")

            with nc.Block() as block:
                @block.tensor
                def _(eng):
                    def BC(i, u):
                        if u % 2:
                            return
                        s, n = 4 * i + u, 2 * i + u // 2
                        if not early(i, 1, s):
                            eng.wait_ge(dBu_ready, s)
                        for half in range(2):
                            t = eng.matmul(ps[:, 4 + half, :], sel[0:3 * E, bass.ds(n, 1), :].rearrange("p a m -> p (a m)"),
                                           bc3[0:3 * E, half * 512:(half + 1) * 512], start=True, stop=True)
                        t.then_inc(B_done, 1)
                        if not early(i, 1, s):
                            eng.wait_ge(C_ready, n)
                        for half in range(2):
                            t = eng.matmul(ps[:, 6 + half, :],
                                           sel[0:3 * E, bass.ds(n + ST, 1), :].rearrange("p a m -> p (a m)"),
                                           bc3[0:3 * E, half * 512:(half + 1) * 512], start=True, stop=True)
                        t.then_inc(C_done, 1)

                    def Y(i, u):
                        s = 4 * i + u
                        eng.wait_ge(hC_ready, s + 1)
                        for half in range(2):
                            t = eng.matmul(ps[:, 2 * (u % 2) + half, :], ident, hC[u][:, half * 512:(half + 1) * 512],
                                           start=early(i, 2, s), stop=isinstance(i, int) and s >= 2 * ST - 2)
                        t.then_inc(y_done, 1)

                    pipeline(eng, rounds, [(2, BC), (-1, Y)], [(0, BC)], [(3, Y)])

                @block.scalar
                def _(eng):
                    def CS(i, u):
                        if u % 2:
                            return
                        n = 2 * i + u // 2
                        eng.wait_ge(C_done, n + 1)
                        if not early(i, 2, n):
                            eng.wait_ge(hC_ready, 2 * n - 2)
                        eng.activation(Csb[u // 2], psC, ACT.Copy).then_inc(C_ready, 1)

                    def DA(i, u):
                        s, n, c = 4 * i + u, 2 * i + u // 2, 2 * cp + u % 2
                        if early(i, 4, s):
                            eng.wait_ge(dA_zero, u + 1)
                        else:
                            eng.wait_ge(h_ready, s - 3)
                        eng.activation(dA[u].rearrange(t8, b=NB)[:, :, 1:P], dts[:, c].rearrange(t8, b=NB)[:, :, 1:P],
                                       ACT.Exp, scale=negA[:, bass.ds(ST * c + n, 1)]).then_inc(dA_ready, 1)

                    pipeline(eng, rounds, [(2, DA), (1, CS)], [(0, DA), (1, DA), (0, CS)], [])

                @block.vector
                def _(eng):
                    def DB(i, u):
                        s, n, c = 4 * i + u, 2 * i + u // 2, 2 * cp + u % 2
                        eng.wait_ge(B_done, n + 1)
                        if not early(i, 2, s):
                            eng.wait_ge(h_ready, s - 1)
                        eng.tensor_tensor(dBu[u % 2], dtu[:, c], psB, ALU.mult).then_inc(dBu_ready, 1)

                    def SC(i, u):
                        s = 4 * i + u
                        eng.wait_ge(dA_ready, s + 1)
                        eng.wait_ge(dBu_ready, s + 1)
                        if not early(i, 4, s):
                            eng.wait_ge(hC_ready, s - 3)
                        eng.tensor_tensor_scan(hst[u], dA[u], dBu[u % 2], 0.0, ALU.mult, ALU.add).then_inc(h_ready, 1)

                    pipeline(eng, rounds, [(1, DB), (0, SC)], [(0, DB)], [])
                    for k in range(2):
                        c = 2 * cp + k
                        eng.wait_ge(y_done, 2 * ST - 1 + k)
                        eng.scalar_tensor_tensor(yg[:, c], xc[:, c], Dp[:, c:c + 1],
                                                 ps[:, 2 * k:2 * k + 2, :].rearrange("p k m -> p (k m)"),
                                                 ALU.mult, ALU.add).then_inc(y_ready, 1)
                    for k in range(2):
                        c = 2 * cp + k
                        eng.wait_ge(y_ready, k + 1)
                        eng.tensor_tensor(yg[:, c], yg[:, c], zs[:, c], ALU.mult).then_inc(y_ready, 1)

                @block.gpsimd
                def _(eng):
                    for u in range(4):
                        eng.memset(dA[u].rearrange(t8, b=NB)[:, :, 0:1], 0.0).then_inc(dA_zero, 1)

                    def HC(i, u):
                        s, n = 4 * i + u, 2 * i + u // 2
                        eng.wait_ge(h_ready, s + 1)
                        eng.wait_ge(C_ready, n + 1)
                        if not early(i, 4, s):
                            eng.wait_ge(y_done, s - 3)
                        eng.tensor_tensor(hC[u], hst[u], Csb[u // 2], ALU.mult).then_inc(hC_ready, 1)

                    pipeline(eng, rounds, [(0, HC)], [], [])

        scan(0)
        scan(1)

        op_done, op_ready = sem("out_proj_done"), sem("out_proj_added")
        normW = Norm("nW")
        with nc.Block() as block:
            @block.tensor
            def _(eng):
                loaded(eng, "w_out")
                for b in range(NB):
                    if b >= 4:
                        eng.wait_ge(op_ready, b - 3)
                    for c in range(CT):
                        t = eng.matmul(ps[:, b % 4, 0:D], yg[:, c, b * P:(b + 1) * P], w_out[:, c, :],
                                       start=c == 0, stop=c == CT - 1)
                    t.then_inc(op_done, 1)

            @block.vector
            def _(eng):
                for b in range(NB):
                    eng.wait_ge(op_done, b + 1)
                    eng.tensor_tensor(x[:, b], x[:, b], ps[:, b % 4, 0:D], ALU.add).then_inc(op_ready, 1)
                    if b:
                        eng.wait_ge(op_ready, b)
                        normW.dve_stats(eng, b - 1)
                eng.wait_ge(op_ready, NB)
                normW.dve_stats(eng, NB - 1)
                normW.dve_variance(eng)

        TP = P + 1
        o = W0
        vT = view(o, 2048, "p (c t) -> p c t", c=DC); o += 2048
        wkv_u = view(o, 2); o += 2
        wkv_w = view(o, 2); o += 2
        names = ("kp", "wp", "op", "no", "a1", "e1", "a2", "e2", "ev", "pp", "qp", "num", "den", "tmp")
        W = {n: [view(o + NB * TP * (2 * k + c), NB * TP, "p (b t) -> p b t", b=NB) for c in range(DC)]
             for k, n in enumerate(names)}
        o += NB * TP * 2 * len(names)
        assert o <= 51104
        flat = lambda v: v.rearrange("p b t -> p (b t)")
        normF = Norm("nF")
        num_ready, den_ready, inv_ready = sem("num_ready"), sem("den_ready"), sem("inv_ready")
        s_w, w_act, w_pool = sem("wkv_step"), sem("wkv_exp"), sem("wkv_pool")
        kp_ready, pre_ready, sc_ready, yw_ready = sem("kp_ready"), sem("wkv_pre"), sem("wkv_scan"), sem("wkv_y")
        yT_done, xw_ready = sem("wkv_T_done"), sem("wkv_added")
        BIG = -1.0e38

        with nc.Block() as block:
            @block.sync
            def _(eng):
                load(eng, "vT", vT, a["ctxT"])
                load(eng, "uw", wkv_u, a["W_u"])
                load(eng, "uw", wkv_w, a["W_w"])

            @block.gpsimd
            def _(eng):
                for c in range(DC):
                    eng.memset(W["kp"][c][:, :, 0:1], BIG).then_inc(w_pool, 1)
                    for n in ("a2", "e2", "ev"):
                        eng.memset(W[n][c][:, :, 0:1], 0.0).then_inc(w_pool, 1)
                normW.pool(eng)
                loaded(eng, "vT")
                for c in range(DC):
                    v = vT[:, c].rearrange(t8, b=NB)
                    eng.wait_ge(w_act, 4 * c + 4)
                    eng.tensor_tensor(W["ev"][c][:, :, 1:], W["e2"][c][:, :, 1:], v, ALU.mult).then_inc(w_pool, 1)
                    eng.tensor_tensor(W["tmp"][c][:, :, 1:], W["e1"][c][:, :, 1:], v, ALU.mult).then_inc(w_pool, 1)

            @block.scalar
            def _(eng):
                normW.act(eng)
                eng.wait_ge(normW.hT_ready, 4)
                for c in range(DC):
                    eng.activation(W["kp"][c][:, :, 1:], hT[:, c].rearrange(t8, b=NB), ACT.Copy).then_inc(kp_ready, 1)
                for c in range(DC):
                    for k, n in enumerate(("e2", "a2", "e1", "a1")):
                        eng.wait_ge(pre_ready, 4 * c + k + 1)
                        if k == 0:
                            eng.wait_ge(w_pool, 4 * DC)
                        eng.activation(W[n][c][:, :, 1:], W[n][c][:, :, 1:], ACT.Exp).then_inc(w_act, 1)
                for c in range(DC):
                    r0 = W["tmp"][c][:, :, 1:]
                    eng.wait_ge(den_ready, c + 1)
                    eng.wait_ge(num_ready, c + 1)
                    eng.activation(r0, W["den"][c][:, :, 0:P], ACT.Ln).then_inc(inv_ready, 1)
                    eng.wait_ge(inv_ready, 2 * c + 1)
                    eng.activation(r0, r0, ACT.Exp, scale=-1.0).then_inc(inv_ready, 1)

            @block.vector
            def _(eng):
                ch = Chain(eng, s_w)
                normW.dve(eng, True)
                loaded(eng, "uw")
                for c in range(DC):
                    w = {n: W[n][c] for n in names}
                    u_, w_ = wkv_u[:, c:c + 1], wkv_w[:, c:c + 1]
                    k, o_prev, o_now = w["kp"][:, :, 1:], w["op"][:, :, 0:P], w["op"][:, :, 1:]
                    eng.wait_ge(kp_ready, c + 1)
                    eng.wait_ge(w_pool, 4 * DC)
                    ch.link(eng.tensor_scalar(w["wp"][:, :, 1:], k, 0.0, w_, ALU.mult, ALU.add))
                    ch.link(eng.memset(w["wp"][:, :, 0:1], BIG))
                    ch.link(eng.tensor_tensor_scan(flat(w["op"]), flat(w["wp"]), flat(w["kp"]), BIG, ALU.add, ALU.max))
                    eng.tensor_tensor(w["e2"][:, :, 1:], k, o_now, ALU.subtract).then_inc(pre_ready, 1)
                    eng.scalar_tensor_tensor(w["a2"][:, :, 1:], o_prev, w_, o_now, ALU.add, ALU.subtract).then_inc(pre_ready, 1)
                    ch.link(eng.scalar_tensor_tensor(w["no"][:, :, 1:], k, u_, o_prev, ALU.add, ALU.max))
                    eng.scalar_tensor_tensor(w["e1"][:, :, 1:], k, u_, w["no"][:, :, 1:], ALU.add, ALU.subtract).then_inc(pre_ready, 1)
                    eng.tensor_tensor(w["a1"][:, :, 1:], o_prev, w["no"][:, :, 1:], ALU.subtract).then_inc(pre_ready, 1)
                for c in range(DC):
                    w = {n: W[n][c] for n in names}
                    eng.wait_ge(w_act, 4 * c + 2)
                    ch.link(eng.tensor_tensor_scan(flat(w["qp"]), flat(w["a2"]), flat(w["e2"]), 0.0, ALU.mult, ALU.add))
                    eng.wait_ge(w_pool, 4 * DC + 2 * c + 1)
                    ch.link(eng.tensor_tensor_scan(flat(w["pp"]), flat(w["a2"]), flat(w["ev"]), 0.0, ALU.mult, ALU.add))
                    eng.wait_ge(w_act, 4 * c + 4)
                    num, den = w["num"][:, :, 0:P], w["den"][:, :, 0:P]
                    ch.mark(eng.tensor_tensor(num, w["a1"][:, :, 1:], w["pp"][:, :, 0:P], ALU.mult))
                    ch.link(eng.tensor_tensor(den, w["a1"][:, :, 1:], w["qp"][:, :, 0:P], ALU.mult))
                    eng.wait_ge(w_pool, 4 * DC + 2 * c + 2)
                    eng.tensor_tensor(num, num, w["tmp"][:, :, 1:], ALU.add).then_inc(num_ready, 1)
                    eng.tensor_tensor(den, den, w["e1"][:, :, 1:], ALU.add).then_inc(den_ready, 1)
                    r0, t0 = w["tmp"][:, :, 1:], w["e1"][:, :, 1:]
                    eng.wait_ge(inv_ready, 2 * c + 2)
                    eng.wait_ge(num_ready, c + 1)
                    eng.wait_ge(den_ready, c + 1)
                    ch.link(eng.tensor_tensor(t0, den, r0, ALU.mult))
                    ch.link(eng.scalar_tensor_tensor(t0, t0, -2.0, r0, ALU.add, ALU.mult))
                    eng.scalar_tensor_tensor(num, t0, -1.0, num, ALU.mult, ALU.mult).then_inc(yw_ready, 1)
                for b in range(NB):
                    eng.wait_ge(yT_done, b + 1)
                    eng.tensor_tensor(x[:, b], x[:, b], ps[:, 2 + b % 4, 0:D], ALU.add).then_inc(xw_ready, 1)
                    if b:
                        eng.wait_ge(xw_ready, b)
                        normF.dve_stats(eng, b - 1)
                eng.wait_ge(xw_ready, NB)
                normF.dve_stats(eng, NB - 1)
                normF.dve_variance(eng)

            @block.tensor
            def _(eng):
                normW.pe(eng)
                eng.wait_ge(yw_ready, DC)
                for b in range(NB):
                    if b >= 4:
                        eng.wait_ge(xw_ready, b - 3)
                    for c in range(DC):
                        t = eng.transpose(ps[:, 2 + b % 4, c * P:(c + 1) * P], W["num"][c][:, b, 0:P], ident)
                    t.then_inc(yT_done, 1)

        o = W0
        hq = view(o, 1024, "p (b f) -> p b f", dt=bf16, b=NB); o += 1024
        hqT = view(o, 256, "p (d k t) -> p d k t", dt=bf16, d=2, k=DC); o += 256
        g1 = view(o, 2048, "p (d f) -> p d f", d=2); o += 2048
        g2 = view(o, 2048, "p (d f) -> p d f", d=2); o += 2048
        gq = view(o, 1024, "p (d f) -> p d f", dt=bf16, d=2); o += 1024
        gqT = view(o, 1024, "p (d k t) -> p d k t", dt=bf16, d=2, k=IC); o += 1024
        junk = view(o, 1024); o += 1024
        tv = view(o, 64, "p (n b) -> p n b", b=NB); o += 64
        hn = view(o, 256); o += 256
        ss1, am1, r1, sc1, f1 = (tv[:, k] for k in range(5))
        tv2 = view(o, 64, "p (n b) -> p n b", b=NB); o += 64
        ss2, am2, r2, sc2, f2 = (tv2[:, k] for k in range(5))
        s_f = sem("ffn_step")
        ss1_ready, r1_ready, hq_ready = sem("ss1_ready"), sem("r1_ready"), sem("hq_ready")
        hqT_done, hqT_ready, up_done = sem("hqT_done"), sem("hqT_ready"), sem("up_done")
        g1_ready, g2_ready, ss2_ready, r2_ready, gq_ready = (sem("g1_ready"), sem("g2_ready"), sem("ss2_ready"),
                                                             sem("r2_ready"), sem("gq_ready"))
        gqT_done, gqT_ready, down_done, x_ready, stored = (sem("gqT_done"), sem("gqT_ready"), sem("down_done"),
                                                           sem("x_ready"), sem("out_stored"))

        def quant_scales(eng, ch, am, r, sc, f, w_clip):
            ch.link(eng.tensor_tensor(f, am, r, ALU.mult))
            ch.link(eng.tensor_scalar(f, f, 1e-5, 1.0 / 127.0, ALU.max, ALU.mult))
            ch.link(eng.reciprocal(sc, f))
            ch.link(eng.tensor_scalar(f, f, w_clip, None, ALU.mult))

        def quantise(eng, ch, dst, src, tmp, r, sc):
            ch.link(eng.tensor_scalar(tmp, src, r, sc, ALU.mult, ALU.mult))
            ch.link(eng.tensor_scalar(tmp, tmp, MAGIC, MAGIC + 127.0, ALU.add, ALU.min))
            return eng.tensor_scalar(dst, tmp, -MAGIC, -128.0, ALU.add, ALU.max)

        with nc.Block() as block:
            @block.sync
            def _(eng):
                for b in range(NB):
                    eng.wait_ge(x_ready, b + 1)
                    eng.dma_start(out[:, b], x[:, b]).then_inc(stored, 16)
                eng.wait_ge(stored, 16 * NB)

            @block.gpsimd
            def _(eng):
                normF.pool(eng)
                eng.wait_ge(ss1_ready, NB)
                eng.wait_ge(normF.rstd_ready, 2)
                eng.tensor_scalar(ss1, ss1, 1e-24, 1.0 / D, ALU.max, ALU.mult).then_inc(r1_ready, 1)
                eng.wait_ge(r1_ready, 1)
                eng.tensor_tensor(r1, ss1, neg_half.to_broadcast([P, NB]), ALU.pow).then_inc(r1_ready, 1)
                for b in range(NB):
                    eng.wait_ge(ss2_ready, b + 1)
                    eng.tensor_scalar(ss2[:, b:b + 1], ss2[:, b:b + 1], 1e-24, 1.0 / INNER, ALU.max, ALU.mult).then_inc(r2_ready, 1)
                    eng.wait_ge(r2_ready, 2 * b + 1)
                    eng.tensor_tensor(r2[:, b:b + 1], ss2[:, b:b + 1], neg_half, ALU.pow).then_inc(r2_ready, 1)

            @block.vector
            def _(eng):
                ch = Chain(eng, s_f)
                normF.dve(eng, True)
                eng.wait_ge(normF.h_ready, NB)
                ch.link(eng.tensor_reduce(am1, h, AX.X, ALU.max, apply_absolute_value=True))
                eng.wait_ge(r1_ready, 2)
                quant_scales(eng, ch, am1, r1, sc1, f1, wcl[:, 0:1])
                for b in range(NB):
                    quantise(eng, ch, hq[:, b], h[:, b], hn, r1[:, b:b + 1], sc1[:, b:b + 1]).then_inc(hq_ready, 1)
                    eng.wait_ge(hq_ready, b + 1)
                for b in range(NB):
                    d = b % 2
                    one = slice(b, b + 1)
                    eng.wait_ge(g2_ready, b + 1)
                    ch.link(eng.tensor_reduce(am2[:, one], g2[:, d], AX.X, ALU.max, apply_absolute_value=True))
                    eng.wait_ge(r2_ready, 2 * b + 2)
                    quant_scales(eng, ch, am2[:, one], r2[:, one], sc2[:, one], f2[:, one], wcl[:, 1:2])
                    if b >= 2:
                        eng.wait_ge(gqT_done, b - 1)
                    quantise(eng, ch, gq[:, d], g2[:, d], g2[:, d], r2[:, one], sc2[:, one]).then_inc(gq_ready, 1)
                    if b:
                        eng.wait_ge(down_done, b)
                        eng.scalar_tensor_tensor(x[:, b - 1], ps[:, 7, 0:D], f2[:, b - 1:b], x[:, b - 1], ALU.mult,
                                                 ALU.add).then_inc(x_ready, 1)
                eng.wait_ge(down_done, NB)
                eng.scalar_tensor_tensor(x[:, NB - 1], ps[:, 7, 0:D], f2[:, NB - 1:NB], x[:, NB - 1], ALU.mult,
                                         ALU.add).then_inc(x_ready, 1)

            @block.scalar
            def _(eng):
                for b in range(NB):
                    eng.wait_ge(normF.h_ready, b + 1)
                    if b:
                        eng.wait_ge(ss1_ready, b)
                    eng.activation(junk[:, 0:D], h[:, b], ACT.Square, accum_out=ss1[:, b:b + 1]).then_inc(ss1_ready, 1)
                def turned(b):
                    eng.wait_ge(hqT_done, b + 1)
                    if b >= 2:
                        eng.wait_ge(up_done, b - 1)
                    eng.activation(hqT[:, b % 2], psb[:, b % 2, 0:D].rearrange("p (k t) -> p k t", k=DC),
                                   ACT.Copy).then_inc(hqT_ready, 1)

                def inner_turned(b):
                    eng.wait_ge(gqT_done, b + 1)
                    if b >= 2:
                        eng.wait_ge(down_done, b - 1)
                    eng.activation(gqT[:, b % 2], psb[:, 6, :].rearrange("p (k t) -> p k t", k=IC),
                                   ACT.Copy).then_inc(gqT_ready, 1)

                turned(0)
                turned(1)
                for b in range(NB):
                    d = b % 2
                    eng.wait_ge(up_done, b + 1)
                    eng.activation(g1[:, d], ps[:, 2 + 2 * d:4 + 2 * d, :].rearrange("p k m -> p (k m)"), ACT.Gelu,
                                   scale=f1[:, b:b + 1]).then_inc(g1_ready, 1)
                    eng.wait_ge(g1_ready, b + 1)
                    if b >= 2:
                        eng.wait_ge(gq_ready, b - 1)
                    eng.activation(g2[:, d], g1[:, d], ACT.Gelu).then_inc(g2_ready, 1)
                    eng.wait_ge(g2_ready, b + 1)
                    eng.activation(g1[:, d], g2[:, d], ACT.Square, accum_out=ss2[:, b:b + 1]).then_inc(ss2_ready, 1)
                    if b + 2 < NB:
                        turned(b + 2)
                    if b:
                        inner_turned(b - 1)
                inner_turned(NB - 1)

            @block.tensor
            def _(eng):
                def turn(b):
                    eng.wait_ge(hq_ready, b + 1)
                    if b >= 2:
                        eng.wait_ge(hqT_ready, b - 1)
                    for k in range(DC):
                        t = eng.transpose(psb[:, b % 2, k * P:(k + 1) * P], hq[:, b, k * P:(k + 1) * P], ident_b)
                    t.then_inc(hqT_done, 1)

                def up_(b):
                    d = b % 2
                    eng.wait_ge(hqT_ready, b + 1)
                    if b >= 2:
                        eng.wait_ge(g1_ready, b - 1)
                    for half in range(2):
                        for k in range(DC):
                            t = eng.matmul(ps[:, 2 + 2 * d + half, :], hqT[:, d, k], w1q[:, k, half * 512:(half + 1) * 512],
                                           start=k == 0, stop=k == DC - 1)
                    t.then_inc(up_done, 1)

                def down(b):
                    d = b % 2
                    eng.wait_ge(gq_ready, b + 1)
                    if b:
                        eng.wait_ge(gqT_ready, b)
                    for k in range(IC):
                        t = eng.transpose(psb[:, 6, k * P:(k + 1) * P], gq[:, d, k * P:(k + 1) * P], ident_b)
                    t.then_inc(gqT_done, 1)
                    eng.wait_ge(gqT_ready, b + 1)
                    if b:
                        eng.wait_ge(x_ready, b)
                    for k in range(IC):
                        t = eng.matmul(ps[:, 7, 0:D], gqT[:, d, k], w2q[:, k, :], start=k == 0, stop=k == IC - 1)
                    t.then_inc(down_done, 1)

                turn(0)
                turn(1)
                up_(0)
                for b in range(NB):
                    if b + 1 < NB:
                        up_(b + 1)
                    if b + 2 < NB:
                        turn(b + 2)
                    if b:
                        down(b - 1)
                down(NB - 1)


def kernel(**inputs):
    import numpy as np
    import concourse.bacc as _bacc
    from concourse import mybir as _mybir
    from concourse.bass_utils import run_bass_kernel_spmd as _run

    g = {k: np.asarray(v) for k, v in inputs.items()}
    arrays = {}

    def put(name, v):
        arrays[name] = np.ascontiguousarray(v)

    def chunked(w, parts=P):
        return w.reshape(-1, parts, w.shape[-1]).transpose(1, 0, 2)

    pos = np.arange(P, dtype=np.float32)
    fA = (1.0 / np.float32(10000.0) ** (np.arange(0, R, 2, dtype=np.float32) / np.float32(R))).astype(np.float32)
    fX = (1.0 / np.float32(10000.0) ** (np.arange(R // 2, dtype=np.float32) / np.float32(R // 2))).astype(np.float32)
    idx, swap = np.arange(R) // 2, np.arange(R) ^ 1
    paired = np.arange(R).reshape(2, R // 2).T.ravel()
    sign = np.where(np.arange(R) % 2 == 0, -1.0, 1.0)
    for name, f in (("A", fA), ("X", fX)):
        ang = (pos[None, :] * f[idx][:, None]).astype(np.float32).astype(np.float64)
        c, s = np.cos(ang).astype(np.float32), (np.sin(ang) * sign[:, None]).astype(np.float32)
        one = np.ones_like(c)
        put("cos" + name, np.stack([np.concatenate([one, c]), np.concatenate([c, one])], 1))
        put("sin" + name, np.concatenate([s, s]))

    put("x", g["x"].transpose(1, 0, 2))
    put("ctxT", chunked(g["ctx_2048"].reshape(T, D).T))
    put("seg", g["itok_BxS_0_1023"].T)
    wq = g["L0_attn_w_query"].reshape(D, H, 2, R)
    put("A_qnT", wq[:, :, 0].transpose(2, 1, 0))
    pe = wq[:, :, 1].reshape(DC, P, H, R).transpose(1, 0, 2, 3)
    put("A_qr", pe.reshape(P, DC, H // 2, 2 * R))
    wkvb = g["L0_attn_wkv_b"].reshape(R, H, R + VH)
    put("A_kbT", wkvb[:, :, :R].transpose(2, 1, 0))
    vT = wkvb[:, :, R:].transpose(2, 1, 0)
    put("A_vT", np.concatenate([vT, vT], -1))
    put("A_o", g["L0_attn_out_proj_w"].reshape(H, VH, D).transpose(1, 0, 2))
    kva = chunked(g["L0_attn_wkv_a"])
    kc, kp = kva[..., :R], kva[..., R:]
    put("A_wkv", np.stack([np.concatenate([kc, kp], -1), np.concatenate([kp, kc], -1),
                           np.concatenate([kp[..., swap]] * 2, -1)], 1))
    put("A_norm", np.concatenate([g["L0_attn_kv_norm_w"]] * 2).reshape(P, 1))
    put("X_kvcT", g["L0_xattn_W_kvc"].T)
    put("X_kr2", np.concatenate([g["L0_xattn_W_kr"][:, paired], g["L0_xattn_W_kr"][:, paired[swap]]], -1))
    put("X_kvc", chunked(g["L0_xattn_W_kvc"]))
    put("X_uqT", g["L0_xattn_W_uq"].reshape(QC, H, VH).transpose(2, 1, 0))
    put("X_ukT", g["L0_xattn_W_uk"].reshape(R, H, VH).transpose(2, 1, 0))
    vT = g["L0_xattn_W_uv"].reshape(R, H, VH).transpose(2, 1, 0)
    put("X_vT", np.concatenate([vT, vT], -1))
    put("X_o", g["L0_xattn_W_o"].reshape(H, VH, D).transpose(1, 0, 2))
    qr = g["L0_xattn_W_qr"].reshape(QC, H, R)[..., paired]
    put("X_qr", qr.reshape(QC, H // 2, 2 * R))
    put("X_dq", chunked(g["L0_xattn_W_dq"]))

    gu = np.concatenate([g["L0_ffn_w_gate"], g["L0_ffn_w_up"]], -1)
    put("E_gu", gu.reshape(E, DC, P, 2 * I).transpose(2, 1, 0, 3))
    put("E_dn", g["L0_ffn_w_down"].transpose(1, 0, 2))
    put("E_gate", chunked(g["L0_ffn_gate_w"].T))
    put("E_gate_b", g["L0_ffn_gate_b"].reshape(1, E))
    bias = np.concatenate([g["L0_ffn_b_gate"], g["L0_ffn_b_up"], g["L0_ffn_b_down"]], -1)
    put("E_bias", np.concatenate([bias] * 3))

    put("M_in", chunked(g["L1_attn_in_proj_w"].T))
    xp = g["L1_attn_x_proj_w"].T
    put("M_bc", chunked(np.concatenate([xp[:, :2 * ST]] * 3, -1)))
    put("M_dt", chunked(np.repeat(xp[:, 2 * ST:], P, -1)))
    put("M_out", chunked(g["L1_attn_out_proj_w"].T))
    col = lambda v: v.reshape(-1, P).T
    put("M_vec", np.concatenate([chunked(g["L1_attn_conv_w"].reshape(DI, KCONV)).reshape(P, CT * KCONV),
                                 col(g["L1_attn_conv_b"]), col(g["L1_attn_dt_w"]), col(g["L1_attn_dt_b"]),
                                 col(g["L1_attn_D_param"]), col(g["L1_attn_norm_w"]),
                                 chunked(g["L1_attn_A_log"]).reshape(P, CT * ST)], -1))
    put("W_u", col(g["L1_xattn_u"]))
    put("W_w", col(g["L1_xattn_w"]))
    put("F_w1", chunked(g["L1_ffn_w1"].T))
    put("F_w2", chunked(g["L1_ffn_w2"].T))

    nc = _bacc.Bacc("TRN2", target_bir_lowering=False, num_devices=1)
    aps = {n: nc.dram_tensor("in_" + n, v.shape, _mybir.dt.from_np(v.dtype), kind="ExternalInput").ap()
           for n, v in arrays.items()}
    out = nc.dram_tensor("out_x", (P, NB, D), fp32, kind="ExternalOutput").ap()
    decoder(nc, aps, out)
    r = _run(nc, [{"in_" + n: v for n, v in arrays.items()}], core_ids=[0])
    return r.results[0]["out_x"].transpose(1, 0, 2)
```

```python
import concourse.bass as bass
from concourse import mybir
from contextlib import ExitStack

fp32 = mybir.dt.float32
bf16 = mybir.dt.bfloat16
i32 = mybir.dt.int32
u32 = mybir.dt.uint32
ALU = mybir.AluOpType
ACT = mybir.ActivationFunctionType
AX = mybir.AxisListType

P = 128
NB = 8
D = 256
DC = D // P
T = NB * P
H = 16
R = 64
GH = 4
NG = H // GH
QC = 96
VH = 128
E = 32
TOPK = 4
I = 128
NBLK = 64
DI = 512
CT = DI // P
ST = 16
KCONV = 4
PAD = KCONV - 1
INNER = 1024
IC = INNER // P
NEG = -1.0e30
MAGIC = 12582912.0
LN_EPS = 1e-5


class Chain:

    def __init__(self, eng, sem):
        self.eng, self.sem, self.base, self.n = eng, sem, 0, 0

    def mark(self, ins):
        ins.then_inc(self.sem, 1)
        self.n += 1

    def wait(self):
        self.eng.wait_ge(self.sem, self.base + self.n)

    def link(self, ins):
        self.mark(ins)
        self.wait()

    def enter(self, i, per):
        self.before, self.per = self.n, per
        self.base, self.n = self.n + i * per, 0

    def leave(self, rounds):
        assert self.n == self.per, (self.n, self.per)
        self.base, self.n = 0, self.before + rounds * self.per


def decoder(nc, a, out):
    ctx = ExitStack()
    with ctx:
        def sem(name):
            return nc.alloc_semaphore(name=name)

        WORDS = 53200

        arena = ctx.enter_context(nc.sbuf_tensor("arena", [P, WORDS], fp32))
        ps = ctx.enter_context(nc.psum_tensor("ps", [P, 8, 512], fp32))
        first_layer = ExitStack()
        first_layer.enter_context(nc.cleanup_on_exit())

        psb = ps[:, :, :].bitcast(bf16)

        def view(at, n, pat=None, dt=fp32, parts=P, **dims):
            assert at + n <= WORDS, (at, n)
            v = arena[0:parts, at:at + n]
            if dt is not fp32:
                v = v.bitcast(dt)
            return v.rearrange(pat, **dims) if pat else v

        x = view(0, 2048, "p (b f) -> p b f", b=NB)
        hT = view(2048, 2048, "p (c t) -> p c t", c=DC)
        h = view(4096, 2048, "p (b f) -> p b f", b=NB)
        ctxT0 = view(4096, 2048, "p (c t) -> p c t", c=DC)
        at = 6144
        ident = view(at, P); at += P
        ones = view(at, P); at += P
        maskA = view(at, P); at += P
        maskX = view(at, 1024, "p (b t) -> p b t", b=NB); at += 1024
        rope = {}
        for name in "AX":
            rope[name] = (view(at, 256, "p (e t) -> p e t", e=2), view(at + 256, P)); at += 384
        small = view(at, 256); at += 256
        tri_b = view(at, 64, dt=bf16); at += 64
        ones_b = view(at, 64, dt=bf16); at += 64
        ident_b = view(at, 64, dt=bf16); at += 64
        stats = view(at, NB * 6, "p (b k) -> p b k", b=NB); at += NB * 6
        mv = view(at, NB * 2, "p (b k) -> p b k", b=NB); at += NB * 2
        var_eps = view(at, NB); at += NB
        rstd = view(at, NB); at += NB
        both = view(at, NB); at += NB
        mean_rstd = view(at, NB); at += NB
        neg_half = view(at, 1); at += 1
        kv_norm = view(at, 1); at += 1
        zeros = view(at, 256); at += 256
        assert at <= 9216
        W0 = 9216
        A0 = W0 + 16384
        X0 = A0 + 11520
        K0 = X0 + 8704
        assert K0 + 6688 <= WORDS, K0

        layer = {}
        for name, base, kc, cw in (("A", A0, P, DC), ("X", X0, QC, 1)):
            o = base
            L = {"kc": kc, "chunks": cw}
            L["wq"] = view(o, cw * 2048, "p (c h m) -> p c h m", c=cw, h=H); o += cw * 2048
            L["wvo"] = view(o, 2048, "p (h m) -> p h m", h=H // 2); o += 2048
            L["wkv"] = view(o, 768, "p (e c m) -> p e c m", e=3, c=DC); o += 768
            L["key"] = view(o, 2048, "p (e t) -> p e t", e=2); o += 2048
            L["kvn"] = view(o, 512, "p (b r) -> p b r", b=NB); o += 512
            if name == "X":
                L["wdq"] = view(o, 192, "p (c m) -> p c m", c=DC); o += 192
                L["qc"] = view(o, 1024); o += 1024
            L["cos"], L["sin"] = rope[name]
            layer[name] = L
            assert o <= (X0 if name == "A" else K0), o
        gate_w = view(A0 + 11008, 64, "p (c e) -> p c e", c=DC)
        gate_b = view(A0 + 11072, 32)
        rawA = W0
        wqnT = view(rawA, 4096, "p (h f) -> p h f", h=H)
        kbT = view(rawA + 4096, 1024, "p (h r) -> p h r", h=H)
        wvT = {"A": view(rawA + 5120, 2048, "p (h r) -> p h r", h=H)}
        wo = {"A": view(rawA + 7168, 4096, "p (h f) -> p h f", h=H)}
        rawX = rawA + 11264
        wuqT = view(rawX, 1536, "p (h q) -> p h q", h=H)
        wukT = view(rawX + 1536, 1024, "p (h r) -> p h r", h=H)
        wvT["X"] = view(rawX + 2560, 2048, "p (h r) -> p h r", h=H)
        wkvcT = view(rawX + 4608, 256)
        wkr2 = view(rawX + 4864, 128)
        wo["X"] = view(K0, 4096, "p (h f) -> p h f", h=H)
        o = K0 + 4096
        keytmp = view(o, 1024, "p (e t) -> p e t", e=2)
        o = K0
        q = view(o, 2048, "p (d h s) -> p d h s", d=NG, h=GH); o += 2048
        qsw = view(o, 512, "p (d h s) -> p d h s", d=2, h=GH // 2); o += 512
        sm = view(o, 1024, "p (d h t) -> p d h t", d=2, h=GH); o += 1024
        pr = view(o, 1024, "p (d h t) -> p d h t", d=2, h=GH); o += 1024
        prT = view(o, 1024, "p (d m) -> p d m", d=2); o += 1024
        uT = view(o, 512, "p (d h s) -> p d h s", d=2, h=GH // 2); o += 512
        un = view(o, 512, "p (d h r) -> p d h r", d=2, h=GH); o += 512
        mx = view(o, 8, "p (d h) -> p d h", d=2); o += 8
        negm = view(o, 8, "p (d h) -> p d h", d=2); o += 8
        rsum = view(o, 8, "p (d h) -> p d h", d=2); o += 8
        rinv = view(o, 8, "p (d h) -> p d h", d=2); o += 8
        assert o <= WORDS

        class Norm:

            def __init__(self, tag, rms=False, parts=((0, NB),)):
                self.rms, self.parts = rms, parts
                if rms:
                    self.rms_step = sem(tag + "_rms_step")
                self.stats_in = sem(tag + "_stats_in")
                self.var_ready = sem(tag + "_var_ready")
                self.rstd_ready = sem(tag + "_rstd_ready")
                self.h_ready = sem(tag + "_h_ready")
                self.hT_done = sem(tag + "_hT_done")
                self.hT_ready = sem(tag + "_hT_ready")

            def dve_stats(self, eng, b):
                eng.bn_stats(stats[:, b, :], x[:, b, :]).then_inc(self.stats_in, 1)

            def dve_variance(self, eng, k=0):
                eng.wait_ge(self.stats_in, self.parts[k][1])
                for b in range(*self.parts[k]):
                    eng.bn_aggr(mv[:, b, :], stats[:, b, :]).then_inc(self.var_ready, 1)

            def dve_begin(self, eng, k):
                for b in range(*self.parts[k]):
                    self.dve_stats(eng, b)
                self.dve_variance(eng, k)

            def dve_end(self, eng, k):
                eng.wait_ge(self.rstd_ready, 2 * k + 2)
                eng.wait_ge(self.var_ready, self.parts[k][1])
                for b in range(*self.parts[k]):
                    eng.tensor_scalar(h[:, b, :], x[:, b, :], mv[:, b, 0:1], rstd[:, b:b + 1], ALU.subtract,
                                      ALU.mult).then_inc(self.h_ready, 1)

            def dve(self, eng, begun=False):
                if not begun:
                    for b in range(NB):
                        self.dve_stats(eng, b)
                    self.dve_variance(eng)
                if not self.rms:
                    for k in range(len(self.parts)):
                        self.dve_end(eng, k)
                    return
                eng.wait_ge(self.rstd_ready, 2)
                eng.wait_ge(self.var_ready, NB)
                eng.wait_ge(self.rms_step, 5)
                for b in range(NB):
                    eng.tensor_scalar(h[:, b, :], x[:, b, :], mv[:, b, 0:1], both[:, b:b + 1], ALU.subtract,
                                      ALU.mult).then_inc(self.h_ready, 1)
                eng.wait_ge(self.rms_step, 7)
                for b in range(NB):
                    eng.tensor_scalar(x[:, b, :], x[:, b, :], rstd[:, b:b + 1], mean_rstd[:, b:b + 1], ALU.mult,
                                      ALU.subtract)

            def pool(self, eng):
                for k, (first, end) in enumerate(self.parts):
                    some = slice(first, end)
                    eng.wait_ge(self.var_ready, end)
                    eng.tensor_scalar(var_eps[:, some], mv[:, some, 1], LN_EPS, None, ALU.add).then_inc(self.rstd_ready, 1)
                    eng.wait_ge(self.rstd_ready, 2 * k + 1)
                    eng.tensor_tensor(rstd[:, some], var_eps[:, some], neg_half.to_broadcast([P, end - first]),
                                      ALU.pow).then_inc(self.rstd_ready, 1)
                if self.rms:
                    mean = mv[:, :, 0]
                    self.pool_mean_square(eng, self.rms_step, both)
                    eng.tensor_scalar(both, both, LN_EPS, None, ALU.add).then_inc(self.rms_step, 1)
                    eng.wait_ge(self.rms_step, 3)
                    eng.tensor_tensor(both, both, neg_half.to_broadcast([P, NB]), ALU.pow).then_inc(self.rms_step, 1)
                    eng.wait_ge(self.rms_step, 4)
                    eng.tensor_tensor(both, both, rstd, ALU.mult).then_inc(self.rms_step, 1)
                    eng.tensor_tensor(mean_rstd, mean, rstd, ALU.mult).then_inc(self.rms_step, 1)
                    eng.wait_ge(self.rms_step, 6)
                    eng.tensor_scalar(rstd, rstd, 1.0, None, ALU.add).then_inc(self.rms_step, 1)

            def pool_mean_square(self, eng, step, dst):
                eng.wait_ge(self.rstd_ready, 2 * len(self.parts))
                eng.tensor_tensor(dst, rstd, rstd, ALU.mult).then_inc(step, 1)
                eng.wait_ge(step, 1)
                eng.tensor_tensor(dst, dst, mv[:, :, 1], ALU.mult).then_inc(step, 1)
                eng.wait_ge(step, 2)

            def pe(self, eng, tiles=(0, NB)):
                for b in range(*tiles):
                    eng.wait_ge(self.h_ready, b + 1)
                    if b % 2 == 0 and b >= 4:
                        eng.wait_ge(self.hT_ready, b // 2 - 1)
                    for c in range(DC):
                        at = (b % 2) * D + c * P
                        t = eng.transpose(ps[:, (b // 2) % 2, at:at + P], h[:, b, c * P:(c + 1) * P], ident)
                    if b % 2:
                        t.then_inc(self.hT_done, 1)

            def act(self, eng, scale=None, pairs=(0, NB // 2), into=None):
                for k in range(*pairs):
                    eng.wait_ge(self.hT_done, k + 1)
                    src = ps[:, k % 2, :].rearrange("p (b c t) -> p c b t", b=2, c=DC)
                    dst = hT[:, :, k * D:(k + 1) * D].rearrange("p c (b t) -> p c b t", b=2)
                    if into:
                        for c in range(DC):
                            t = eng.activation(into[c][:, 2 * k:2 * k + 2, 1:], src[:, c], ACT.Copy)
                        t.then_inc(self.hT_ready, 1)
                    elif scale is None:
                        eng.activation(dst, src, ACT.Copy).then_inc(self.hT_ready, 1)
                    else:
                        for c in range(DC):
                            t = eng.activation(dst[:, c], src[:, c], ACT.Copy, scale=scale[:, c:c + 1])
                        t.then_inc(self.hT_ready, 1)

        class Keys:

            def __init__(self, tag):
                self.raw = sem(tag + "_key_raw")
                self.scaled = sem(tag + "_key_scaled")
                self.rotated = sem(tag + "_key_rotated")
                self.sq = sem(tag + "_key_sq")
                self.ssq = sem(tag + "_key_ssq")
                self.inv = sem(tag + "_key_inv")
                self.tok_done = sem(tag + "_kvn_done")
                self.tok = sem(tag + "_kvn")

        def pe_key_raw(eng, L, K, src, half):
            if half:
                eng.wait_ge(K.scaled, 3)
            for e in range(3):
                for c in range(DC):
                    t = eng.matmul(ps[:, 5 + e, :], L["wkv"][:, e, c, :], src[:, c, half * 512:half * 512 + 512],
                                   start=c == 0, stop=c == DC - 1)
            t.then_inc(K.raw, 1)

        def pe_key_ssq(eng, K, half):
            eng.wait_ge(K.sq, half + 1)
            eng.matmul(ps[:, 4, :], ones[0:R, :], keytmp[0:R, 1, :], start=True, stop=True).then_inc(K.ssq, 1)

        def pe_key_tokens(eng, L, K):
            eng.wait_ge(K.rotated, 2)
            for b in range(NB):
                t = eng.transpose(ps[:, 4, b * R:(b + 1) * R], L["key"][0:R, 0, b * P:(b + 1) * P], ident[0:R, 0:R])
            t.then_inc(K.tok_done, 1)

        def dve_keys(eng, ch, L, K, rms):
            for half in range(2):
                ts = slice(half * 512, half * 512 + 512)
                t4 = "p (b t) -> p b t"
                eng.wait_ge(K.raw, half + 1)
                for e in range(2):
                    tab = L["cos"][:, e, :].unsqueeze(1).to_broadcast([P, 4, P])
                    eng.tensor_tensor(L["key"][:, e, ts].rearrange(t4, b=4), ps[:, 5 + e, :].rearrange(t4, b=4),
                                      tab, ALU.mult).then_inc(K.scaled, 1)
                tab = L["sin"].unsqueeze(1).to_broadcast([P, 4, P])
                eng.tensor_tensor(keytmp[:, 0, :].rearrange(t4, b=4), ps[:, 7, :].rearrange(t4, b=4),
                                  tab, ALU.mult).then_inc(K.scaled, 1)
                eng.wait_ge(K.scaled, 3 * half + 3)
                ch.mark(eng.tensor_tensor(L["key"][R:P, 0, ts], L["key"][R:P, 0, ts], keytmp[R:P, 0, :], ALU.add))
                last = eng.tensor_tensor(L["key"][0:R, 1, ts], L["key"][0:R, 1, ts], keytmp[0:R, 0, :], ALU.add)
                if rms:
                    ch.mark(last)
                    eng.wait_ge(K.ssq, half + 1)
                    eng.tensor_scalar(keytmp[:, 1, :], ps[:, 4, :], 1.0 / R, 1e-6, ALU.mult, ALU.add).then_inc(K.inv, 1)
                    eng.wait_ge(K.inv, 3 * half + 2)
                    eng.reciprocal(keytmp[:, 1, :], keytmp[:, 1, :]).then_inc(K.inv, 1)
                    eng.wait_ge(K.inv, 3 * half + 3)
                    ch.mark(eng.scalar_tensor_tensor(L["key"][0:R, 0, ts], L["key"][0:R, 0, ts], kv_norm[0:R, :],
                                                     keytmp[0:R, 1, :], ALU.mult, ALU.mult))
                    last = eng.scalar_tensor_tensor(L["key"][R:P, 1, ts], L["key"][R:P, 1, ts], kv_norm[R:P, :],
                                                    keytmp[R:P, 1, :], ALU.mult, ALU.mult)
                ch.wait()
                last.then_inc(K.rotated, 1)
                eng.wait_ge(K.rotated, half + 1)

        def act_key_rms(eng, K, half):
            eng.wait_ge(K.scaled, 3 * half + 1)
            if half:
                eng.wait_ge(K.rotated, 1)
            eng.activation(keytmp[0:R, 1, :], ps[0:R, 5, :], ACT.Square).then_inc(K.sq, 1)
            eng.wait_ge(K.inv, 3 * half + 1)
            eng.activation(keytmp[:, 1, :], keytmp[:, 1, :], ACT.Sqrt).then_inc(K.inv, 1)

        def act_key_tokens(eng, L, K):
            eng.wait_ge(K.tok_done, 1)
            eng.activation(L["kvn"], ps[:, 4, :].rearrange("p (b r) -> p b r", b=NB), ACT.Copy).then_inc(K.tok, 1)

        loads = {}

        def load(eng, name, dst, src):
            if name not in loads:
                loads[name] = [sem("ld_" + name), 0]
            loads[name][1] += 16
            eng.dma_start(dst, src).then_inc(loads[name][0], 16)

        def loaded(eng, *names):
            for n in names:
                eng.wait_ge(loads[n][0], loads[n][1])

        s_const = sem("const_step")
        s_seg = sem("mask_step")
        kr_done, kr_ready = sem("kr_done"), sem("kr_ready")
        absX_done, absX_ready = sem("absX_done"), sem("absX_ready")
        absA_done, absA_ready = sem("absA_done"), sem("absA_ready")
        vo_done, vo_even, vo_odd = sem("vo_done"), sem("vo_even"), sem("vo_odd")
        s_zero = sem("zeros_ready")
        keysX, keysA = Keys("X"), Keys("A")
        normA = Norm("nA")
        s_ch1 = sem("dve_chain1")
        LA, LX = layer["A"], layer["X"]
        NCONST = 6

        with nc.Block() as block:
            @block.sync
            def _(eng):
                load(eng, "krX", wkvcT[0:R, :], a["X_kvcT"])
                load(eng, "krX", wkr2[0:R, :], a["X_kr2"])
                load(eng, "ctx", ctxT0, a["ctxT"])
                load(eng, "kvX", LX["wkv"][:, 0, :, 0:R], a["X_kvc"])
                load(eng, "kvX", LX["wkv"][:, 1, :, R:P], a["X_kvc"])
                load(eng, "ropeX", rope["X"][0], a["cosX"])
                load(eng, "ropeX", rope["X"][1], a["sinX"])
                load(eng, "x", x, a["x"])
                load(eng, "absX", wuqT, a["X_uqT"])
                load(eng, "absX", wukT, a["X_ukT"])
                load(eng, "ropeA", rope["A"][0], a["cosA"])
                load(eng, "ropeA", rope["A"][1], a["sinA"])
                load(eng, "kvA", LA["wkv"], a["A_wkv"])
                load(eng, "kvA", kv_norm, a["A_norm"])
                load(eng, "absA", wqnT[0:R], a["A_qnT"])
                load(eng, "absA", kbT[0:R], a["A_kbT"])
                load(eng, "voX", wvT["X"], a["X_vT"])
                load(eng, "voX", wo["X"], a["X_o"])
                load(eng, "voA", wvT["A"], a["A_vT"])
                load(eng, "voA", wo["A"], a["A_o"])
                load(eng, "qX", LX["wq"][0:QC, 0].rearrange("p (q e) m -> p q (e m)", e=2)[:, :, R:P + R], a["X_qr"])
                load(eng, "qX", LX["wdq"], a["X_dq"])
                for c in range(DC):
                    load(eng, "qA", LA["wq"][:, c].rearrange("p (q e) m -> p q (e m)", e=2)[:, :, R:P + R],
                         a["A_qr"][:, c])
                load(eng, "seg", small[:, 0:NB].bitcast(i32), a["seg"])
                load(eng, "gate", gate_w, a["E_gate"])
                load(eng, "gate", gate_b[0:1, :], a["E_gate_b"])

            @block.gpsimd
            def _(eng):
                eng.memset(zeros, 0.0).then_inc(s_zero, 1)
                eng.memset(ident, 0.0).then_inc(s_const, 1)
                eng.memset(maskA, 0.0).then_inc(s_const, 1)
                eng.memset(ones, 1.0).then_inc(s_const, 1)
                eng.memset(neg_half, -0.5).then_inc(s_const, 1)
                eng.wait_ge(s_const, 2)
                eng.affine_select(out=ident, in_=ident, compare_op=ALU.not_equal, fill=1.0, base=0,
                                  pattern=[[-1, P]], channel_multiplier=1).then_inc(s_const, 1)
                eng.affine_select(out=maskA, in_=maskA, compare_op=ALU.is_ge, fill=NEG, base=0,
                                  pattern=[[-1, P]], channel_multiplier=1).then_inc(s_const, 1)
                eng.memset(small[:, 128:256], 1.0).then_inc(s_const, 1)
                eng.wait_ge(s_const, 7)
                eng.affine_select(out=small[:, 128:256], in_=small[:, 128:256], compare_op=ALU.is_gt, fill=0.0, base=0,
                                  pattern=[[1, P]], channel_multiplier=-1).then_inc(s_const, 1)
                eng.wait_ge(s_const, 8)
                eng.tensor_copy(tri_b, small[:, 128:256]).then_inc(s_const, 1)
                eng.tensor_copy(ones_b, ones).then_inc(s_const, 1)
                eng.tensor_copy(ident_b, ident).then_inc(s_const, 1)
                eng.iota(maskX[:, :, :], pattern=[[0, NB], [1, P]], base=0, channel_multiplier=0,
                         allow_small_or_imprecise_dtypes=True).then_inc(s_const, 1)
                normA.pool(eng)

            @block.vector
            def _(eng):
                ch = Chain(eng, s_ch1)
                eng.wait_ge(kr_done, 1)
                src = ps[:, 0, 0:256].rearrange("p (c m) -> p c m", c=DC)
                for k, dst in enumerate((LX["wkv"][:, 0, :, R:P], LX["wkv"][:, 1, :, 0:R],
                                         LX["wkv"][:, 2, :, 0:R], LX["wkv"][:, 2, :, R:P])):
                    eng.tensor_copy(dst, src[:, :, R * (k // 2):R * (k // 2) + R]).then_inc(kr_ready, 1)
                loaded(eng, "ropeX")
                dve_keys(eng, ch, LX, keysX, False)
                eng.wait_ge(keysX.raw, 2)
                loaded(eng, "x")
                normA.dve(eng)
                loaded(eng, "kvA", "ropeA")
                dve_keys(eng, ch, LA, keysA, True)
                loaded(eng, "seg")
                eng.wait_ge(s_const, 12)
                eng.tensor_copy(small[:, 16:16 + NB], small[:, 0:NB].bitcast(i32)).then_inc(s_seg, 1)
                eng.wait_ge(s_seg, 1)
                for b in range(NB):
                    eng.tensor_scalar(maskX[:, b, :], maskX[:, b, :], small[:, 16 + b:17 + b], None,
                                      ALU.subtract).then_inc(s_seg, 1)
                flat = maskX.rearrange("p b t -> p (b t)")
                late = view(rawA, 1024)
                eng.wait_ge(s_seg, 1 + NB)
                eng.wait_ge(absA_done, 4)
                eng.tensor_scalar(late, flat, 0.0, NEG, ALU.is_gt, ALU.mult).then_inc(s_seg, 1)
                eng.wait_ge(s_seg, 2 + NB)
                eng.tensor_scalar(flat, flat, -8.0, NEG, ALU.is_lt, ALU.mult).then_inc(s_seg, 1)
                eng.wait_ge(s_seg, 3 + NB)
                eng.tensor_tensor(flat, flat, late, ALU.add).then_inc(s_seg, 1)
                for n in range(H):
                    L, p = (LX, n) if n < 8 else (LA, n - 8)
                    eng.wait_ge(vo_done, n + 1)
                    eng.tensor_copy(L["wvo"][R:P, p, :], ps[R:P, 2 + n % 2, D:2 * D]).then_inc(vo_odd, 1)

            @block.scalar
            def _(eng):
                act_key_tokens(eng, LX, keysX)
                for g in range(2):
                    eng.wait_ge(absX_done, g + 1)
                    for e in range(2):
                        dst = LX["wq"][0:QC, 0, 8 * g:8 * g + 8].rearrange("p (q e) m -> p q (e m)", e=2)
                        src = ps[0:QC, 2 + g, :].rearrange("p (q e r) -> p q e r", q=4, e=2)
                        t = eng.activation(dst[:, :, 192 * e:192 * e + R], src[:, :, e], ACT.Copy)
                    t.then_inc(absX_ready, 1)
                normA.act(eng)
                for k in range(4):
                    c, g = k // 2, k % 2
                    if k < 2:
                        act_key_rms(eng, keysA, k)
                    eng.wait_ge(absA_done, k + 1)
                    for e in range(2):
                        dst = LA["wq"][:, c, 8 * g:8 * g + 8].rearrange("p (q e) m -> p q (e m)", e=2)
                        src = ps[:, k % 2, :].rearrange("p (q e r) -> p q e r", q=4, e=2)
                        t = eng.activation(dst[:, :, 192 * e:192 * e + R], src[:, :, e], ACT.Copy)
                    t.then_inc(absA_ready, 1)
                act_key_tokens(eng, LA, keysA)
                for n in range(H):
                    L, p = (LX, n) if n < 8 else (LA, n - 8)
                    eng.wait_ge(vo_done, n + 1)
                    eng.activation(L["wvo"][0:R, p, :], ps[0:R, 2 + n % 2, 0:D], ACT.Copy).then_inc(vo_even, 1)

            @block.tensor
            def _(eng):
                loaded(eng, "krX")
                for c in range(DC):
                    t = eng.matmul(ps[:, 0, c * P:(c + 1) * P], wkvcT[0:R, c * P:(c + 1) * P], wkr2[0:R, :],
                                   start=True, stop=True)
                t.then_inc(kr_done, 1)
                loaded(eng, "ctx", "kvX")
                eng.wait_ge(kr_ready, 4)
                eng.wait_ge(s_const, 6)
                for half in range(2):
                    pe_key_raw(eng, LX, keysX, ctxT0, half)
                loaded(eng, "absX")
                for g in range(2):
                    for j in range(8):
                        hd = 8 * g + j
                        t = eng.matmul(ps[0:QC, 2 + g, j * R:(j + 1) * R], wuqT[:, hd, :], wukT[:, hd, :],
                                       start=True, stop=True)
                    t.then_inc(absX_done, 1)
                pe_key_tokens(eng, LX, keysX)
                normA.pe(eng)
                eng.wait_ge(normA.hT_ready, 4)
                loaded(eng, "kvA")
                pe_key_raw(eng, LA, keysA, hT, 0)
                loaded(eng, "absA")
                for k in range(4):
                    c, g = k // 2, k % 2
                    if k >= 2:
                        eng.wait_ge(absA_ready, k - 1)
                    for j in range(8):
                        hd = 8 * g + j
                        t = eng.matmul(ps[:, k % 2, j * R:(j + 1) * R], wqnT[0:R, hd, c * P:(c + 1) * P],
                                       kbT[0:R, hd, :], start=True, stop=True)
                    t.then_inc(absA_done, 1)
                    if k < 2:
                        if k == 0:
                            eng.wait_ge(keysX.tok, 1)
                        pe_key_ssq(eng, keysA, k)
                    if k == 0:
                        pe_key_raw(eng, LA, keysA, hT, 1)
                pe_key_tokens(eng, LA, keysA)
                loaded(eng, "voX", "voA")
                for n in range(H):
                    name, p = ("X", n) if n < 8 else ("A", n - 8)
                    if n < 2:
                        eng.wait_ge(absX_ready, n + 1)
                    else:
                        eng.wait_ge(vo_even, n - 1)
                        eng.wait_ge(vo_odd, n - 1)
                    for e in range(2):
                        t = eng.matmul(ps[:, 2 + n % 2, e * D:(e + 1) * D], wvT[name][:, 2 * p + e, :],
                                       wo[name][:, 2 * p + e, :], start=True, stop=True)
                    t.then_inc(vo_done, 1)
                loaded(eng, "qA", "qX", "gate")

        def near(b, g, off):
            g += off
            return (b - 1, g + 4) if g < 0 else (b + 1, g - 4) if g > 3 else (b, g)

        def four(stages, b, first, last):
            for g in range(4):
                for off, emit in stages:
                    if not ((first and g + off < 0) or (last and g + off > 3)):
                        emit(*near(b, g, off))

        def pipeline(eng, rounds, stages, ahead, behind):
            for off, emit in ahead:
                emit(0, off)
            four(stages, 0, True, False)
            with eng.Fori(1, rounds - 1) as b:
                four(stages, b, False, False)
            four(stages, rounds - 1, False, True)
            for off, emit in behind:
                emit(rounds - 1, off)

        swap_pairs = [k ^ 1 for k in range(32)]

        def attention(tag, L, scale, mask, per_batch_mask, prefetch, norm, tail_pe, tail_act):
            q_done, q_scaled, q_roped = sem(tag + "_q_done"), sem(tag + "_q_scaled"), sem(tag + "_q_roped")
            sc_done, masked, negm_ready = sem(tag + "_scores_done"), sem(tag + "_masked"), sem(tag + "_negm_ready")
            mx_ready = sem(tag + "_mx_ready")
            exp_done, rinv_ready = sem(tag + "_exp_done"), sem(tag + "_rinv_ready")
            prT_done, prT_ready = sem(tag + "_prT_done"), sem(tag + "_prT_ready")
            u_done, un_ready, v_done = sem(tag + "_u_done"), sem(tag + "_un_ready"), sem(tag + "_v_done")
            uT_ready, o_done, res_ready = sem(tag + "_uT_ready"), sem(tag + "_o_done"), sem(tag + "_res_ready")
            rotation = sem(tag + "_rotation")
            kc, chunks = L["kc"], L["chunks"]
            psQ, psS, psT, psU, psV, psO = 0, 2, 4, 5, 6, 7
            src = hT if chunks == DC else L["qc"].unsqueeze(1)

            def tok(b):
                return bass.ds(b * P, P)

            def pe_queries(eng, b, g):
                d, s = g % 2, 4 * b + g
                if not (isinstance(b, int) and s < 2):
                    eng.wait_ge(q_scaled, s - 1)
                for j in range(GH):
                    for c in range(chunks):
                        t = eng.matmul(ps[:, psQ + d, j * P:(j + 1) * P], L["wq"][0:kc, c, GH * g + j, :],
                                       src[0:kc, c, tok(b)], start=c == 0, stop=c == chunks - 1)
                t.then_inc(q_done, 1)

            def pe_scores(eng, b, g):
                d, s = g % 2, 4 * b + g
                eng.wait_ge(q_roped, s + 1)
                if not (isinstance(b, int) and s < 2):
                    eng.wait_ge(masked, s - 1)
                for j in range(GH):
                    t = eng.matmul(ps[:, psS + d, j * P:(j + 1) * P], q[:, g, j, :],
                                   L["key"][:, j % 2, tok(b)], start=True, stop=True)
                t.then_inc(sc_done, 1)

            def pe_transpose(eng, b, g):
                d, s = g % 2, 4 * b + g
                eng.wait_ge(exp_done, s + 1)
                if not (isinstance(b, int) and s < 1):
                    eng.wait_ge(prT_ready, s)
                for j in range(GH):
                    t = eng.transpose(ps[:, psT, j * P:(j + 1) * P], pr[:, d, j, :], ident)
                t.then_inc(prT_done, 1)

            def pe_values(eng, b, g):
                d, s = g % 2, 4 * b + g
                eng.wait_ge(prT_ready, s + 1)
                if not (isinstance(b, int) and s < 1):
                    eng.wait_ge(un_ready, s)
                for j in range(GH):
                    t = eng.matmul(ps[:, psU, j * R:(j + 1) * R], prT[:, d, j * P:(j + 1) * P],
                                   L["kvn"][:, bass.ds(b, 1), :].rearrange("p a r -> p (a r)"), start=True, stop=True)
                t.then_inc(u_done, 1)

            def pe_turn(eng, b, g):
                d, s = g % 2, 4 * b + g
                eng.wait_ge(un_ready, s + 1)
                if not (isinstance(b, int) and s < 1):
                    eng.wait_ge(uT_ready, s)
                for j in range(GH // 2):
                    t = eng.transpose(ps[:, psV, j * P:(j + 1) * P],
                                      un[:, d, 2 * j:2 * j + 2].rearrange("p h r -> p (h r)"), ident)
                t.then_inc(v_done, 1)

            def pe_output(eng, b, g):
                d, s = g % 2, 4 * b + g
                eng.wait_ge(uT_ready, s + 1)
                if g == 0 and not (isinstance(b, int) and b < 1):
                    eng.wait_ge(res_ready, b)
                for j in range(GH // 2):
                    t = eng.matmul(ps[:, psO, 0:D], uT[:, d, j, :], L["wvo"][:, GH // 2 * g + j, :],
                                   start=g == 0 and j == 0, stop=g == NG - 1 and j == GH // 2 - 1)
                t.then_inc(o_done, 1)

            def dve_queries(eng, b, g):
                d, s = g % 2, 4 * b + g
                eng.wait_ge(q_done, s + 1)
                if not (isinstance(b, int) and s < 2):
                    eng.wait_ge(q_roped, s - 1)
                if not (isinstance(b, int) and s < NG):
                    eng.wait_ge(sc_done, s - 3)
                pq = ps[:, psQ + d, :].rearrange("p (a e s) -> p a e s", a=2, e=2)
                eng.tensor_tensor(q[:, g].rearrange("p (a e) s -> p a e s", e=2), pq,
                                  L["cos"].unsqueeze(1).to_broadcast([P, 2, 2, P]), ALU.mult)
                eng.stream_shuffle(qsw[R:P, d], pq[R:P, :, 0], swap_pairs)
                eng.stream_shuffle(qsw[0:R, d], pq[0:R, :, 1], swap_pairs).then_inc(q_scaled, 1)

            def pool_rotate(eng, b, g):
                d, s = g % 2, 4 * b + g
                eng.wait_ge(q_scaled, s + 1)
                eng.tensor_tensor(qsw[:, d], qsw[:, d], L["sin"].unsqueeze(1).to_broadcast([P, 2, P]),
                                  ALU.mult).then_inc(rotation, 1)
                eng.wait_ge(rotation, 2 * s + 1)
                qe = q[:, g].rearrange("p (a e) s -> p a e s", e=2)
                eng.tensor_tensor(qe[R:P, :, 0], qe[R:P, :, 0], qsw[R:P, d], ALU.add).then_inc(rotation, 1)
                eng.wait_ge(rotation, 2 * s + 2)
                eng.tensor_tensor(qe[0:R, :, 1], qe[0:R, :, 1], qsw[0:R, d], ALU.add).then_inc(q_roped, 1)

            def dve_softmax(eng, b, g):
                d, s = g % 2, 4 * b + g
                eng.wait_ge(sc_done, s + 1)
                if not (isinstance(b, int) and s < 2):
                    eng.wait_ge(exp_done, s - 1)
                m = mask[:, b, :] if per_batch_mask and isinstance(b, int) else (
                    mask[:, bass.ds(b, 1), :].rearrange("p a t -> p (a t)") if per_batch_mask else mask)
                eng.tensor_tensor(sm[:, d], ps[:, psS + d, :].rearrange("p (h t) -> p h t", h=GH),
                                  m.unsqueeze(1).to_broadcast([P, GH, P]), ALU.add).then_inc(masked, 1)
                eng.wait_ge(masked, s + 1)
                eng.tensor_reduce(mx[:, d], sm[:, d], AX.X, ALU.max).then_inc(mx_ready, 1)
                eng.wait_ge(mx_ready, s + 1)
                eng.tensor_scalar(negm[:, d], mx[:, d], -scale, None, ALU.mult).then_inc(negm_ready, 1)

            def dve_inverse(eng, b, g):
                d, s = g % 2, 4 * b + g
                eng.wait_ge(exp_done, s + 1)
                eng.reciprocal(rinv[:, d], rsum[:, d]).then_inc(rinv_ready, 1)

            def dve_normalise(eng, b, g):
                d, s = g % 2, 4 * b + g
                eng.wait_ge(rinv_ready, s + 1)
                eng.wait_ge(u_done, s + 1)
                if not (isinstance(b, int) and s < 2):
                    eng.wait_ge(v_done, s - 1)
                eng.tensor_tensor(un[:, d], ps[:, psU, 0:GH * R].rearrange("p (h r) -> p h r", h=GH),
                                  rinv[:, d].unsqueeze(2).to_broadcast([P, GH, R]), ALU.mult).then_inc(un_ready, 1)

            def dve_residual(eng, b):
                eng.wait_ge(o_done, 4 * b + 4)
                eng.tensor_tensor(x[:, bass.ds(b, 1), :].rearrange("p a f -> p (a f)"),
                                  x[:, bass.ds(b, 1), :].rearrange("p a f -> p (a f)"),
                                  ps[:, psO, 0:D], ALU.add).then_inc(res_ready, 1)

            def act_exp(eng, b, g):
                d, s = g % 2, 4 * b + g
                eng.wait_ge(negm_ready, s + 1)
                if not (isinstance(b, int) and s < 2):
                    eng.wait_ge(prT_done, s - 1)
                    eng.wait_ge(rinv_ready, s - 1)
                for j in range(GH):
                    t = eng.activation(pr[:, d, j, :], sm[:, d, j, :], ACT.Exp, bias=negm[:, d, j:j + 1],
                                       scale=scale, accum_out=rsum[:, d, j:j + 1])
                t.then_inc(exp_done, 1)

            def act_probs(eng, b, g):
                d, s = g % 2, 4 * b + g
                eng.wait_ge(prT_done, s + 1)
                if not (isinstance(b, int) and s < 2):
                    eng.wait_ge(u_done, s - 1)
                eng.activation(prT[:, d, :], ps[:, psT, :], ACT.Copy).then_inc(prT_ready, 1)

            def act_values(eng, b, g):
                d, s = g % 2, 4 * b + g
                eng.wait_ge(v_done, s + 1)
                if not (isinstance(b, int) and s < 2):
                    eng.wait_ge(o_done, s - 1)
                eng.activation(uT[:, d], ps[:, psV, 0:D].rearrange("p (a s) -> p a s", a=2),
                               ACT.Copy).then_inc(uT_ready, 1)

            with nc.Block() as block:
                @block.tensor
                def _(eng):
                    Q = lambda b, g: pe_queries(eng, b, g)
                    S = lambda b, g: pe_scores(eng, b, g)
                    TR = lambda b, g: pe_transpose(eng, b, g)
                    U = lambda b, g: pe_values(eng, b, g)
                    O = lambda b, g: pe_output(eng, b, g)
                    V = lambda b, g: pe_turn(eng, b, g)
                    pipeline(eng, NB, [(-3, O), (-2, V), (-1, U), (1, S), (3, Q), (0, TR)],
                             [(0, Q), (1, Q), (2, Q), (0, S)], [(1, O), (2, V), (3, U), (2, O), (3, V), (3, O)])
                    for k in range(2):
                        norm.pe(eng, (4 * k, 4 * k + 4))
                        tail_pe(eng, k)

                @block.vector
                def _(eng):
                    SF = lambda b, g: dve_softmax(eng, b, g)
                    QS = lambda b, g: dve_queries(eng, b, g)
                    IN = lambda b, g: dve_inverse(eng, b, g)
                    UN = lambda b, g: dve_normalise(eng, b, g)

                    def early_stats(eng):
                        eng.wait_ge(res_ready, NB - 1)
                        norm.dve_begin(eng, 0)

                    def RS(b, g):
                        if g == NG - 1:
                            dve_residual(eng, b)
                    pipeline(eng, NB, [(-3, RS), (-1, IN), (-1, UN), (1, SF), (3, QS)],
                             [(0, QS), (1, QS), (2, QS), (0, SF)],
                             [(3, lambda b, g: early_stats(eng)), (3, IN), (3, UN), (3, lambda b, g: norm.dve_end(eng, 0)), (3, RS)])
                    eng.wait_ge(res_ready, NB)
                    norm.dve_begin(eng, 1)
                    norm.dve_end(eng, 1)

                @block.scalar
                def _(eng):
                    EX = lambda b, g: act_exp(eng, b, g)
                    PT = lambda b, g: act_probs(eng, b, g)
                    UT = lambda b, g: act_values(eng, b, g)
                    pipeline(eng, NB, [(-2, UT), (0, PT), (1, EX)], [(0, EX)], [(2, UT), (3, UT)])
                    eng.wait_ge(q_done, 4 * NB)
                    for k in range(2):
                        norm.act(eng, pairs=(2 * k, 2 * k + 2))
                        tail_act(eng, k)

                @block.gpsimd
                def _(eng):
                    RO = lambda b, g: pool_rotate(eng, b, g)
                    pipeline(eng, NB, [(3, RO)], [(0, RO), (1, RO), (2, RO)], [])
                    norm.pool(eng)

                @block.sync
                def _(eng):
                    prefetch(eng)

        wgu = view(W0, 16384, "p (c e m) -> p c e m", c=DC, e=E)
        hd = nc.dram_tensor("tokens", (T, D), fp32).ap()
        ys = nc.dram_tensor("expert_out", (NBLK * P, D), fp32).ap()

        def prefetch_up(eng):
            for e in range(0, E, 8):
                for c in range(DC):
                    load(eng, "wgu", wgu[:, c, e:e + 8], a["E_gu"][:, c, e:e + 8])

        qc_done, qc_ready = sem("qc_done"), sem("qc_ready")
        EARLY = ((0, NB - 1), (NB - 1, NB))
        normX, normM = Norm("nX", parts=EARLY), Norm("nM", parts=EARLY)

        def pe_latents(eng, k):
            eng.wait_ge(normX.hT_ready, 2 * k + 2)
            for c in range(DC):
                t = eng.matmul(ps[0:QC, 2 + k, :], LX["wdq"][:, c, :], hT[:, c, k * 512:(k + 1) * 512],
                               start=c == 0, stop=c == DC - 1)
            t.then_inc(qc_done, 1)

        def act_latents(eng, k):
            eng.wait_ge(qc_done, k + 1)
            eng.activation(LX["qc"][0:QC, k * 512:(k + 1) * 512], ps[0:QC, 2 + k, :], ACT.Copy).then_inc(qc_ready, 1)

        attention("A", LA, float(P) ** -0.5, maskA, False, prefetch_up, normX, pe_latents, act_latents)

        wdn = view(A0, 8192, "p (e m) -> p e m", e=E)
        sel = view(51104, 2048, "p (e m) -> p e m", dt=bf16, e=E)
        bias_f = view(A0 + 10240, 512)
        bias_b = view(A0 + 10752, 256, dt=bf16)

        def prefetch_down(eng):
            load(eng, "wdn", wdn, a["E_dn"])
            load(eng, "bias", bias_f[0:3 * E, :], a["E_bias"])
            for b in range(NB):
                eng.wait_ge(normM.h_ready, b + 1)
                eng.dma_start(hd[b * P:(b + 1) * P], h[:, b]).then_inc(tokens_out, 16)

        lg_done = sem("logits_done")
        tokens_out = sem("tokens_out")

        def pe_logits(eng, k):
            for b in range(4 * k, 4 * k + 4):
                eng.wait_ge(normM.hT_ready, b // 2 + 1)
                dst = ps[:, 2 + k, (b % 4) * E:(b % 4 + 1) * E]
                for c in range(DC):
                    eng.matmul(dst, hT[:, c, b * P:(b + 1) * P], gate_w[:, c, :], start=c == 0, stop=False)
                t = eng.matmul(dst, ones[0:1, :], gate_b[0:1, :], start=False, stop=True)
            t.then_inc(lg_done, 1)

        attention("X", LX, float(VH + R) ** -0.5, maskX, True, prefetch_down, normM, pe_logits, lambda eng, k: None)

        o = X0
        top = view(o, 64, "p (b k) -> p b k", b=NB); o += 64
        topi = view(o, 64, "p (b k) -> p b k", dt=u32, b=NB); o += 64
        idxf = view(o, 32, "p (b k) -> p b k", b=NB); o += 32
        gw = view(o, 32, "p (b k) -> p b k", b=NB); o += 32
        gsum = view(o, NB); o += NB
        iotaE = view(o, E); o += E
        iotaJ = view(o, NBLK); o += NBLK
        pick = view(o, 1024, "p (n e) -> p n e", e=E); o += 1024
        prod = view(o, 1024, "p (n e) -> p n e", e=E); o += 1024
        memb, cum, keep = (view(o + 288 * k, 288, "p (e b) -> p e b", e=E) for k in range(3)); o += 3 * 288
        memb_b = view(o, 128, dt=bf16); o += 128
        cum_b = view(o, 144, dt=bf16); o += 144
        nblk = view(o, E); o += E
        incl = view(o, E); o += E
        base = view(o, E); o += E
        place = view(o, 256, "p (b e) -> p b e", b=NB); o += 256
        slot = view(o, 32); o += 32
        slot_i = view(o, 32, dt=i32); o += 32
        cmp = view(o, E); o += E
        owner = view(o, 1); o += 1
        owner_i = view(o, NBLK, dt=i32); o += NBLK
        biastmp = view(o, 256, dt=bf16); o += 256
        assert o <= K0
        o = K0
        at_pos = view(o, 2048, "p (m t) -> p m t", dt=bf16, m=NB * TOPK); o += 2048
        at_blk = view(o, 1024, "p (m j) -> p m j", dt=bf16, m=NB * TOPK); o += 1024
        id_blk = view(o, 2048, "p (e m j) -> p e m j", dt=bf16, e=2, m=NB * TOPK); o += 2048
        tok_lo = view(o, NBLK); o += NBLK
        blk = view(o, 32); o += 32
        assert o <= 51104
        tok_i = small[:, 0:NBLK + 1].bitcast(i32)
        iotaT, iotaP = small[:, 64:65], small[:, 128:256]
        tok_u = small[:, 68:72].bitcast(i32)
        s_iota, s_sel = sem("iota_ready"), sem("sel_ready")
        pos_done = sem("positions_done")
        s_route, w_exp = sem("route_step"), sem("gate_exp")
        memb_ready, slot_ready, owner_ready = sem("memb_ready"), sem("slot_ready"), sem("owner_ready")
        gw_ready, s_top = sem("gate_weights_ready"), sem("top_step")
        neg_top = sem("neg_top")
        map_in, map_done, map_ready = sem("map_in"), sem("map_done"), sem("map_ready")

        SPLIT_STEPS = 6

        def split3(eng, ch, dst, src, tmp):
            n = 3 * E
            ch.link(eng.tensor_copy(dst[0:n], src[0:n]))
            ch.link(eng.tensor_tensor(src[0:n], src[0:n], dst[0:n], ALU.subtract))
            ch.mark(eng.tensor_copy(dst[E:2 * E], src[E:2 * E]))
            ch.link(eng.tensor_copy(tmp[0:n], src[0:n]))
            ch.link(eng.tensor_tensor(src[2 * E:n], src[2 * E:n], tmp[2 * E:n], ALU.subtract))
            ch.link(eng.tensor_copy(dst[2 * E:n], src[2 * E:n]))

        with nc.Block() as block:
            @block.gpsimd
            def _(eng):
                eng.iota(iotaE, pattern=[[1, E]], base=0, channel_multiplier=0,
                         allow_small_or_imprecise_dtypes=True).then_inc(s_iota, 1)
                eng.iota(iotaJ, pattern=[[1, NBLK]], base=0, channel_multiplier=0,
                         allow_small_or_imprecise_dtypes=True).then_inc(s_iota, 1)
                eng.iota(iotaP, pattern=[[1, P]], base=0, channel_multiplier=0,
                         allow_small_or_imprecise_dtypes=True).then_inc(s_iota, 1)
                eng.iota(iotaT, pattern=[[0, 1]], base=0, channel_multiplier=1,
                         allow_small_or_imprecise_dtypes=True).then_inc(s_iota, 1)
                eng.memset(memb, 0.0).then_inc(s_iota, 1)
                eng.memset(keep, 1.0).then_inc(s_sel, 1)
                eng.wait_ge(s_sel, 1)
                eng.memset(keep[:, :, 0:1], 0.0).then_inc(s_iota, 1)
                eng.memset(sel[0:3 * E], 0.0).then_inc(s_sel, 1)
                for m in range(3):
                    eng.wait_ge(s_sel, m + 2)
                    eng.affine_select(out=sel[0:3 * E], in_=sel[0:3 * E], compare_op=ALU.not_equal, fill=1.0,
                                      base=-E * m, pattern=[[-1, E], [0, P]], channel_multiplier=1).then_inc(s_sel, 1)
                eng.wait_ge(tokens_out, 16 * NB)

            @block.vector
            def _(eng):
                ch = Chain(eng, s_route)
                def in_psum(b):
                    return ps[:, 2 + b // 4, (b % 4) * E:(b % 4 + 1) * E]

                for half in range(2):
                    eng.wait_ge(lg_done, half + 1)
                    for b in range(4 * half, 4 * half + 4):
                        eng.max(top[:, b], in_psum(b)).then_inc(s_top, 1)
                for b in range(NB):
                    eng.wait_ge(s_top, b + 1)
                    eng.max_index(topi[:, b], top[:, b], in_psum(b)).then_inc(s_top, 1)
                eng.wait_ge(s_top, 2 * NB)
                ch.mark(eng.tensor_copy(idxf, topi[:, :, 0:TOPK]))
                eng.tensor_tensor(gw, top[:, :, 0:TOPK], top[:, :, 0:1].to_broadcast([P, NB, TOPK]),
                                  ALU.subtract).then_inc(neg_top, 1)
                ch.wait()
                eng.wait_ge(s_iota, 6)
                pk = "p (b k) e -> p b k e"
                ch.link(eng.tensor_tensor(pick, idxf.rearrange("p b k -> p (b k)").unsqueeze(2).to_broadcast([P, 32, E]),
                                          iotaE.unsqueeze(1).to_broadcast([P, 32, E]), ALU.is_equal))
                ch.link(eng.tensor_reduce(memb[:, :, 1:].rearrange("p e b -> p b e"),
                                          pick.rearrange("p (b k) e -> p b e k", b=NB), AX.X, ALU.add))
                eng.tensor_copy(memb_b.rearrange("p (b e) -> p b e", b=NB),
                                memb[:, :, 1:].rearrange("p e b -> p b e")).then_inc(memb_ready, 1)
                ch.link(eng.tensor_tensor_scan(cum.rearrange("p e b -> p (e b)"), keep.rearrange("p e b -> p (e b)"),
                                               memb.rearrange("p e b -> p (e b)"), 0.0, ALU.mult, ALU.add))
                eng.tensor_copy(cum_b.rearrange("p (b e) -> p b e", b=NB + 1),
                                cum.rearrange("p e b -> p b e")).then_inc(memb_ready, 1)
                eng.wait_ge(pos_done, 1)
                ch.link(eng.tensor_scalar(nblk, ps[:, 4, 0:E], 1.0 / P, (P - 1.0) / P - 0.5 + 1.0 / 256, ALU.mult, ALU.add))
                ch.link(eng.tensor_scalar(nblk, nblk, MAGIC, None, ALU.add))
                ch.link(eng.tensor_scalar(nblk, nblk, -MAGIC, None, ALU.add))
                ch.link(eng.tensor_tensor_scan(incl, ones[:, 0:E], nblk, 0.0, ALU.mult, ALU.add))
                ch.link(eng.tensor_tensor(base, incl, nblk, ALU.subtract))
                ch.link(eng.scalar_tensor_tensor(place, base.unsqueeze(1).to_broadcast([P, NB, E]), float(P),
                                                 ps[:, 5, 0:256].rearrange("p (b e) -> p b e", b=NB), ALU.mult, ALU.add))
                ch.link(eng.tensor_tensor(prod.rearrange(pk, b=NB), pick.rearrange(pk, b=NB),
                                          place.unsqueeze(2).to_broadcast([P, NB, TOPK, E]), ALU.mult))
                ch.link(eng.tensor_reduce(slot, prod, AX.X, ALU.add))
                eng.tensor_copy(slot_i, slot).then_inc(slot_ready, 1)
                ch.link(eng.tensor_scalar(blk, slot, 1.0 / P, 1.0 / 256 - 0.5, ALU.mult, ALU.add))
                ch.link(eng.tensor_scalar(blk, blk, MAGIC, None, ALU.add))
                ch.link(eng.tensor_scalar(blk, blk, -MAGIC, None, ALU.add))
                ch.link(eng.scalar_tensor_tensor(slot, blk, -float(P), slot, ALU.mult, ALU.add))
                ch.mark(eng.tensor_tensor(at_blk, blk.unsqueeze(2).to_broadcast([P, NB * TOPK, NBLK]),
                                          iotaJ.unsqueeze(1).to_broadcast([P, NB * TOPK, NBLK]), ALU.is_equal))
                ch.wait()
                eng.tensor_scalar(id_blk[:, 0], at_blk, iotaT, None, ALU.mult).then_inc(map_in, 1)
                for b in range(NB):
                    ns = slice(b * TOPK, (b + 1) * TOPK)
                    eng.tensor_scalar(id_blk[:, 1, ns], at_blk[:, ns], float(b), None, ALU.mult).then_inc(map_in, 1)
                for k in range(4):
                    ns = slice(8 * k, 8 * k + 8)
                    eng.tensor_tensor(at_pos[:, ns], slot[:, ns].unsqueeze(2).to_broadcast([P, 8, P]),
                                      iotaP.unsqueeze(1).to_broadcast([P, 8, P]), ALU.is_equal).then_inc(map_in, 1)
                ch.link(eng.tensor_scalar(cmp, incl, iotaT, None, ALU.is_le))
                ch.link(eng.tensor_reduce(owner, cmp, AX.X, ALU.add))
                eng.tensor_scalar(owner, owner, E - 1.0, None, ALU.min).then_inc(owner_ready, 1)
                eng.wait_ge(w_exp, 1)
                ch.link(eng.tensor_reduce(gsum, gw, AX.X, ALU.add))
                ch.link(eng.reciprocal(gsum, gsum))
                eng.tensor_tensor(gw, gw, gsum.unsqueeze(2).to_broadcast([P, NB, TOPK]), ALU.mult).then_inc(gw_ready, 1)
                eng.wait_ge(map_done, 2)
                eng.tensor_copy(owner_i[0:1, :], ps[0:1, 7, 0:NBLK]).then_inc(map_ready, 1)
                ch.link(eng.tensor_copy(tok_lo, ps[:, 6, 0:NBLK]))
                eng.scalar_tensor_tensor(tok_i[:, 0:NBLK], ps[:, 6, NBLK:2 * NBLK], float(P), tok_lo, ALU.mult,
                                         ALU.add).then_inc(map_ready, 1)
                eng.wait_ge(map_ready, 2)

            @block.scalar
            def _(eng):
                eng.wait_ge(neg_top, 1)
                eng.activation(gw, gw, ACT.Exp).then_inc(w_exp, 1)

            @block.tensor
            def _(eng):
                eng.wait_ge(memb_ready, 2)
                eng.matmul(ps[:, 4, 0:E], ones_b, cum_b[:, NB * E:(NB + 1) * E], start=True, stop=True)
                eng.matmul(ps[:, 5, 0:256], ones_b, cum_b[:, 0:256], start=True, stop=False)
                eng.matmul(ps[:, 5, 0:256], tri_b, memb_b, start=False, stop=True).then_inc(pos_done, 1)
                for n in range(NB * TOPK):
                    if n % 8 == 0:
                        eng.wait_ge(map_in, 1 + NB + n // 8 + 1)
                    t = eng.matmul(ps[:, 6, 0:2 * NBLK], at_pos[:, n], id_blk[:, :, n],
                                   start=n == 0, stop=n == NB * TOPK - 1)
                t.then_inc(map_done, 1)
                eng.wait_ge(owner_ready, 1)
                eng.matmul(ps[0:1, 7, 0:NBLK], owner, ident[:, 0:NBLK], start=True, stop=True).then_inc(map_done, 1)

        o = K0
        xin = view(o, 1024, "p (u f) -> p u f", u=4); o += 1024
        xinT = view(o, 512, "p (d c t) -> p d c t", d=2, c=DC); o += 512
        gate = view(o, 256, "p (d m) -> p d m", d=2); o += 256
        sig = view(o, 256, "p (d m) -> p d m", d=2); o += 256
        up = view(o, 256, "p (d m) -> p d m", d=2); o += 256
        act_ = view(o, 256, "p (d m) -> p d m", d=2); o += 256
        actT = view(o, 256, "p (d m) -> p d m", d=2); o += 256
        yout = view(o, 1024, "p (u f) -> p u f", u=4); o += 1024
        x_in = [sem(f"block_in{u}") for u in range(4)]
        bias_step = sem("bias_step")
        tok_ready = sem("block_tokens")
        y_out = [sem(f"block_out{u}") for u in range(4)]
        xT_done, xT_ready, gu_done, gate_ready = sem("xT_done"), sem("xT_ready"), sem("gu_done"), sem("gate_ready")
        up_ready, sig_ready, gs_ready, act_ready = sem("up_ready"), sem("sig_ready"), sem("gs_ready"), sem("act_ready")
        aT_done, aT_ready, dn_done, y_ready = sem("aT_done"), sem("aT_ready"), sem("dn_done"), sem("y_ready")

        def early(b, n, s):
            return isinstance(b, int) and s < n

        with nc.Block() as block:
            @block.gpsimd
            def _(eng):
                def LD(i, u):
                    s, (i1, v) = 4 * i + u, near(i, u, 1)
                    if not early(i1, 4, s + 1):
                        eng.wait_ge(x_in[v], 16 * i1)
                    if not early(i, 4, s):
                        eng.wait_ge(xT_done, s - 3)
                    eng.wait_ge(tok_ready, s + 1)
                    eng.tensor_copy(tok_u[:, v:v + 1], tok_i[:, bass.ds(s + 1, 1)]).then_inc(tok_ready, 1)
                    eng.indirect_dma_start(xin[:, u], None, hd,
                                           bass.IndirectOffsetOnAxis(ap=tok_u[:, u:u + 1].bitcast(u32), axis=0)
                                           ).then_inc(x_in[u], 16)

                eng.tensor_copy(tok_u[:, 0:1], tok_i[:, 0:1]).then_inc(tok_ready, 1)
                pipeline(eng, NBLK // 4, [(4, LD)], [(u, LD) for u in range(4)], [])

            @block.sync
            def _(eng):
                def SR(i, u):
                    s = 4 * i + u
                    eng.wait_ge(y_ready, s + 1)
                    eng.dma_start(ys[bass.ds(s * P, P), :], yout[:, u]).then_inc(y_out[u], 16)

                pipeline(eng, NBLK // 4, [(-3, SR)], [], [(u, SR) for u in range(1, 4)])
                for u in range(4):
                    eng.wait_ge(y_out[u], 16 * (NBLK // 4))

            @block.tensor
            def _(eng):
                loaded(eng, "wgu", "wdn")

                def TX(i, u):
                    s, d = 4 * i + u, u % 2
                    eng.wait_ge(x_in[u], 16 * i + 16)
                    if not early(i, 2, s):
                        eng.wait_ge(xT_ready, s - 1)
                    for c in range(DC):
                        t = eng.transpose(ps[:, d, c * P:(c + 1) * P], xin[:, u, c * P:(c + 1) * P], ident)
                    t.then_inc(xT_done, 1)

                e_up, e_mid, e_low, e_down = (eng.alloc_register(n) for n in ("e_up", "e_mid", "e_low", "e_down"))

                def OW(i, u):
                    eng.reg_load(e_up, owner_i[0:1, bass.ds(4 * i + u, 1)])

                def SH(i, u):
                    eng.reg_mov(e_down, e_low)
                    eng.reg_mov(e_low, e_mid)
                    eng.reg_mov(e_mid, e_up)

                eng.reg_mov(e_mid, 0)
                eng.reg_mov(e_low, 0)

                def GU(i, u):
                    s, d = 4 * i + u, u % 2
                    e = eng.snap(e_up, min_val=0, max_val=E - 1)
                    eng.wait_ge(xT_ready, s + 1)
                    if not early(i, 2, s):
                        eng.wait_ge(gate_ready, s - 1)
                        eng.wait_ge(up_ready, s - 1)
                    for c in range(DC):
                        eng.matmul(ps[:, 2 + d, 0:2 * I], xinT[:, d, c, :],
                                   wgu[:, c, bass.ds(e, 1), :].rearrange("p a m -> p (a m)"), start=c == 0, stop=False)
                    eng.matmul(ps[:, 2 + d, 0:2 * I], sel[0:3 * E, bass.ds(e, 1), :].rearrange("p a m -> p (a m)"),
                               bias_b[0:3 * E, 0:2 * I], start=False, stop=True).then_inc(gu_done, 1)

                def TA(i, u):
                    s, d = 4 * i + u, u % 2
                    eng.wait_ge(act_ready, s + 1)
                    if not early(i, 2, s):
                        eng.wait_ge(aT_ready, s - 1)
                    eng.transpose(ps[:, 4 + d, 0:P], act_[:, d], ident).then_inc(aT_done, 1)

                def DN(i, u):
                    s, d = 4 * i + u, u % 2
                    e = eng.snap(e_down, min_val=0, max_val=E - 1)
                    eng.wait_ge(aT_ready, s + 1)
                    if not early(i, 2, s):
                        eng.wait_ge(y_ready, s - 1)
                    eng.matmul(ps[:, 6 + d, 0:D], actT[:, d], wdn[:, bass.ds(e, 1), :].rearrange("p a m -> p (a m)"),
                               start=True, stop=False)
                    eng.matmul(ps[:, 6 + d, 0:D], sel[0:3 * E, bass.ds(e, 1), :].rearrange("p a m -> p (a m)"),
                               bias_b[0:3 * E, 2 * I:2 * I + D], start=False, stop=True).then_inc(dn_done, 1)

                eng.wait_ge(bias_step, SPLIT_STEPS)
                pipeline(eng, NBLK // 4, [(2, TX), (-2, DN), (1, GU), (0, SH), (2, OW), (0, TA)],
                         [(0, OW), (0, TX), (1, TX), (0, GU), (0, SH), (1, OW)], [(2, DN), (3, SH), (3, DN)])

            @block.scalar
            def _(eng):
                def XT(i, u):
                    s, d = 4 * i + u, u % 2
                    eng.wait_ge(xT_done, s + 1)
                    if not early(i, 2, s):
                        eng.wait_ge(gu_done, s - 1)
                    eng.activation(xinT[:, d], ps[:, d, 0:D].rearrange("p (c t) -> p c t", c=DC),
                                   ACT.Copy).then_inc(xT_ready, 1)

                def SG(i, u):
                    s, d = 4 * i + u, u % 2
                    eng.wait_ge(gate_ready, s + 1)
                    if not early(i, 2, s):
                        eng.wait_ge(gs_ready, s - 1)
                    eng.activation(sig[:, d], gate[:, d], ACT.Sigmoid, scale=1.702).then_inc(sig_ready, 1)

                def AT(i, u):
                    s, d = 4 * i + u, u % 2
                    eng.wait_ge(aT_done, s + 1)
                    if not early(i, 2, s):
                        eng.wait_ge(dn_done, s - 1)
                    eng.activation(actT[:, d], ps[:, 4 + d, 0:P], ACT.Copy).then_inc(aT_ready, 1)

                pipeline(eng, NBLK // 4, [(2, XT), (1, SG), (0, AT)], [(0, XT), (1, XT), (0, SG)], [])

            @block.vector
            def _(eng):
                ch = Chain(eng, bias_step)
                loaded(eng, "bias")
                split3(eng, ch, bias_b, bias_f, biastmp)

                def GL(i, u):
                    s, d = 4 * i + u, u % 2
                    eng.wait_ge(gu_done, s + 1)
                    eng.tensor_scalar(gate[:, d], ps[:, 2 + d, 0:I], 7.0, None, ALU.min).then_inc(gate_ready, 1)
                    eng.tensor_scalar(up[:, d], ps[:, 2 + d, I:2 * I], 1.0, 8.0, ALU.add, ALU.min).then_inc(up_ready, 1)

                def GS(i, u):
                    s, d = 4 * i + u, u % 2
                    eng.wait_ge(sig_ready, s + 1)
                    eng.tensor_tensor(gate[:, d], gate[:, d], sig[:, d], ALU.mult).then_inc(gs_ready, 1)
                    eng.wait_ge(gs_ready, s + 1)
                    if not early(i, 2, s):
                        eng.wait_ge(aT_done, s - 1)
                    eng.scalar_tensor_tensor(act_[:, d], up[:, d], -6.0, gate[:, d], ALU.max,
                                             ALU.mult).then_inc(act_ready, 1)

                def YO(i, u):
                    s = 4 * i + u
                    eng.wait_ge(dn_done, s + 1)
                    if not early(i, 4, s):
                        eng.wait_ge(y_out[u], 16 * i)
                    eng.tensor_copy(yout[:, u], ps[:, 6 + u % 2, 0:D]).then_inc(y_ready, 1)

                pipeline(eng, NBLK // 4, [(1, GL), (-2, YO), (1, GS)], [(0, GL), (0, GS)], [(2, YO), (3, YO)])

        first_layer.close()

        yg = view(W0, 8192, "p (n f) -> p n f", f=D)
        gathered = [sem(f"gathered{b}") for b in range(NB)]
        s_comb = sem("combine_step")
        w1 = view(A0, 2048, "p (k m) -> p k m", k=DC)
        w2 = view(A0 + 2048, 2048, "p (k m) -> p k m", k=IC)
        o = 6144 + 2 * P
        w1q = view(o, 1024, "p (k m) -> p k m", dt=bf16, k=DC); o += 1024
        w2q = view(o, 1024, "p (k m) -> p k m", dt=bf16, k=IC); o += 1024
        wab, wcl, wsc = view(o, 2), view(o + 2, 2), view(o + 4, 2)
        wab_ready, wsum_done, s_wq = sem("wab_ready"), sem("wsum_done"), sem("ternary_step")
        normS = Norm("nS", True)
        with nc.Block() as block:
            @block.sync
            def _(eng):
                load(eng, "w1", w1, a["F_w1"])
                load(eng, "w2", w2, a["F_w2"])

            @block.tensor
            def _(eng):
                eng.wait_ge(wab_ready, 2)
                eng.matmul(ps[:, 7, 0:2], ones, wab, start=True, stop=True).then_inc(wsum_done, 1)

            @block.gpsimd
            def _(eng):
                for n in range(NB * TOPK):
                    eng.indirect_dma_start(yg[:, n, :], None, ys,
                                           bass.IndirectOffsetOnAxis(ap=slot_i[:, n:n + 1].bitcast(u32), axis=0)
                                           ).then_inc(gathered[n // TOPK], 16)

            @block.vector
            def _(eng):
                ch = Chain(eng, s_comb)
                cw_ = Chain(eng, s_wq)

                def mean_abs(k, w):
                    loaded(eng, f"w{k + 1}")
                    eng.tensor_reduce(wab[:, k:k + 1], w.rearrange("p k m -> p (k m)"), AX.X, ALU.add,
                                      apply_absolute_value=True).then_inc(wab_ready, 1)

                def scales():
                    eng.wait_ge(wsum_done, 1)
                    cw_.link(eng.tensor_scalar(wcl, ps[:, 7, 0:2], 1.0 / (D * INNER), 1e-5, ALU.mult, ALU.max))
                    cw_.link(eng.reciprocal(wsc, wcl))

                def ternary(k, w, wq):
                    cw_.link(eng.tensor_scalar(w, w, wsc[:, k:k + 1], MAGIC, ALU.mult, ALU.add))
                    cw_.link(eng.tensor_scalar(w, w, -MAGIC, -1.0, ALU.add, ALU.max))
                    cw_.mark(eng.tensor_scalar(wq, w, 1.0, None, ALU.min))

                meanwhile = {3: lambda: mean_abs(0, w1), 4: lambda: mean_abs(1, w2), 5: scales,
                             6: lambda: ternary(0, w1, w1q), 7: lambda: ternary(1, w2, w2q)}
                for b in range(NB):
                    if b in meanwhile:
                        meanwhile[b]()
                    eng.wait_ge(gathered[b], 16 * TOPK)
                    for k in range(TOPK):
                        ch.link(eng.scalar_tensor_tensor(x[:, b], yg[:, b * TOPK + k], gw[:, b, k:k + 1], x[:, b],
                                                         ALU.mult, ALU.add))
                    normS.dve_stats(eng, b)
                normS.dve_variance(eng)
                cw_.wait()

        o = W0
        xc = view(o, 4096, "p (c t) -> p c t", c=CT); o += 4096
        zs = view(o, 4096, "p (c t) -> p c t", c=CT); o += 4096
        dts = view(o, 4096, "p (c t) -> p c t", c=CT); o += 4096
        dtu = view(o, 4096, "p (c t) -> p c t", c=CT); o += 4096
        yg = view(o, 4096, "p (c t) -> p c t", c=CT); o += 4096
        room = [o + 1024 * k for k in range(4)] + [35840 + 1024 * k for k in range(7)] + [45568 + 1024 * k for k in range(5)]
        B_ = [view(r, 1024) for r in room]
        w_in = view(33792, 2048, "p (k m) -> p k m", k=DC)
        bc3 = view(43008, 512, dt=bf16)
        o = 43520
        w_bc = view(o, 384, "p (k m) -> p k m", k=CT); o += 384
        w_dt = view(o, 512, "p (k m) -> p k m", k=CT); o += 512
        w_out = view(o, 1024, "p (k m) -> p k m", k=CT); o += 1024
        vecs = view(o, 128)
        cw, cb, dtw, dtb, Dp = vecs[:, 0:16], vecs[:, 16:20], vecs[:, 20:24], vecs[:, 24:28], vecs[:, 28:32]
        nw, negA = vecs[:, 32:34], vecs[:, 34:98]
        padded = [view(room[4], 1048, "p (b t) -> p b t", b=NB), view(room[4] + 1048, 1048, "p (b t) -> p b t", b=NB)]
        conv = [B_[7], B_[8]]
        bcf, bct = B_[9], B_[10].bitcast(bf16)[:, 0:1024]
        zz, ez = B_[0:4], B_[11:15]
        in_done, xi_ready, z_ready = sem("in_done"), sem("xi_ready"), sem("z_ready")
        conv_ready, xc_ready, pad_ready = sem("conv_ready"), sem("xc_ready"), sem("pad_ready")
        bc_done, dt_done, bc_ready, s_split = sem("bc_done"), sem("dt_done"), sem("bc_ready"), sem("split_step")
        zz_ready, sp_ready, dt_ready = sem("zz_ready"), sem("sp_ready"), sem("dt_ready")
        s_actm, s_negA = sem("act_step_m"), sem("negA_step")
        t8 = "p (b t) -> p b t"

        with nc.Block() as block:
            @block.sync
            def _(eng):
                load(eng, "w_in", w_in, a["M_in"])
                load(eng, "w_bc", w_bc[:, :, :], a["M_bc"])
                load(eng, "w_bc", w_dt, a["M_dt"])
                load(eng, "vecs", vecs[:, 0:98], a["M_vec"])
                load(eng, "w_out", w_out, a["M_out"])

            @block.gpsimd
            def _(eng):
                for k in range(2):
                    eng.memset(padded[k][:, :, 0:PAD], 0.0).then_inc(pad_ready, 1)
                normS.pool(eng)
                for c in range(0, CT, 2):
                    eng.wait_ge(dt_ready, c + 1)
                    eng.tensor_tensor(dtu[:, c], dts[:, c], xc[:, c], ALU.mult)

            @block.tensor
            def _(eng):
                normS.pe(eng)
                loaded(eng, "w_in")
                eng.wait_ge(normS.hT_ready, 4)

                def project(m):
                    r = 2 * (m % 4)
                    if m >= 4:
                        eng.wait_ge(xi_ready, m - 3)
                    for half in range(2):
                        for k in range(DC):
                            t = eng.matmul(ps[:, r + half, :], w_in[:, k, m * P:(m + 1) * P],
                                           hT[:, k, half * 512:(half + 1) * 512], start=k == 0, stop=k == DC - 1)
                    t.then_inc(in_done, 1)

                for m in range(CT + 2):
                    project(m)
                loaded(eng, "w_bc")
                eng.wait_ge(xc_ready, CT)
                eng.wait_ge(z_ready, 2)
                for half in range(2):
                    for c in range(CT):
                        t = eng.matmul(ps[:, 2 + half, :], w_dt[:, c, :], xc[:, c, half * 512:(half + 1) * 512],
                                       start=c == 0, stop=c == CT - 1)
                t.then_inc(dt_done, 1)
                for half in range(2):
                    for c in range(CT):
                        t = eng.matmul(ps[0:3 * E, half, :], w_bc[:, c, :], xc[:, c, half * 512:(half + 1) * 512],
                                       start=c == 0, stop=c == CT - 1)
                t.then_inc(bc_done, 1)
                for m in range(CT + 2, 2 * CT):
                    project(m)

            @block.scalar
            def _(eng):
                loaded(eng, "vecs")
                normS.act(eng, nw)
                for c in range(CT):
                    eng.wait_ge(in_done, c + 1)
                    if c < 2:
                        eng.wait_ge(pad_ready, c + 1)
                    else:
                        eng.wait_ge(conv_ready, c - 1)
                    r = 2 * c
                    eng.activation(padded[c % 2][:, :, PAD:], ps[:, r:r + 2, :].rearrange("p k (b t) -> p (k b) t", b=4),
                                   ACT.Copy).then_inc(xi_ready, 1)

                def gate_in(c):
                    eng.wait_ge(in_done, CT + c + 1)
                    eng.activation(zs[:, c], ps[:, 2 * c:2 * c + 2, :].rearrange("p k m -> p (k m)"),
                                   ACT.Silu).then_inc(z_ready, 1)

                for c in range(CT):
                    eng.wait_ge(conv_ready, c + 1)
                    eng.activation(xc[:, c], conv[c % 2], ACT.Silu).then_inc(xc_ready, 1)
                    if c in (1, 2):
                        gate_in(c - 1)
                eng.activation(negA, negA, ACT.Exp).then_inc(s_negA, 1)
                for c in range(CT):
                    eng.wait_ge(zz_ready, c + 1)
                    eng.activation(ez[c], zz[c], ACT.Abs).then_inc(s_actm, 1)
                    eng.wait_ge(s_actm, 2 * c + 1)
                    eng.activation(ez[c], ez[c], ACT.Exp, scale=-1.0).then_inc(s_actm, 1)
                for c in range(CT):
                    eng.wait_ge(s_actm, 2 * CT)
                    eng.activation(ez[c], ez[c], ACT.Ln, bias=1.0).then_inc(sp_ready, 1)
                for c in (2, 3):
                    gate_in(c)

            @block.vector
            def _(eng):
                ch = Chain(eng, s_split)
                normS.dve(eng, True)
                for c in range(CT):
                    d = c % 2
                    acc = conv[d].rearrange(t8, b=NB)
                    eng.wait_ge(xi_ready, c + 1)
                    if c >= 2:
                        eng.wait_ge(xc_ready, c - 1)
                    ch.link(eng.tensor_scalar(acc, padded[d][:, :, 0:P], cw[:, 4 * c:4 * c + 1], cb[:, c:c + 1],
                                              ALU.mult, ALU.add))
                    for k in range(1, KCONV):
                        t = eng.scalar_tensor_tensor(acc, padded[d][:, :, k:k + P], cw[:, 4 * c + k:4 * c + k + 1],
                                                     acc, ALU.mult, ALU.add)
                        if k < KCONV - 1:
                            ch.link(t)
                        else:
                            t.then_inc(conv_ready, 1)

                eng.wait_ge(dt_done, 1)
                for c in range(CT):
                    eng.tensor_scalar(zz[c], ps[:, 2:4, :].rearrange("p k m -> p (k m)"), dtw[:, c:c + 1],
                                      dtb[:, c:c + 1], ALU.mult, ALU.add).then_inc(zz_ready, 1)
                eng.wait_ge(s_negA, 1)
                ch.mark(eng.tensor_scalar(negA, negA, -1.0, None, ALU.mult))
                eng.wait_ge(bc_done, 1)
                ch.link(eng.tensor_copy(bcf[0:3 * E], ps[0:3 * E, 0:2, :].rearrange("p k m -> p (k m)")))
                split3(eng, ch, bc3, bcf, bct)
                for c in range(CT):
                    eng.wait_ge(sp_ready, c + 1)
                    eng.wait_ge(zz_ready, c + 1)
                    eng.scalar_tensor_tensor(dts[:, c], zz[c], 0.0, ez[c], ALU.max, ALU.add).then_inc(dt_ready, 1)
                    if c % 2:
                        eng.wait_ge(dt_ready, c + 1)
                        eng.tensor_tensor(dtu[:, c], dts[:, c], xc[:, c], ALU.mult)

        dA = [B_[k] for k in range(4)]
        dBu = [B_[4], B_[5]]
        hst = [B_[6], B_[7], B_[8], B_[9]]
        hC = [B_[10], B_[11], B_[12], B_[13]]
        Csb = [B_[14], B_[15]]

        B_done, C_done, C_ready = sem("scan_B"), sem("scan_C"), sem("scan_C_sbuf")
        dA_ready, dBu_ready, h_ready, hC_ready = sem("scan_dA"), sem("scan_dBu"), sem("scan_h"), sem("scan_hC")
        y_done, dA_zero, y_read, y_gated = sem("scan_y"), sem("scan_dA_zero"), sem("scan_y_read"), sem("scan_gated")
        rounds = ST // 2
        SLOTS = 2 * ST
        psB, psC = ps[:, 4:6, :].rearrange("p k m -> p (k m)"), ps[:, 6:8, :].rearrange("p k m -> p (k m)")

        with nc.Block() as block:
            @block.tensor
            def _(eng):
                for cp in range(2):
                    def BC(i, u):
                        if u % 2:
                            return
                        s, n = SLOTS * cp + 4 * i + u, 2 * i + u // 2
                        if not early(i, 1, s):
                            eng.wait_ge(dBu_ready, s)
                        for half in range(2):
                            t = eng.matmul(ps[:, 4 + half, :], sel[0:3 * E, bass.ds(n, 1), :].rearrange("p a m -> p (a m)"),
                                           bc3[0:3 * E, half * 512:(half + 1) * 512], start=True, stop=True)
                        t.then_inc(B_done, 1)
                        if not early(i, 1, s):
                            eng.wait_ge(C_ready, ST * cp + n)
                        for half in range(2):
                            t = eng.matmul(ps[:, 6 + half, :],
                                           sel[0:3 * E, bass.ds(n + ST, 1), :].rearrange("p a m -> p (a m)"),
                                           bc3[0:3 * E, half * 512:(half + 1) * 512], start=True, stop=True)
                        t.then_inc(C_done, 1)

                    def Y(i, u):
                        s = 4 * i + u
                        eng.wait_ge(hC_ready, SLOTS * cp + s + 1)
                        if cp and early(i, 2, s):
                            eng.wait_ge(y_read, u + 1)
                        for half in range(2):
                            t = eng.matmul(ps[:, 2 * (u % 2) + half, :], ident, hC[u][:, half * 512:(half + 1) * 512],
                                           start=early(i, 2, s), stop=isinstance(i, int) and s >= SLOTS - 2)
                        t.then_inc(y_done, 1)

                    pipeline(eng, rounds, [(2, BC), (-1, Y)], [(0, BC)], [(3, Y)])

            @block.scalar
            def _(eng):
                for cp in range(2):
                    def CS(i, u):
                        if u % 2:
                            return
                        n = ST * cp + 2 * i + u // 2
                        eng.wait_ge(C_done, n + 1)
                        if not early(i, 2, n):
                            eng.wait_ge(hC_ready, 2 * n - 2)
                        eng.activation(Csb[u // 2], psC, ACT.Copy).then_inc(C_ready, 1)

                    def DA(i, u):
                        s, n, c = SLOTS * cp + 4 * i + u, 2 * i + u // 2, 2 * cp + u % 2
                        if early(i, 4, s):
                            eng.wait_ge(dA_zero, u + 1)
                        else:
                            eng.wait_ge(h_ready, s - 3)
                        eng.activation(dA[u].rearrange(t8, b=NB)[:, :, 1:P], dts[:, c].rearrange(t8, b=NB)[:, :, 1:P],
                                       ACT.Exp, scale=negA[:, bass.ds(ST * c + n, 1)]).then_inc(dA_ready, 1)

                    pipeline(eng, rounds, [(2, DA), (1, CS)], [(0, DA), (1, DA), (0, CS)], [])

            @block.vector
            def _(eng):
                def gate(cp):
                    for k in range(2):
                        c = 2 * cp + k
                        eng.wait_ge(y_done, SLOTS * cp + SLOTS - 1 + k)
                        eng.scalar_tensor_tensor(yg[:, c], xc[:, c], Dp[:, c:c + 1],
                                                 ps[:, 2 * k:2 * k + 2, :].rearrange("p k m -> p (k m)"),
                                                 ALU.mult, ALU.add).then_inc(y_read, 1)
                    for k in range(2):
                        c = 2 * cp + k
                        eng.wait_ge(y_read, c + 1)
                        eng.tensor_tensor(yg[:, c], yg[:, c], zs[:, c], ALU.mult).then_inc(y_gated, 1)

                for cp in range(2):
                    def DB(i, u):
                        s, n, c = SLOTS * cp + 4 * i + u, 2 * i + u // 2, 2 * cp + u % 2
                        eng.wait_ge(B_done, ST * cp + n + 1)
                        if not early(i, 2, s):
                            eng.wait_ge(h_ready, s - 1)
                        eng.tensor_tensor(dBu[u % 2], dtu[:, c], psB, ALU.mult).then_inc(dBu_ready, 1)

                    def SC(i, u):
                        s = SLOTS * cp + 4 * i + u
                        eng.wait_ge(dA_ready, s + 1)
                        eng.wait_ge(dBu_ready, s + 1)
                        if not early(i, 4, s):
                            eng.wait_ge(hC_ready, s - 3)
                        eng.tensor_tensor_scan(hst[u], dA[u], dBu[u % 2], 0.0, ALU.mult, ALU.add).then_inc(h_ready, 1)

                    def GT(i, u):
                        if cp and u == 1 and early(i, 2, 4 * i + u):
                            gate(0)

                    pipeline(eng, rounds, [(1, DB), (0, SC), (0, GT)], [(0, DB)], [])
                gate(1)

            @block.gpsimd
            def _(eng):
                for u in range(4):
                    eng.memset(dA[u].rearrange(t8, b=NB)[:, :, 0:1], 0.0).then_inc(dA_zero, 1)
                for cp in range(2):
                    def HC(i, u):
                        s, n = SLOTS * cp + 4 * i + u, 2 * i + u // 2
                        eng.wait_ge(h_ready, s + 1)
                        eng.wait_ge(C_ready, ST * cp + n + 1)
                        if not early(i, 4, s):
                            eng.wait_ge(y_done, s - 3)
                        eng.tensor_tensor(hC[u], hst[u], Csb[u // 2], ALU.mult).then_inc(hC_ready, 1)

                    pipeline(eng, rounds, [(0, HC)], [], [])

        TP = P + 1
        o = W0
        vT = view(o, 2048, "p (c t) -> p c t", c=DC); o += 2048
        wkv_u = view(o, 2); o += 2
        wkv_w = view(o, 2); o += 2
        names = ("kp", "wp", "op", "no", "a1", "e1", "a2", "e2", "ev", "pp", "qp", "num", "den", "tmp")
        W = {n: [view(o + NB * TP * (2 * k + c), NB * TP, "p (b t) -> p b t", b=NB) for c in range(DC)]
             for k, n in enumerate(names)}
        o += NB * TP * 2 * len(names)
        assert o <= 51104
        flat = lambda v: v.rearrange("p b t -> p (b t)")
        HALVES = ((0, NB // 2), (NB // 2, NB))
        op_done, op_ready = sem("out_proj_done"), sem("out_proj_added")
        normW = Norm("nW", parts=HALVES)
        with nc.Block() as block:
            @block.sync
            def _(eng):
                load(eng, "uw", wkv_u, a["W_u"])
                load(eng, "uw", wkv_w, a["W_w"])
                load(eng, "vT", vT, a["ctxT"])

            @block.tensor
            def _(eng):
                loaded(eng, "w_out")
                for b in range(NB):
                    if b >= 4:
                        eng.wait_ge(op_ready, b - 3)
                    for c in range(CT):
                        t = eng.matmul(ps[:, 4 + b % 4, 0:D], yg[:, c, b * P:(b + 1) * P], w_out[:, c, :],
                                       start=c == 0, stop=c == CT - 1)
                    t.then_inc(op_done, 1)
                normW.pe(eng)

            @block.vector
            def _(eng):
                for b in range(NB + 1):
                    if b < NB:
                        eng.wait_ge(op_done, b + 1)
                        eng.tensor_tensor(x[:, b], x[:, b], ps[:, 4 + b % 4, 0:D], ALU.add).then_inc(op_ready, 1)
                    if b:
                        eng.wait_ge(op_ready, b)
                        normW.dve_stats(eng, b - 1)
                    if b == NB // 2:
                        normW.dve_variance(eng, 0)
                normW.dve_variance(eng, 1)
                normW.dve(eng, True)

            @block.gpsimd
            def _(eng):
                normW.pool(eng)

            @block.scalar
            def _(eng):
                normW.act(eng, into=W["kp"])

        normF = Norm("nF", parts=HALVES)
        num_ready, den_ready, inv_ready = sem("num_ready"), sem("den_ready"), sem("inv_ready")
        s_w, edges, yw_ready = sem("wkv_step"), sem("wkv_edges"), sem("wkv_y")
        op_scanned, no_ready = sem("wkv_max"), sem("wkv_no")
        pre = {n: sem("wkv_pre_" + n) for n in ("a2", "e2", "e1", "a1")}
        ex = {n: sem("wkv_exp_" + n) for n in ("a2", "e2", "e1", "a1")}
        ev_ready, tmp_ready = sem("wkv_ev"), sem("wkv_e1v")
        yT_done, xw_ready = sem("wkv_T_done"), sem("wkv_added")
        BIG = -1.0e38

        with nc.Block() as block:
            @block.gpsimd
            def _(eng):
                for c in range(DC):
                    eng.memset(W["kp"][c][:, :, 0:1], BIG).then_inc(edges, 1)
                for c in range(DC):
                    for n in ("a2", "e2", "ev"):
                        eng.memset(W[n][c][:, :, 0:1], 0.0).then_inc(edges, 1)

                def exponents(c):
                    w = {n: W[n][c] for n in names}
                    eng.wait_ge(op_scanned, c + 1)
                    eng.tensor_tensor(w["e2"][:, :, 1:], w["kp"][:, :, 1:], w["op"][:, :, 1:],
                                      ALU.subtract).then_inc(pre["e2"], 1)
                    eng.wait_ge(no_ready, c + 1)
                    eng.tensor_tensor(w["a1"][:, :, 1:], w["op"][:, :, 0:P], w["no"][:, :, 1:],
                                      ALU.subtract).then_inc(pre["a1"], 1)

                def values(c):
                    v = vT[:, c].rearrange(t8, b=NB)
                    eng.wait_ge(ex["e2"], c + 1)
                    eng.tensor_tensor(W["ev"][c][:, :, 1:], W["e2"][c][:, :, 1:], v, ALU.mult).then_inc(ev_ready, 1)
                    eng.wait_ge(ex["e1"], c + 1)
                    eng.tensor_tensor(W["tmp"][c][:, :, 1:], W["e1"][c][:, :, 1:], v, ALU.mult).then_inc(tmp_ready, 1)

                exponents(0)
                loaded(eng, "vT")
                values(0)
                exponents(1)
                values(1)
                normF.pool(eng)

            @block.scalar
            def _(eng):
                for c in range(DC):
                    for n in ("a2", "e2", "e1", "a1"):
                        eng.wait_ge(pre[n], c + 1)
                        if n in ("a2", "e2"):
                            eng.wait_ge(edges, 4 * DC)
                        eng.activation(W[n][c][:, :, 1:], W[n][c][:, :, 1:], ACT.Exp).then_inc(ex[n], 1)
                for c in range(DC):
                    eng.wait_ge(den_ready, c + 1)
                    eng.wait_ge(num_ready, c + 1)
                    eng.activation(W["tmp"][c][:, :, 1:], W["den"][c][:, :, 0:P], ACT.Ln).then_inc(inv_ready, 1)
                for c in range(DC):
                    r0 = W["tmp"][c][:, :, 1:]
                    eng.wait_ge(inv_ready, DC)
                    eng.activation(r0, r0, ACT.Exp, scale=-1.0).then_inc(inv_ready, 1)

            @block.vector
            def _(eng):
                ch = Chain(eng, s_w)
                loaded(eng, "uw")
                eng.wait_ge(edges, DC)
                for c in range(DC):
                    w = {n: W[n][c] for n in names}
                    u_, w_ = wkv_u[:, c:c + 1], wkv_w[:, c:c + 1]
                    k, o_prev, o_now = w["kp"][:, :, 1:], w["op"][:, :, 0:P], w["op"][:, :, 1:]
                    ch.link(eng.tensor_scalar(w["wp"][:, :, 1:], k, 0.0, w_, ALU.mult, ALU.add))
                    ch.link(eng.memset(w["wp"][:, :, 0:1], BIG))
                    eng.tensor_tensor_scan(flat(w["op"]), flat(w["wp"]), flat(w["kp"]), BIG, ALU.add,
                                           ALU.max).then_inc(op_scanned, 1)
                    eng.wait_ge(op_scanned, c + 1)
                    eng.scalar_tensor_tensor(w["a2"][:, :, 1:], o_prev, w_, o_now, ALU.add,
                                             ALU.subtract).then_inc(pre["a2"], 1)
                    eng.scalar_tensor_tensor(w["no"][:, :, 1:], k, u_, o_prev, ALU.add, ALU.max).then_inc(no_ready, 1)
                    eng.wait_ge(no_ready, c + 1)
                    eng.scalar_tensor_tensor(w["e1"][:, :, 1:], k, u_, w["no"][:, :, 1:], ALU.add,
                                             ALU.subtract).then_inc(pre["e1"], 1)
                for c in range(DC):
                    w = {n: W[n][c] for n in names}
                    num, den = w["num"][:, :, 0:P], w["den"][:, :, 0:P]
                    eng.wait_ge(ex["a2"], c + 1)
                    eng.wait_ge(ex["e2"], c + 1)
                    ch.link(eng.tensor_tensor_scan(flat(w["qp"]), flat(w["a2"]), flat(w["e2"]), 0.0, ALU.mult, ALU.add))
                    eng.wait_ge(ev_ready, c + 1)
                    ch.link(eng.tensor_tensor_scan(flat(w["pp"]), flat(w["a2"]), flat(w["ev"]), 0.0, ALU.mult, ALU.add))
                    eng.wait_ge(ex["a1"], c + 1)
                    eng.wait_ge(ex["e1"], c + 1)
                    ch.mark(eng.tensor_tensor(num, w["a1"][:, :, 1:], w["pp"][:, :, 0:P], ALU.mult))
                    ch.link(eng.tensor_tensor(den, w["a1"][:, :, 1:], w["qp"][:, :, 0:P], ALU.mult))
                    eng.tensor_tensor(den, den, w["e1"][:, :, 1:], ALU.add).then_inc(den_ready, 1)
                    eng.wait_ge(tmp_ready, c + 1)
                    eng.tensor_tensor(num, num, w["tmp"][:, :, 1:], ALU.add).then_inc(num_ready, 1)
                for c in range(DC):
                    w = {n: W[n][c] for n in names}
                    num, den = w["num"][:, :, 0:P], w["den"][:, :, 0:P]
                    r0, t0 = w["tmp"][:, :, 1:], w["e1"][:, :, 1:]
                    eng.wait_ge(inv_ready, DC + c + 1)
                    eng.wait_ge(num_ready, c + 1)
                    eng.wait_ge(den_ready, c + 1)
                    ch.link(eng.tensor_tensor(t0, den, r0, ALU.mult))
                    ch.link(eng.scalar_tensor_tensor(t0, t0, -2.0, r0, ALU.add, ALU.mult))
                    eng.scalar_tensor_tensor(num, t0, -1.0, num, ALU.mult, ALU.mult).then_inc(yw_ready, 1)
                for b in range(NB + 1):
                    if b < NB:
                        eng.wait_ge(yT_done, b + 1)
                        eng.tensor_tensor(x[:, b], x[:, b], ps[:, 2 + b % 4, 0:D], ALU.add).then_inc(xw_ready, 1)
                    if b:
                        eng.wait_ge(xw_ready, b)
                        normF.dve_stats(eng, b - 1)
                    if b == NB // 2:
                        normF.dve_variance(eng, 0)
                normF.dve_variance(eng, 1)
                normF.dve(eng, True)

            @block.tensor
            def _(eng):
                eng.wait_ge(yw_ready, DC)
                for b in range(NB):
                    if b >= 4:
                        eng.wait_ge(xw_ready, b - 3)
                    for c in range(DC):
                        t = eng.transpose(ps[:, 2 + b % 4, c * P:(c + 1) * P], W["num"][c][:, b, 0:P], ident)
                    t.then_inc(yT_done, 1)

        o = W0
        hq = view(o, 1024, "p (b f) -> p b f", dt=bf16, b=NB); o += 1024
        hqT = view(o, 1024, "p (b k t) -> p b k t", dt=bf16, b=NB, k=DC); o += 1024
        g1 = view(o, 2048, "p (d f) -> p d f", d=2); o += 2048
        g2 = view(o, 2048, "p (d f) -> p d f", d=2); o += 2048
        gq = view(o, 1024, "p (d f) -> p d f", dt=bf16, d=2); o += 1024
        gqT = view(o, 1024, "p (d k t) -> p d k t", dt=bf16, d=2, k=IC); o += 1024
        tv = view(o, 64, "p (n b) -> p n b", b=NB); o += 64
        hn = view(o, 2048, "p (b f) -> p b f", b=NB); o += 2048
        ss1, am1, r1, sc1, f1 = (tv[:, k] for k in range(5))
        tv2 = view(o, 64, "p (n b) -> p n b", b=NB); o += 64
        ss2, am2, r2, sc2, f2 = (tv2[:, k] for k in range(5))
        s_f = sem("ffn_step")
        r1_ready, hq_ready = sem("r1_ready"), sem("hq_ready")
        hqT_done, hqT_ready, up_done = sem("hqT_done"), sem("hqT_ready"), sem("up_done")
        g1_ready, g2_ready, ss2_ready, r2_ready, gq_ready = (sem("g1_ready"), sem("g2_ready"), sem("ss2_ready"),
                                                             sem("r2_ready"), sem("gq_ready"))
        gqT_done, gqT_ready, down_done, x_ready, stored = (sem("gqT_done"), sem("gqT_ready"), sem("down_done"),
                                                           sem("x_ready"), sem("out_stored"))

        TURNS = (((0, 2), psb[:, 0, 0:512]), ((2, 6), psb[:, 1, 0:1024]), ((6, 8), psb[:, 0, 512:1024]))

        def quant_scales(eng, ch, am, r, sc, f, w_clip):
            ch.link(eng.tensor_tensor(f, am, r, ALU.mult))
            ch.link(eng.tensor_scalar(f, f, 1e-5, 1.0 / 127.0, ALU.max, ALU.mult))
            ch.link(eng.reciprocal(sc, f))
            ch.link(eng.tensor_scalar(f, f, w_clip, None, ALU.mult))

        def quantise(eng, ch, dst, src, tmp, r, sc):
            ch.link(eng.tensor_scalar(tmp, src, r, sc, ALU.mult, ALU.mult))
            ch.link(eng.tensor_scalar(tmp, tmp, MAGIC, MAGIC + 127.0, ALU.add, ALU.min))
            return eng.tensor_scalar(dst, tmp, -MAGIC, -128.0, ALU.add, ALU.max)

        with nc.Block() as block:
            @block.sync
            def _(eng):
                for b in range(NB):
                    eng.wait_ge(x_ready, b + 1)
                    eng.dma_start(out[:, b], x[:, b]).then_inc(stored, 16)
                eng.wait_ge(stored, 16 * NB)

            @block.gpsimd
            def _(eng):
                normF.pool_mean_square(eng, r1_ready, ss1)
                eng.tensor_scalar(ss1, ss1, 1e-24 / D, None, ALU.max).then_inc(r1_ready, 1)
                eng.wait_ge(r1_ready, 3)
                eng.tensor_tensor(r1, ss1, neg_half.to_broadcast([P, NB]), ALU.pow).then_inc(r1_ready, 1)
                for b in range(NB):
                    eng.wait_ge(ss2_ready, b + 1)
                    eng.tensor_scalar(ss2[:, b:b + 1], ss2[:, b:b + 1], 1e-24, 1.0 / INNER, ALU.max, ALU.mult).then_inc(r2_ready, 1)
                    eng.wait_ge(r2_ready, 2 * b + 1)
                    eng.tensor_tensor(r2[:, b:b + 1], ss2[:, b:b + 1], neg_half, ALU.pow).then_inc(r2_ready, 1)

            @block.vector
            def _(eng):
                ch = Chain(eng, s_f)
                eng.wait_ge(normF.h_ready, NB)
                ch.link(eng.tensor_reduce(am1, h, AX.X, ALU.max, apply_absolute_value=True))
                eng.wait_ge(r1_ready, 4)
                quant_scales(eng, ch, am1, r1, sc1, f1, wcl[:, 0:1])
                for first, end in ((0, 2), (2, NB)):
                    for b in range(first, end):
                        ch.mark(eng.tensor_scalar(hn[:, b], h[:, b], r1[:, b:b + 1], sc1[:, b:b + 1], ALU.mult, ALU.mult))
                    ch.wait()
                    some = slice(first, end)
                    ch.link(eng.tensor_scalar(hn[:, some], hn[:, some], MAGIC, MAGIC + 127.0, ALU.add, ALU.min))
                    eng.tensor_scalar(hq[:, some], hn[:, some], -MAGIC, -128.0, ALU.add,
                                      ALU.max).then_inc(hq_ready, end - first)
                for b in range(NB):
                    d = b % 2
                    one = slice(b, b + 1)
                    eng.wait_ge(g2_ready, b + 1)
                    ch.link(eng.tensor_reduce(am2[:, one], g2[:, d], AX.X, ALU.max, apply_absolute_value=True))
                    eng.wait_ge(r2_ready, 2 * b + 2)
                    quant_scales(eng, ch, am2[:, one], r2[:, one], sc2[:, one], f2[:, one], wcl[:, 1:2])
                    if b >= 2:
                        eng.wait_ge(gqT_done, b - 1)
                    quantise(eng, ch, gq[:, d], g2[:, d], g2[:, d], r2[:, one], sc2[:, one]).then_inc(gq_ready, 1)
                    if b:
                        eng.wait_ge(down_done, b)
                        eng.scalar_tensor_tensor(x[:, b - 1], ps[:, 7, 0:D], f2[:, b - 1:b], x[:, b - 1], ALU.mult,
                                                 ALU.add).then_inc(x_ready, 1)
                eng.wait_ge(down_done, NB)
                eng.scalar_tensor_tensor(x[:, NB - 1], ps[:, 7, 0:D], f2[:, NB - 1:NB], x[:, NB - 1], ALU.mult,
                                         ALU.add).then_inc(x_ready, 1)

            @block.scalar
            def _(eng):
                def turned(k):
                    (first, end), bank = TURNS[k]
                    eng.wait_ge(hqT_done, k + 1)
                    eng.activation(hqT[:, first:end], bank.rearrange("p (b k t) -> p b k t", k=DC, t=P),
                                   ACT.Copy).then_inc(hqT_ready, 1)

                def inner_turned(b):
                    eng.wait_ge(gqT_done, b + 1)
                    if b >= 2:
                        eng.wait_ge(down_done, b - 1)
                    eng.activation(gqT[:, b % 2], psb[:, 6, :].rearrange("p (k t) -> p k t", k=IC),
                                   ACT.Copy).then_inc(gqT_ready, 1)

                turned(0)
                for b in range(NB):
                    d = b % 2
                    eng.wait_ge(up_done, b + 1)
                    eng.activation(g1[:, d], ps[:, 2 + 2 * d:4 + 2 * d, :].rearrange("p k m -> p (k m)"), ACT.Gelu,
                                   scale=f1[:, b:b + 1]).then_inc(g1_ready, 1)
                    eng.wait_ge(g1_ready, b + 1)
                    if b >= 2:
                        eng.wait_ge(gq_ready, b - 1)
                    eng.activation(g2[:, d], g1[:, d], ACT.Gelu).then_inc(g2_ready, 1)
                    eng.wait_ge(g2_ready, b + 1)
                    eng.activation(g1[:, d], g2[:, d], ACT.Square, accum_out=ss2[:, b:b + 1]).then_inc(ss2_ready, 1)
                    if b < 2:
                        turned(b + 1)
                    if b:
                        inner_turned(b - 1)
                inner_turned(NB - 1)

            @block.tensor
            def _(eng):
                def turn(k):
                    (first, end), bank = TURNS[k]
                    eng.wait_ge(hq_ready, end)
                    if k == 2:
                        eng.wait_ge(hqT_ready, 1)
                    for b in range(first, end):
                        for c in range(DC):
                            at = (b - first) * D + c * P
                            t = eng.transpose(bank[:, at:at + P], hq[:, b, c * P:(c + 1) * P], ident_b)
                    t.then_inc(hqT_done, 1)

                def up_(b):
                    d = b % 2
                    eng.wait_ge(hqT_ready, 1 + (b >= 2) + (b >= 6))
                    if b >= 2:
                        eng.wait_ge(g1_ready, b - 1)
                    for half in range(2):
                        for k in range(DC):
                            t = eng.matmul(ps[:, 2 + 2 * d + half, :], hqT[:, b, k], w1q[:, k, half * 512:(half + 1) * 512],
                                           start=k == 0, stop=k == DC - 1)
                    t.then_inc(up_done, 1)

                def down(b):
                    d = b % 2
                    eng.wait_ge(gq_ready, b + 1)
                    if b:
                        eng.wait_ge(gqT_ready, b)
                    for k in range(IC):
                        t = eng.transpose(psb[:, 6, k * P:(k + 1) * P], gq[:, d, k * P:(k + 1) * P], ident_b)
                    t.then_inc(gqT_done, 1)
                    eng.wait_ge(gqT_ready, b + 1)
                    if b:
                        eng.wait_ge(x_ready, b)
                    for k in range(IC):
                        t = eng.matmul(ps[:, 7, 0:D], gqT[:, d, k], w2q[:, k, :], start=k == 0, stop=k == IC - 1)
                    t.then_inc(down_done, 1)

                turn(0)
                up_(0)
                turn(1)
                turn(2)
                for b in range(NB):
                    if b + 1 < NB:
                        up_(b + 1)
                    if b:
                        down(b - 1)
                down(NB - 1)


def kernel(**inputs):
    import numpy as np
    import concourse.bacc as _bacc
    from concourse import mybir as _mybir
    from concourse.bass_utils import run_bass_kernel_spmd as _run

    g = {k: np.asarray(v) for k, v in inputs.items()}
    arrays = {}

    def put(name, v):
        arrays[name] = np.ascontiguousarray(v)

    def chunked(w, parts=P):
        return w.reshape(-1, parts, w.shape[-1]).transpose(1, 0, 2)

    pos = np.arange(P, dtype=np.float32)
    fA = (1.0 / np.float32(10000.0) ** (np.arange(0, R, 2, dtype=np.float32) / np.float32(R))).astype(np.float32)
    fX = (1.0 / np.float32(10000.0) ** (np.arange(R // 2, dtype=np.float32) / np.float32(R // 2))).astype(np.float32)
    idx, swap = np.arange(R) // 2, np.arange(R) ^ 1
    paired = np.arange(R).reshape(2, R // 2).T.ravel()
    sign = np.where(np.arange(R) % 2 == 0, -1.0, 1.0)
    for name, f in (("A", fA), ("X", fX)):
        ang = (pos[None, :] * f[idx][:, None]).astype(np.float32).astype(np.float64)
        c, s = np.cos(ang).astype(np.float32), (np.sin(ang) * sign[:, None]).astype(np.float32)
        one = np.ones_like(c)
        put("cos" + name, np.stack([np.concatenate([one, c]), np.concatenate([c, one])], 1))
        put("sin" + name, np.concatenate([s, s]))

    put("x", g["x"].transpose(1, 0, 2))
    put("ctxT", chunked(g["ctx_2048"].reshape(T, D).T))
    put("seg", g["itok_BxS_0_1023"].T)
    wq = g["L0_attn_w_query"].reshape(D, H, 2, R)
    put("A_qnT", wq[:, :, 0].transpose(2, 1, 0))
    pe = wq[:, :, 1].reshape(DC, P, H, R).transpose(1, 0, 2, 3)
    put("A_qr", pe.reshape(P, DC, H // 2, 2 * R))
    wkvb = g["L0_attn_wkv_b"].reshape(R, H, R + VH)
    put("A_kbT", wkvb[:, :, :R].transpose(2, 1, 0))
    vT = wkvb[:, :, R:].transpose(2, 1, 0)
    put("A_vT", np.concatenate([vT, vT], -1))
    put("A_o", g["L0_attn_out_proj_w"].reshape(H, VH, D).transpose(1, 0, 2))
    kva = chunked(g["L0_attn_wkv_a"])
    kc, kp = kva[..., :R], kva[..., R:]
    put("A_wkv", np.stack([np.concatenate([kc, kp], -1), np.concatenate([kp, kc], -1),
                           np.concatenate([kp[..., swap]] * 2, -1)], 1))
    put("A_norm", np.concatenate([g["L0_attn_kv_norm_w"]] * 2).reshape(P, 1))
    put("X_kvcT", g["L0_xattn_W_kvc"].T)
    put("X_kr2", np.concatenate([g["L0_xattn_W_kr"][:, paired], g["L0_xattn_W_kr"][:, paired[swap]]], -1))
    put("X_kvc", chunked(g["L0_xattn_W_kvc"]))
    put("X_uqT", g["L0_xattn_W_uq"].reshape(QC, H, VH).transpose(2, 1, 0))
    put("X_ukT", g["L0_xattn_W_uk"].reshape(R, H, VH).transpose(2, 1, 0))
    vT = g["L0_xattn_W_uv"].reshape(R, H, VH).transpose(2, 1, 0)
    put("X_vT", np.concatenate([vT, vT], -1))
    put("X_o", g["L0_xattn_W_o"].reshape(H, VH, D).transpose(1, 0, 2))
    qr = g["L0_xattn_W_qr"].reshape(QC, H, R)[..., paired]
    put("X_qr", qr.reshape(QC, H // 2, 2 * R))
    put("X_dq", chunked(g["L0_xattn_W_dq"]))

    gu = np.concatenate([g["L0_ffn_w_gate"], g["L0_ffn_w_up"]], -1)
    put("E_gu", gu.reshape(E, DC, P, 2 * I).transpose(2, 1, 0, 3))
    put("E_dn", g["L0_ffn_w_down"].transpose(1, 0, 2))
    put("E_gate", chunked(g["L0_ffn_gate_w"].T))
    put("E_gate_b", g["L0_ffn_gate_b"].reshape(1, E))
    bias = np.concatenate([g["L0_ffn_b_gate"], g["L0_ffn_b_up"], g["L0_ffn_b_down"]], -1)
    put("E_bias", np.concatenate([bias] * 3))

    put("M_in", chunked(g["L1_attn_in_proj_w"].T))
    xp = g["L1_attn_x_proj_w"].T
    put("M_bc", chunked(np.concatenate([xp[:, :2 * ST]] * 3, -1)))
    put("M_dt", chunked(np.repeat(xp[:, 2 * ST:], P, -1)))
    put("M_out", chunked(g["L1_attn_out_proj_w"].T))
    col = lambda v: v.reshape(-1, P).T
    put("M_vec", np.concatenate([chunked(g["L1_attn_conv_w"].reshape(DI, KCONV)).reshape(P, CT * KCONV),
                                 col(g["L1_attn_conv_b"]), col(g["L1_attn_dt_w"]), col(g["L1_attn_dt_b"]),
                                 col(g["L1_attn_D_param"]), col(g["L1_attn_norm_w"]),
                                 chunked(g["L1_attn_A_log"]).reshape(P, CT * ST)], -1))
    put("W_u", col(g["L1_xattn_u"]))
    put("W_w", col(g["L1_xattn_w"]))
    put("F_w1", chunked(g["L1_ffn_w1"].T))
    put("F_w2", chunked(g["L1_ffn_w2"].T))

    nc = _bacc.Bacc("TRN2", target_bir_lowering=False, num_devices=1)
    aps = {n: nc.dram_tensor("in_" + n, v.shape, _mybir.dt.from_np(v.dtype), kind="ExternalInput").ap()
           for n, v in arrays.items()}
    out = nc.dram_tensor("out_x", (P, NB, D), fp32, kind="ExternalOutput").ap()
    decoder(nc, aps, out)
    r = _run(nc, [{"in_" + n: v for n, v in arrays.items()}], core_ids=[0])
    return r.results[0]["out_x"].transpose(1, 0, 2)
```
